# Optimizing a Trainium2 kernel written in Bass

```python
import numpy as np
import jax
import jax.numpy as jnp

def _softmax(x, axis=-1):
    return jax.nn.softmax(x, axis=axis)

def _gelu(x):
    return jax.nn.gelu(x, approximate=True)

def _silu(x):
    return jax.nn.silu(x)

def _sigmoid(x):
    return jax.nn.sigmoid(x)

def _layernorm(x, axis=-1, eps=1e-05):
    m = jnp.mean(x, axis=axis, keepdims=True)
    v = jnp.var(x, axis=axis, keepdims=True)
    return (x - m) / jnp.sqrt(v + eps)

def _scatter_add(tgt, idx, src, axis=0):
    return tgt.at[idx].add(src)

def _segment_sum(src, seg, n):
    return jax.ops.segment_sum(src, seg, n)
kernel_name = 'mk_conv_attn_hybrid_d2_conv_nchw128_r4_257eec'

def setup_inputs(seed: int=0):
    np.random.seed(seed)
    _w = jnp.asarray

    def _rec_inputs():
        import jax
        import jax.numpy as jnp
        _gk = jax.random.key(seed)
        x = -0.0002928 + 1 * jax.random.normal(jax.random.fold_in(_gk, 1), (8, 32, 16, 16), jnp.float32)
        return x
    x = _rec_inputs()

    def _L0_conv_setup():
        import jax, jax.numpy as jnp
        import numpy as np
        from jax import lax
        B, C, H, W = (8, 32, 16, 16)
        L = H * W
        DM, DI, DS, DC, NH, HD = (32, 16, 16, 4, 1, 16)

        def _causal_dwconv1d(x, w, b):
            xc = jnp.transpose(x, (0, 2, 1))
            xc = jnp.pad(xc, ((0, 0), (0, 0), (DC - 1, 0)))
            o = lax.conv_general_dilated(xc, w[:, None, :], (1,), 'VALID', feature_group_count=w.shape[0], dimension_numbers=('NCH', 'OIH', 'NCH'))
            return jnp.transpose(o + b[None, :, None], (0, 2, 1))

        def _mamba2(u, W_in, conv_w, conv_b, dt_bias, A_log, D, norm_w, W_out):
            b, l, _ = u.shape
            zxbcdt = u @ W_in
            z = zxbcdt[..., :DI]
            xBC = zxbcdt[..., DI:DI + DI + 2 * DS]
            dt = zxbcdt[..., -NH:]
            xBC = jax.nn.silu(_causal_dwconv1d(xBC, conv_w, conv_b))
            xs = xBC[..., :DI]
            Bm = xBC[..., DI:DI + DS]
            Cm = xBC[..., DI + DS:]
            dt = jax.nn.softplus(dt + dt_bias)
            dA = jnp.exp(dt * -jnp.exp(A_log))
            xh = xs.reshape(b, l, NH, HD)
            dtx = dt[..., None] * xh

            def step(h, inp):
                dA_t, dtx_t, B_t, C_t = inp
                h = dA_t[:, :, None, None] * h + dtx_t[..., None] * B_t[:, None, None, :]
                y = jnp.einsum('bhpn,bn->bhp', h, C_t)
                return (h, y)
            h0 = jnp.zeros((b, NH, HD, DS), u.dtype)
            _, ys = lax.scan(step, h0, (jnp.moveaxis(dA, 1, 0), jnp.moveaxis(dtx, 1, 0), jnp.moveaxis(Bm, 1, 0), jnp.moveaxis(Cm, 1, 0)))
            y = jnp.moveaxis(ys, 0, 1) + D[None, None, :, None] * xh
            y = y.reshape(b, l, DI)
            y = y * jax.nn.silu(z)
            y = y * lax.rsqrt(jnp.mean(y * y, -1, keepdims=True) + 1e-05) * norm_w
            return y @ W_out

        def _forward(x, lin1_w, lin1_b, dw_w, dw_b, fc_in_w, mam_in_w, mam_conv_w, mam_conv_b, mam_dt_bias, mam_A_log, mam_D, mam_norm_w, mam_out_w, fc_out_w, bn_g, bn_b, conv4_w, conv4_b):
            b, c, h, w = x.shape
            o = jnp.einsum('bihw,io->bohw', x, lin1_w) + lin1_b[None, :, None, None]
            o = lax.conv_general_dilated(o, dw_w, (1, 1), 'SAME', feature_group_count=c, dimension_numbers=('NCHW', 'OIHW', 'NCHW')) + dw_b[None, :, None, None]
            o = jax.nn.silu(o)
            s = jnp.einsum('bcl,cd->bld', o.reshape(b, c, h * w), fc_in_w)
            y1 = _mamba2(s, mam_in_w[0], mam_conv_w[0], mam_conv_b[0], mam_dt_bias[0], mam_A_log[0], mam_D[0], mam_norm_w[0], mam_out_w[0])
            y2 = jnp.flip(_mamba2(jnp.flip(s, 1), mam_in_w[1], mam_conv_w[1], mam_conv_b[1], mam_dt_bias[1], mam_A_log[1], mam_D[1], mam_norm_w[1], mam_out_w[1]), 1)
            o = jnp.transpose((y1 + y2) @ fc_out_w, (0, 2, 1)).reshape(b, c, h, w)
            mu = jnp.mean(o, (0, 2, 3), keepdims=True)
            var = jnp.mean((o - mu) ** 2, (0, 2, 3), keepdims=True)
            o = (o - mu) * lax.rsqrt(var + 1e-05) * bn_g[None, :, None, None] + bn_b[None, :, None, None]
            g = jax.nn.sigmoid(jnp.einsum('bihw,io->bohw', o, conv4_w) + conv4_b[None, :, None, None])
            return g * x + x
        key = jax.random.key(seed)
        ks = jax.random.split(key, 12)

        def r(i, shape, s):
            return jax.random.normal(ks[i], shape, jnp.float32) * s
        return {'x': jax.random.normal(ks[0], (B, C, H, W), jnp.float32), 'lin1_w': r(1, (C, C), 0.05), 'lin1_b': jnp.zeros((C,), jnp.float32), 'dw_w': r(2, (C, 1, 3, 3), 0.1), 'dw_b': jnp.zeros((C,), jnp.float32), 'fc_in_w': r(3, (C, DM), 0.05), 'mam_in_w': r(4, (2, DM, 2 * DI + 2 * DS + NH), 0.05), 'mam_conv_w': r(5, (2, DI + 2 * DS, DC), 0.1), 'mam_conv_b': jnp.zeros((2, DI + 2 * DS), jnp.float32), 'mam_dt_bias': r(6, (2, NH), 0.1), 'mam_A_log': jnp.zeros((2, NH), jnp.float32), 'mam_D': jnp.ones((2, NH), jnp.float32), 'mam_norm_w': jnp.ones((2, DI), jnp.float32), 'mam_out_w': r(7, (2, DI, DM), 0.05), 'fc_out_w': r(8, (DM, C), 0.05), 'bn_g': jnp.ones((C,), jnp.float32), 'bn_b': jnp.zeros((C,), jnp.float32), 'conv4_w': r(9, (C, C), 0.05), 'conv4_b': jnp.zeros((C,), jnp.float32)}
    _L0_conv_all = _L0_conv_setup()
    _L0_conv_in = {k: v for k, v in _L0_conv_all.items() if k in ('lin1_w', 'lin1_b', 'dw_w', 'dw_b', 'fc_in_w', 'mam_in_w', 'mam_conv_w', 'mam_conv_b', 'mam_dt_bias', 'mam_A_log', 'mam_D', 'mam_norm_w', 'mam_out_w', 'fc_out_w', 'bn_g', 'bn_b', 'conv4_w', 'conv4_b')}
    del _L0_conv_all

    def _L1_attn_setup():
        import jax, jax.numpy as jnp
        import numpy as np
        B, S, D = (4, 1024, 32)
        key = jax.random.key(seed)
        k1, k2, k3, k4 = jax.random.split(key, 4)
        emb = jax.random.normal(k1, (B, S, D), dtype=jnp.float32)
        lim = float(np.sqrt(6.0 / (D + D)))
        W_Q = jax.random.uniform(k2, (D, D), jnp.float32, -lim, lim)
        W_K = jax.random.uniform(k3, (D, D), jnp.float32, -lim, lim)
        W_V = jax.random.uniform(k4, (D, D), jnp.float32, -lim, lim)
        return {'embeddings': emb, 'W_Q': W_Q, 'W_K': W_K, 'W_V': W_V}
    _L1_attn_all = _L1_attn_setup()
    _L1_attn_in = {k: v for k, v in _L1_attn_all.items() if k in ('W_Q', 'W_K', 'W_V')}
    del _L1_attn_all

    def _L1_ffn_setup():
        import jax, jax.numpy as jnp
        import numpy as np
        B, N, D, C, E, K = (8, 2048, 32, 32, 8, 2)
        key = jax.random.key(seed)
        k0, k1, k2 = jax.random.split(key, 3)
        x = jax.random.normal(k0, (B, N, D), dtype=jnp.float32)
        router_w = jax.random.normal(k1, (D, E), dtype=jnp.float32) * 0.05
        router_b = jnp.zeros((E,), dtype=jnp.float32)
        expert_w = jax.random.normal(k2, (E, D, C), dtype=jnp.float32) * (1.0 / np.sqrt(D))
        expert_b = jnp.zeros((E, C), dtype=jnp.float32)
        return {'x': x, 'router_w': router_w, 'router_b': router_b, 'expert_w': expert_w, 'expert_b': expert_b}
    _L1_ffn_all = _L1_ffn_setup()
    _L1_ffn_in = {k: v for k, v in _L1_ffn_all.items() if k in ('router_w', 'router_b', 'expert_w', 'expert_b')}
    del _L1_ffn_all
    return {'x': x, 'L0_conv_lin1_w': _L0_conv_in['lin1_w'], 'L0_conv_lin1_b': _L0_conv_in['lin1_b'], 'L0_conv_dw_w': _L0_conv_in['dw_w'], 'L0_conv_dw_b': _L0_conv_in['dw_b'], 'L0_conv_fc_in_w': _L0_conv_in['fc_in_w'], 'L0_conv_mam_in_w': _L0_conv_in['mam_in_w'], 'L0_conv_mam_conv_w': _L0_conv_in['mam_conv_w'], 'L0_conv_mam_conv_b': _L0_conv_in['mam_conv_b'], 'L0_conv_mam_dt_bias': _L0_conv_in['mam_dt_bias'], 'L0_conv_mam_A_log': _L0_conv_in['mam_A_log'], 'L0_conv_mam_D': _L0_conv_in['mam_D'], 'L0_conv_mam_norm_w': _L0_conv_in['mam_norm_w'], 'L0_conv_mam_out_w': _L0_conv_in['mam_out_w'], 'L0_conv_fc_out_w': _L0_conv_in['fc_out_w'], 'L0_conv_bn_g': _L0_conv_in['bn_g'], 'L0_conv_bn_b': _L0_conv_in['bn_b'], 'L0_conv_conv4_w': _L0_conv_in['conv4_w'], 'L0_conv_conv4_b': _L0_conv_in['conv4_b'], 'L1_attn_W_Q': _L1_attn_in['W_Q'], 'L1_attn_W_K': _L1_attn_in['W_K'], 'L1_attn_W_V': _L1_attn_in['W_V'], 'L1_ffn_router_w': _L1_ffn_in['router_w'], 'L1_ffn_router_b': _L1_ffn_in['router_b'], 'L1_ffn_expert_w': _L1_ffn_in['expert_w'], 'L1_ffn_expert_b': _L1_ffn_in['expert_b']}

def reference(x, L0_conv_lin1_w, L0_conv_lin1_b, L0_conv_dw_w, L0_conv_dw_b, L0_conv_fc_in_w, L0_conv_mam_in_w, L0_conv_mam_conv_w, L0_conv_mam_conv_b, L0_conv_mam_dt_bias, L0_conv_mam_A_log, L0_conv_mam_D, L0_conv_mam_norm_w, L0_conv_mam_out_w, L0_conv_fc_out_w, L0_conv_bn_g, L0_conv_bn_b, L0_conv_conv4_w, L0_conv_conv4_b, L1_attn_W_Q, L1_attn_W_K, L1_attn_W_V, L1_ffn_router_w, L1_ffn_router_b, L1_ffn_expert_w, L1_ffn_expert_b):
    import jax
    import jax.numpy as jnp

    def _L0_conv_ref(x, lin1_w, lin1_b, dw_w, dw_b, fc_in_w, mam_in_w, mam_conv_w, mam_conv_b, mam_dt_bias, mam_A_log, mam_D, mam_norm_w, mam_out_w, fc_out_w, bn_g, bn_b, conv4_w, conv4_b):
        import jax, jax.numpy as jnp
        import numpy as np
        from jax import lax
        B, C, H, W = (8, 32, 16, 16)
        L = H * W
        DM, DI, DS, DC, NH, HD = (32, 16, 16, 4, 1, 16)

        def _causal_dwconv1d(x, w, b):
            xc = jnp.transpose(x, (0, 2, 1))
            xc = jnp.pad(xc, ((0, 0), (0, 0), (DC - 1, 0)))
            o = lax.conv_general_dilated(xc, w[:, None, :], (1,), 'VALID', feature_group_count=w.shape[0], dimension_numbers=('NCH', 'OIH', 'NCH'))
            return jnp.transpose(o + b[None, :, None], (0, 2, 1))

        def _mamba2(u, W_in, conv_w, conv_b, dt_bias, A_log, D, norm_w, W_out):
            b, l, _ = u.shape
            zxbcdt = u @ W_in
            z = zxbcdt[..., :DI]
            xBC = zxbcdt[..., DI:DI + DI + 2 * DS]
            dt = zxbcdt[..., -NH:]
            xBC = jax.nn.silu(_causal_dwconv1d(xBC, conv_w, conv_b))
            xs = xBC[..., :DI]
            Bm = xBC[..., DI:DI + DS]
            Cm = xBC[..., DI + DS:]
            dt = jax.nn.softplus(dt + dt_bias)
            dA = jnp.exp(dt * -jnp.exp(A_log))
            xh = xs.reshape(b, l, NH, HD)
            dtx = dt[..., None] * xh

            def step(h, inp):
                dA_t, dtx_t, B_t, C_t = inp
                h = dA_t[:, :, None, None] * h + dtx_t[..., None] * B_t[:, None, None, :]
                y = jnp.einsum('bhpn,bn->bhp', h, C_t)
                return (h, y)
            h0 = jnp.zeros((b, NH, HD, DS), u.dtype)
            _, ys = lax.scan(step, h0, (jnp.moveaxis(dA, 1, 0), jnp.moveaxis(dtx, 1, 0), jnp.moveaxis(Bm, 1, 0), jnp.moveaxis(Cm, 1, 0)))
            y = jnp.moveaxis(ys, 0, 1) + D[None, None, :, None] * xh
            y = y.reshape(b, l, DI)
            y = y * jax.nn.silu(z)
            y = y * lax.rsqrt(jnp.mean(y * y, -1, keepdims=True) + 1e-05) * norm_w
            return y @ W_out

        def _forward(x, lin1_w, lin1_b, dw_w, dw_b, fc_in_w, mam_in_w, mam_conv_w, mam_conv_b, mam_dt_bias, mam_A_log, mam_D, mam_norm_w, mam_out_w, fc_out_w, bn_g, bn_b, conv4_w, conv4_b):
            b, c, h, w = x.shape
            o = jnp.einsum('bihw,io->bohw', x, lin1_w) + lin1_b[None, :, None, None]
            o = lax.conv_general_dilated(o, dw_w, (1, 1), 'SAME', feature_group_count=c, dimension_numbers=('NCHW', 'OIHW', 'NCHW')) + dw_b[None, :, None, None]
            o = jax.nn.silu(o)
            s = jnp.einsum('bcl,cd->bld', o.reshape(b, c, h * w), fc_in_w)
            y1 = _mamba2(s, mam_in_w[0], mam_conv_w[0], mam_conv_b[0], mam_dt_bias[0], mam_A_log[0], mam_D[0], mam_norm_w[0], mam_out_w[0])
            y2 = jnp.flip(_mamba2(jnp.flip(s, 1), mam_in_w[1], mam_conv_w[1], mam_conv_b[1], mam_dt_bias[1], mam_A_log[1], mam_D[1], mam_norm_w[1], mam_out_w[1]), 1)
            o = jnp.transpose((y1 + y2) @ fc_out_w, (0, 2, 1)).reshape(b, c, h, w)
            mu = jnp.mean(o, (0, 2, 3), keepdims=True)
            var = jnp.mean((o - mu) ** 2, (0, 2, 3), keepdims=True)
            o = (o - mu) * lax.rsqrt(var + 1e-05) * bn_g[None, :, None, None] + bn_b[None, :, None, None]
            g = jax.nn.sigmoid(jnp.einsum('bihw,io->bohw', o, conv4_w) + conv4_b[None, :, None, None])
            return g * x + x
        return _forward(x, lin1_w, lin1_b, dw_w, dw_b, fc_in_w, mam_in_w, mam_conv_w, mam_conv_b, mam_dt_bias, mam_A_log, mam_D, mam_norm_w, mam_out_w, fc_out_w, bn_g, bn_b, conv4_w, conv4_b)

    def _L1_attn_ref(embeddings, W_Q, W_K, W_V):
        import jax, jax.numpy as jnp
        import numpy as np
        B, S, D = (4, 1024, 32)
        _, seq_len, d = embeddings.shape
        Q = embeddings @ W_Q
        K = embeddings @ W_K
        V = embeddings @ W_V
        scale = 1.0 / jnp.sqrt(jnp.float32(d))
        scores = jnp.einsum('bqd,bkd->bqk', Q, K) * scale
        causal = jnp.tril(jnp.ones((seq_len, seq_len), dtype=bool))
        masked = jnp.where(causal[None, :, :], scores, jnp.float32(-jnp.inf))
        probs = jax.nn.softmax(masked, axis=-1)
        return jnp.einsum('bqk,bkd->bqd', probs, V)

    def _L1_ffn_ref(x, router_w, router_b, expert_w, expert_b):
        import jax, jax.numpy as jnp
        import numpy as np
        B, N, D, C, E, K = (8, 2048, 32, 32, 8, 2)
        router_probs = jax.nn.softmax(x @ router_w + router_b, axis=-1)
        top_p, top_i = jax.lax.top_k(router_probs, K)
        top_p = top_p / jnp.sum(top_p, axis=-1, keepdims=True)
        expert_out = jnp.einsum('bnd,edc->bnec', x, expert_w) + expert_b
        gathered = jnp.take_along_axis(expert_out, top_i[..., None], axis=2)
        return jnp.einsum('bnk,bnkc->bnc', top_p, gathered)

    def _gn(v, G=32, eps=1e-05):
        B_, C_, H_, W_ = v.shape
        g = v.reshape(B_, G, C_ // G, H_, W_)
        m = jnp.mean(g, axis=(2, 3, 4), keepdims=True)
        s = jnp.var(g, axis=(2, 3, 4), keepdims=True)
        return ((g - m) / jnp.sqrt(s + eps)).reshape(v.shape)

    def _ln_c(v, eps=1e-06):
        m = jnp.mean(v, axis=1, keepdims=True)
        s = jnp.var(v, axis=1, keepdims=True)
        return (v - m) / jnp.sqrt(s + eps)

    def _ln_t(v, eps=1e-05):
        m = jnp.mean(v, axis=-1, keepdims=True)
        s = jnp.var(v, axis=-1, keepdims=True)
        return (v - m) / jnp.sqrt(s + eps)

    def _to_tokens(v):
        B_, C_, H_, W_ = v.shape
        return v.reshape(B_, C_, H_ * W_).transpose(0, 2, 1)

    def _from_tokens(t, like):
        B_, C_, H_, W_ = like.shape
        return t.transpose(0, 2, 1).reshape(B_, C_, H_, W_)
    x = _L0_conv_ref(x, L0_conv_lin1_w, L0_conv_lin1_b, L0_conv_dw_w, L0_conv_dw_b, L0_conv_fc_in_w, L0_conv_mam_in_w, L0_conv_mam_conv_w, L0_conv_mam_conv_b, L0_conv_mam_dt_bias, L0_conv_mam_A_log, L0_conv_mam_D, L0_conv_mam_norm_w, L0_conv_mam_out_w, L0_conv_fc_out_w, L0_conv_bn_g, L0_conv_bn_b, L0_conv_conv4_w, L0_conv_conv4_b)
    t = _to_tokens(x)
    t = t + _L1_attn_ref(_ln_t(t), L1_attn_W_Q, L1_attn_W_K, L1_attn_W_V)
    t = t + _L1_ffn_ref(_ln_t(t), L1_ffn_router_w, L1_ffn_router_b, L1_ffn_expert_w, L1_ffn_expert_b)
    x = _from_tokens(t, x)
    return x

_drawn_inputs = setup_inputs


def setup_inputs(seed=0):
    import zlib

    import numpy as np

    out = dict(_drawn_inputs(seed))
    spreads = {'L0_conv_lin1_b': (0.0, 0.683),
     'L0_conv_dw_b': (0.0, 0.492),
     'L0_conv_mam_conv_b': (0.0, 0.1),
     'L0_conv_mam_A_log': (0.0, 2.0),
     'L0_conv_mam_D': (1.0, 0.551),
     'L0_conv_mam_norm_w': (1.0, 0.579),
     'L0_conv_bn_g': (1.0, 0.6),
     'L0_conv_bn_b': (0.0, 0.302),
     'L0_conv_conv4_b': (0.0, 0.1),
     'L1_ffn_router_b': (0.0, 0.1),
     'L1_ffn_expert_b': (0.0, 0.1)}
    factors = {'L0_conv_mam_conv_w': 8.0, 'L0_conv_mam_dt_bias': 200.0}
    for name, (base, spread) in spreads.items():
        noise = np.random.default_rng([zlib.crc32(name.encode()), seed]).standard_normal(out[name].shape)
        drawn = base * np.exp(spread * noise) if base else spread * noise
        out[name] = jnp.asarray(drawn.astype(out[name].dtype))
    for name, factor in factors.items():
        out[name] = (out[name] * factor).astype(out[name].dtype)
    return out
```

```python
from contextlib import ExitStack

import concourse.bass as bass
from concourse import mybir

F32 = mybir.dt.float32
BF16 = mybir.dt.bfloat16
ALU = mybir.AluOpType
ACT = mybir.ActivationFunctionType
AX_X = mybir.AxisListType.X

P = 128
B, C, H, W = 8, 32, 16, 16
L = H * W
BQ = P // C
BH = B // BQ
Q = 128
NC = L // Q
NBLK = BH * NC
N = BH * L
DIRS = 2
DI = 16
TAPS1 = 4
PAD = TAPS1 - 1
HP, WP = H + 2, W + 2
E = 8
EPS = 1e-5
MASKED = -1.0e30
SIG_CLAMP = -40.0

PACKS = {
    "pa": [("lin1", 128), ("ident", 128), ("lin1_b", 1), ("dw", 9), ("dw_b", 1)],
    "pb": [("fc_in_t", 128), ("mam_in", 130), ("taps", 16 * C), ("mask4", 4), ("conv_b", 4),
           ("dt_bias", 32), ("a_log", 32), ("keep_da", 32), ("skip_d", 2), ("rev", 128),
           ("tri", 256)],
    "pc": [("out_t", 256), ("fc_out", 128), ("norm_w", 2), ("mask", 128), ("mean16", 128),
           ("bn_avg", 128), ("bn_g", 1), ("bn_b", 1), ("conv4", 128), ("conv4_b", 1),
           ("centre", 128), ("mean32", 128), ("wq_t", 128), ("wk_t", 128), ("wv", 128),
           ("causal", 384)],
    "pd": [("router", 32), ("router_b", 128), ("experts", 256), ("experts_b", 128), ("rank", 128)],
}


def columns(pack):
    at, out = 0, {}
    for name, width in PACKS[pack]:
        out[name] = (at, at + width)
        at += width
    return out, at


def program(nc, x_in, pa_in, pb_in, pc_in, pd_in, out):
    ctx = ExitStack()
    with ctx:
        def sb(name, shape, dt=F32):
            return ctx.enter_context(nc.sbuf_tensor(name, shape, dt))

        def sem(name):
            return ctx.enter_context(nc.semaphore(name))

        packs = {}
        tiles = {}
        for pack in PACKS:
            where, width = columns(pack)
            tiles[pack] = sb(pack, [P, width])
            for name, (a, b) in where.items():
                packs[name] = tiles[pack][:, a:b]

        x4 = sb("x4", [P, N])
        warm = sb("warm", [P, 512], BF16)
        o1p = sb("o1p", [P, BH, HP, WP])
        diag = sb("diag", [P, 9, P])
        conv = sb("conv", [P, 2, BH, L])
        convs = sb("convs", [P, BH, L])
        o4 = sb("o4", [P, BH, L + 2 * PAD])
        wc = sb("wc", [P, 130])
        proj_w = sb("proj_w", [P, 16, BQ, C])
        dt_w = sb("dt_w", [P, DIRS, BQ])
        s1 = sb("s1", [P, DIRS, BH, L])
        s2 = sb("s2", [P, DIRS, BH, L])
        cbd = sb("cbd", [P, DIRS, NBLK, BQ, Q])
        dtx_ = sb("dtx_", [P, 8, 32])
        neg_a = sb("neg_a", [P, 32])
        a_tok = sb("a_tok", [P, 32])
        da = sb("da", [P, 32])
        pfx = sb("pfx", [P, DIRS, BH, BQ, C])
        data1 = sb("data1", [P, DIRS, BQ * Q])
        lmat = sb("lmat", [P, 8, BQ * Q])
        mmat = sb("mmat", [P, 8, BQ, Q])
        dtbx = sb("dtbx", [P, DIRS, NBLK, BQ, C])
        wbx = sb("wbx", [P, DIRS, BH, BQ, C])
        hst = sb("hst", [P, DIRS, BH, C])
        cpfx = sb("cpfx", [P, DIRS, BH, Q])
        yd = sb("yd", [P, DIRS, N])
        yg = sb("yg", [P, DIRS, N])
        ysq = sb("ysq", [P, DIRS, N])
        yln = sb("yln", [P, DIRS, N])
        yrs = sb("yrs", [P, DIRS, N])
        yn = sb("yn", [P, DIRS, N])
        out_w = sb("out_w", [P, DIRS, P])
        mq = sb("mq", [P, P])
        eps_t = sb("eps_t", [P, 2])
        bst = sb("bst", [P, 6])
        bmv = sb("bmv", [P, 2])
        bme = sb("bme", [P, 2])
        bm = sb("bm", [P, 2])
        bsm = sb("bsm", [P, 8])
        obn = sb("obn", [P, N])
        u4 = sb("u4", [P, N])
        g1 = sb("g1", [P, N])
        g2 = sb("g2", [P, N])
        g3 = sb("g3", [P, N])
        x1 = sb("x1", [P, N])
        c1sq = sb("c1sq", [P, N])
        l1 = sb("l1", [P, N])
        l1r = sb("l1r", [P, N])
        h1 = sb("h1", [P, N])
        at_ = sb("at_", [P, N])
        vaug = sb("vaug", [P, NBLK, BQ, C + 1])
        idb = sb("idb", [P, P], BF16)
        caus = sb("caus", [P, 384], BF16)
        nmax = sb("nmax", [P, B, 2])
        prob = mmat[:, :, :, :].rearrange("p g q t -> p (g q t)")[:, 0:B * 384].rearrange("p (b t) -> p b t", b=B)
        probt = cbd[:, :, :, :, :].rearrange("p d k q t -> p (d k q t)")[:, 0:B * 384].rearrange("p (b t) -> p b t", b=B)
        x1t = sb("x1t", [P, NBLK, BQ, C])
        rden = sb("rden", [P, NBLK, BQ])
        att = sb("att", [P, NBLK, BQ, C])
        t2 = sb("t2", [P, NBLK, BQ, C])
        t2s = sb("t2s", [P, NBLK, BQ])
        t2m = sb("t2m", [P, NBLK, BQ])
        t2c = sb("t2c", [P, NBLK, BQ, C])
        t2q = sb("t2q", [P, NBLK, BQ, C])
        t2v = sb("t2v", [P, NBLK, BQ])
        t2l = sb("t2l", [P, NBLK, BQ])
        t2r = sb("t2r", [P, NBLK, BQ])
        h2 = sb("h2", [P, NBLK, BQ, C])
        h2t = sb("h2t", [P, N])
        lg = sb("lg", [P, 12, 16, E])
        lg1 = sb("lg1", [P, 8, 16])
        wtok = sb("wtok", [P, 16, E])
        wtt = sb("wtt", [P, P])
        mix = lmat[:, :, :].rearrange("p g c -> p (g c)").rearrange("p (k e q c) -> p k e q c", k=NBLK, q=BQ, e=E)
        fin = sb("fin", [P, N])

        bank = [ctx.enter_context(nc.psum_tensor(f"bank{i}", [P, 512], F32)) for i in range(8)]

        names = (
            "x_in pa_in pb_in pc_in pd_in stored zeroed warmed lin1_done lin1_copied diag_ready conv_part "
            "taps_done conv_summed silu_done wc_done wc_copied proj_w_ready dt_w_ready dt_done "
            "proj_done proj_silu cbd_ready dt_step dt_act a_ready da_ready da_masked cum_done "
            "pfx_ready pfxb_done cpfx_ready data1_ready dab_done scanned g_done m_ready s1t_done "
            "dtbx_ready wbx_ready h_done h_copied y_done yd_ready yg_ready ysq_ready yms_done "
            "yln_ready yrs_ready yn_ready fold_done out_w_ready mq_ready neg_a_ready o_done "
            "bn_step bn_avg_done bn_act obn_ready conv4_done u4_ready gate_step x1_ready "
            "cen_done csq_ready var_done ln1_step h1_ready q_done q_copied v_done v_copied x1t_done "
            "x1t_copied bf_ready s_done nmax_ready prob_ready pt_done pt_copied o_att_done "
            "att_step t2_ready ln2_step ln2_act h2_ready h2t_done h2t_copied router_done "
            "route_step route_act w_ready wt_done wt_copied e_done mix_ready mixed fin_ready wsel".split())
        S = {n: sem(n) for n in names}

        block = ctx.enter_context(nc.Block())

        def blk_of(d, bh, step):
            return NC * bh + (step if d == 0 else NC - 1 - step)

        groups = [(d, bh, step) for d in range(DIRS) for bh in range(BH) for step in range(NC)]
        DT, CUM, HC, PB = 0, 32, 64, 192
        small = bank[7]
        dt_ps = small[:, DT:DT + 32]
        cum_ps = small[:, CUM:CUM + 32].rearrange("p (d g) -> p d g", d=DIRS)
        h_ps = small[:, HC:HC + DIRS * BH * C].rearrange("p (d b c) -> p d b c", d=DIRS, b=BH)
        pb_ps = small[:, PB:PB + BH * Q].rearrange("p (b q) -> p b q", b=BH)
        proj_bank = [bank[2], bank[3], bank[4], bank[5]]
        t_bank = [bank[0], bank[1]]
        y_bank = [bank[6], bank[0]]
        dab_bank = [bank[2], bank[3]]
        g_bank = [bank[4], bank[5]]
        ms_bank = [bank[2], bank[3]]
        PE_TAPS = [0, 1, 2, 3, 4]
        DVE_TAPS = [5, 6, 7, 8]

        def blocks(ap):
            return ap.rearrange("p (k q) -> p k q", q=Q)

        def back(ap):
            n = ap.shape[-1]
            return ap[:, n - 1::-1] if len(ap.shape) == 2 else ap[:, :, n - 1::-1]

        @block.sync
        def _(sp):
            sp.dma_start(x4[:, :], x_in).then_inc(S["x_in"], 16)
            sp.dma_start(tiles["pb"][:, :], pb_in).then_inc(S["pb_in"], 16)
            sp.dma_start(tiles["pc"][:, :], pc_in).then_inc(S["pc_in"], 16)
            sp.dma_start(tiles["pd"][:, :], pd_in).then_inc(S["pd_in"], 16)
            for k in range(NBLK):
                sp.wait_ge(S["fin_ready"], k + 1)
                sp.dma_start(out[:, k * Q:(k + 1) * Q], fin[:, k * Q:(k + 1) * Q]).then_inc(S["stored"], 16)
            sp.wait_ge(S["stored"], 16 * NBLK)

        @block.gpsimd
        def _(pool):
            pool.memset(warm[:, :], 0.0).then_inc(S["warmed"], 1)
            pool.memset(o1p[:, :, :, :], 0.0).then_inc(S["zeroed"], 1)
            pool.memset(o4[:, :, :], 0.0).then_inc(S["zeroed"], 1)
            pool.memset(proj_w[:, :, :, :], 0.0).then_inc(S["zeroed"], 1)
            pool.memset(cbd[:, :, :, :, :], 0.0).then_inc(S["zeroed"], 1)
            pool.memset(vaug[:, :, :, C:C + 1], 1.0).then_inc(S["zeroed"], 1)

        @block.scalar
        def _(act):
            act.dma_start(tiles["pa"][:, :], pa_in).then_inc(S["pa_in"], 16)
            act.preload_act_table(ACT.Silu)
            act.wait_ge(S["zeroed"], 1)
            act.wait_ge(S["pa_in"], 16)
            act.wait_ge(S["lin1_done"], 1)
            act.activation(o1p[:, :, 1:H + 1, 1:W + 1],
                           bank[0][:, :].rearrange("p (b h w) -> p b h w", b=BH, h=H),
                           ACT.Identity, bias=packs["lin1_b"]).then_inc(S["lin1_copied"], 1)
            act.wait_ge(S["wc_done"], 1)
            act.activation(wc[:, :], bank[2][:, 0:130], ACT.Copy).then_inc(S["wc_copied"], 1)
            act.wait_ge(S["zeroed"], 2)
            act.wait_ge(S["conv_summed"], 2)
            act.activation(o4[:, :, PAD:PAD + L], convs[:, :, :], ACT.Silu, bias=packs["dw_b"])\
               .then_inc(S["silu_done"], 1)
            act.wait_ge(S["pb_in"], 16)
            act.wait_ge(S["zeroed"], 4)
            for d in range(DIRS):
                for g in range(2):
                    n = 2 * d + g
                    act.wait_ge(S["proj_done"], n + 1)
                    ps = proj_bank[n][:, :].rearrange("p (b l) -> p b l", b=BH)
                    dst = (s1, s2)[g]
                    act.activation(dst[:, d, :, :], ps, ACT.Silu, bias=packs["conv_b"][:, n:n + 1])\
                       .then_inc(S["proj_silu"], 1)
                    if g == 1:
                        for q in range(BQ):
                            r = slice(C * q, C * q + DI)
                            act.activation(cbd[r, d, :, q, :], blocks(proj_bank[n][r, :]), ACT.Silu,
                                           bias=packs["conv_b"][r, n:n + 1]).then_inc(S["cbd_ready"], 1)
            act.preload_act_table_set("natural_log_exp_and_others")
            act.activation(neg_a[:, :], packs["a_log"], ACT.Exp).then_inc(S["neg_a_ready"], 1)
            act.wait_ge(S["dt_step"], 2)
            act.activation(dtx_[:, 2, :], dtx_[:, 1, :], ACT.Exp).then_inc(S["dt_act"], 1)
            act.wait_ge(S["dt_act"], 1)
            act.activation(dtx_[:, 3, :], dtx_[:, 2, :], ACT.Ln, bias=1.0).then_inc(S["dt_act"], 1)
            act.wait_ge(S["a_ready"], 1)
            act.activation(da[:, :], a_tok[:, :], ACT.Exp).then_inc(S["da_ready"], 1)
            act.wait_ge(S["cum_done"], 2)
            for d in range(DIRS):
                for bh in range(BH):
                    k = blk_of(d, bh, 1)
                    act.activation(pfx[:, d, bh, :, :],
                                   cum_ps[:, d, BQ * k:BQ * k + BQ].rearrange("p (q o) -> p q o", o=1)
                                   .to_broadcast([P, BQ, C]), ACT.Exp).then_inc(S["pfx_ready"], 1)
            for d in range(DIRS):
                act.wait_ge(S["h_done"], BH * BQ * (d + 1))
                act.activation(hst[:, d, :, :], h_ps[:, d, :, :], ACT.Copy).then_inc(S["h_copied"], 1)
            for d in range(DIRS):
                act.wait_ge(S["yg_ready"], d + 1)
                act.activation(ysq[:, d, :], yg[:, d, :], ACT.Square).then_inc(S["ysq_ready"], 1)
            for d in range(DIRS):
                act.wait_ge(S["yms_done"], d + 1)
                act.activation(yln[:, d, :], ms_bank[d][:, :], ACT.Ln, bias=eps_t[:, 0:1]).then_inc(S["yln_ready"], 1)
                act.wait_ge(S["yln_ready"], d + 1)
                act.activation(yrs[:, d, :], yln[:, d, :], ACT.Exp, scale=-0.5).then_inc(S["yrs_ready"], 1)
            act.wait_ge(S["bn_step"], 6)
            act.activation(bsm[:, 1:2], bsm[:, 0:1], ACT.Ln, bias=eps_t[:, 0:1]).then_inc(S["bn_act"], 1)
            act.wait_ge(S["bn_act"], 1)
            act.activation(bsm[:, 2:3], bsm[:, 1:2], ACT.Exp, scale=-0.5).then_inc(S["bn_act"], 1)
            act.wait_ge(S["u4_ready"], 1)
            act.activation(g1[:, :], u4[:, :], ACT.Exp, scale=-1.0).then_inc(S["gate_step"], 1)
            act.wait_ge(S["gate_step"], 1)
            act.activation(g2[:, :], g1[:, :], ACT.Ln, bias=1.0).then_inc(S["gate_step"], 1)
            act.wait_ge(S["gate_step"], 2)
            act.activation(g3[:, :], g2[:, :], ACT.Exp, scale=-1.0).then_inc(S["gate_step"], 1)
            act.wait_ge(S["cen_done"], 1)
            act.activation(c1sq[:, :], bank[6][:, :], ACT.Square).then_inc(S["csq_ready"], 1)
            act.wait_ge(S["var_done"], 1)
            act.activation(l1[:, :], bank[7][:, :], ACT.Ln, bias=eps_t[:, 0:1]).then_inc(S["ln1_step"], 1)
            act.wait_ge(S["ln1_step"], 1)
            act.activation(l1r[:, :], l1[:, :], ACT.Exp, scale=-0.5).then_inc(S["ln1_step"], 1)
            act.wait_ge(S["q_done"], 1)
            act.activation(at_[:, :], bank[1][:, :], ACT.Copy).then_inc(S["q_copied"], 1)
            for b in range(B):
                act.wait_ge(S["nmax_ready"], 2 * b + 2)
                sc = bank[3 + b % 3]
                act.activation(prob[:, b, 0:Q], sc[:, 0:Q], ACT.Exp, bias=nmax[:, b, 0:1]).then_inc(S["prob_ready"], 1)
                act.activation(prob[:, b, Q:3 * Q], sc[:, Q:3 * Q], ACT.Exp, bias=nmax[:, b, 1:2])\
                   .then_inc(S["prob_ready"], 1)
                act.wait_ge(S["pt_done"], b + 1)
                act.activation(probt[:, b, :], bank[6 + b % 2][:, 0:384], ACT.Copy).then_inc(S["pt_copied"], 1)
            act.wait_ge(S["ln2_step"], 3)
            act.activation(t2q[:, :, :, :], t2c[:, :, :, :], ACT.Square).then_inc(S["ln2_act"], 1)
            act.wait_ge(S["ln2_step"], 4)
            act.activation(t2l[:, :, :], t2v[:, :, :], ACT.Ln, scale=1.0 / C, bias=eps_t[:, 0:1])\
               .then_inc(S["ln2_act"], 1)
            act.wait_ge(S["ln2_act"], 2)
            act.activation(t2r[:, :, :], t2l[:, :, :], ACT.Exp, scale=-0.5).then_inc(S["ln2_act"], 1)
            act.wait_ge(S["h2t_done"], 4)
            act.activation(h2t[:, :], bank[0][:, :], ACT.Copy).then_inc(S["h2t_copied"], 1)
            act.wait_ge(S["route_step"], 6)
            act.activation(lg1[:, 4, :], lg1[:, 3, :], ACT.Exp).then_inc(S["route_act"], 1)
            act.wait_ge(S["wt_done"], 1)
            act.activation(wtt[:, :], bank[2][:, 0:P], ACT.Copy).then_inc(S["wt_copied"], 1)
            for k in range(NBLK):
                act.wait_ge(S["mixed"], k + 1)
                act.activation(fin[:, k * Q:(k + 1) * Q], bank[6 + k % 2][:, 0:Q], ACT.Copy)\
                   .then_inc(S["fin_ready"], 1)

        @block.tensor
        def _(pe):
            pe.wait_ge(S["warmed"], 1)
            for _ in range(8):
                pe.matmul(bank[7][:, :], warm[:, 0:P], warm[:, :], start=True, stop=True)
            pe.wait_ge(S["pa_in"], 16)
            pe.wait_ge(S["x_in"], 16)
            pe.matmul(bank[0][:, :], packs["lin1"], x4[:, :], start=True, stop=True).then_inc(S["lin1_done"], 1)
            pe.wait_ge(S["pb_in"], 16)
            pe.matmul(bank[2][:, 0:130], packs["fc_in_t"][0:C, :], packs["mam_in"][0:C, :],
                      start=True, stop=True).then_inc(S["wc_done"], 1)
            pe.wait_ge(S["diag_ready"], len(PE_TAPS))
            pe.wait_ge(S["lin1_copied"], 1)
            for i, t in enumerate(PE_TAPS):
                mm = pe.matmul(bank[1][:, :], diag[:, t, :],
                               o1p[:, :, t // 3:t // 3 + H, t % 3:t % 3 + W],
                               start=(i == 0), stop=(i == len(PE_TAPS) - 1))
            mm.then_inc(S["conv_part"], 1)
            pe.wait_ge(S["pc_in"], 16)
            for d in range(DIRS):
                pe.matmul(bank[6][:, P * d:P * d + P], packs["out_t"][0:C, P * d:P * d + P],
                          packs["fc_out"][0:C, :], start=True, stop=True)
            pe.matmul(bank[6][:, 2 * P:3 * P], packs["wq_t"][0:C, :], packs["wk_t"][0:C, :],
                      start=True, stop=True).then_inc(S["fold_done"], 1)
            pe.wait_ge(S["silu_done"], 1)
            pe.wait_ge(S["dt_w_ready"], 1)
            for bh in range(BH):
                for c in range(NC):
                    k = NC * bh + c
                    mm = pe.matmul(dt_ps[:, 8 * k:8 * k + 8], o4[:, bh, PAD + Q * c:PAD + Q * c + Q],
                                   dt_w[:, :, :], start=True, stop=True)
            mm.then_inc(S["dt_done"], 1)
            pe.wait_ge(S["wc_copied"], 1)
            pe.wait_ge(S["proj_w_ready"], BQ)
            for d in range(DIRS):
                for g in range(2):
                    n = 2 * d + g
                    for k in range(TAPS1):
                        at = k if d == 0 else 2 * PAD - k
                        mm = pe.matmul(proj_bank[n][:, :], proj_w[:, n * TAPS1 + k, :, :], o4[:, :, at:at + L],
                                       start=(k == 0), stop=(k == TAPS1 - 1))
                    mm.then_inc(S["proj_done"], 1)
            pe.wait_ge(S["a_ready"], 1)
            for d in range(DIRS):
                pe.matmul(cum_ps[:, d, :], packs["tri"][:, P * d:P * d + P],
                          a_tok[:, :].rearrange("p (k d q) -> p d k q", d=DIRS, q=BQ)[:, d, :, :],
                          start=True, stop=True).then_inc(S["cum_done"], 1)

            def transposed(d):
                pe.wait_ge(S["proj_silu"], 2 * d + 1)
                for k in range(NBLK):
                    mm = pe.transpose(t_bank[d][:, Q * k:Q * k + Q], s1[:, d, k // NC, Q * (k % NC):Q * (k % NC) + Q],
                                      packs["ident"])
                mm.then_inc(S["s1t_done"], 1)

            def decays(i):
                d, bh, step = groups[i]
                k = blk_of(d, bh, step)
                pe.wait_ge(S["da_masked"], 1)
                if i < 2:
                    pe.wait_ge(S["proj_silu"], 2)
                    pe.wait_ge(S["cbd_ready"], BQ)
                else:
                    pe.wait_ge(S["scanned"], i - 1)
                for q in range(BQ):
                    col = 8 * k + 4 * d + q
                    mm = pe.transpose(dab_bank[i % 2][:, Q * q:Q * q + Q],
                                      da[:, col:col + 1].to_broadcast([P, P]),
                                      packs["ident"] if d == 0 else packs["rev"])
                mm.then_inc(S["dab_done"], 1)

            def products(i):
                d, bh, step = groups[i]
                k = blk_of(d, bh, step)
                if i < 2:
                    pe.wait_ge(S["proj_silu"], 4)
                    pe.wait_ge(S["cbd_ready"], 2 * BQ)
                else:
                    pe.wait_ge(S["m_ready"], i - 1)
                c = cbd[:, d, k, :, :]
                pe.matmul(g_bank[i % 2][:, :], s1[:, d, bh, Q * (k % NC):Q * (k % NC) + Q],
                          c if d == 0 else back(c), start=True, stop=True).then_inc(S["g_done"], 1)

            def prefix_rows(d):
                pe.wait_ge(S["pfx_ready"], DIRS * BH)
                if d == 1:
                    pe.wait_ge(S["h_copied"], 1)
                for bh in range(BH):
                    mm = pe.transpose(pb_ps[:, bh, :], pfx[:, d, bh, :, :].rearrange("p q c -> p (q c)"),
                                      packs["ident"])
                mm.then_inc(S["pfxb_done"], 1)

            def states(d):
                pe.wait_ge(S["dtbx_ready"], d + 1)
                pe.wait_ge(S["wbx_ready"], BH * (d + 1))
                pe.wait_ge(S["cpfx_ready"], d + 1)
                for bh in range(BH):
                    k = blk_of(d, bh, 0)
                    for q in range(BQ):
                        pe.matmul(h_ps[C * q:C * q + C, d, bh, :], dtbx[:, d, k, q, :], wbx[:, d, bh, q, :],
                                  start=True, stop=True).then_inc(S["h_done"], 1)

            def outputs(i):
                d, bh, step = groups[i]
                k = blk_of(d, bh, step)
                if d == 1 and bh == 0 and step == 0:
                    pe.wait_ge(S["dtbx_ready"], 1)
                    pe.wait_ge(S["wbx_ready"], BH)
                pe.wait_ge(S["m_ready"], i + 1)
                pe.wait_ge(S["dtbx_ready"], d + 1)
                if step == 1:
                    pe.wait_ge(S["h_copied"], d + 1)
                    pe.wait_ge(S["cpfx_ready"], d + 1)
                for q in range(BQ):
                    y = y_bank[d][C * q:C * q + C, Q * k:Q * k + Q]
                    m = mmat[:, i, q, :]
                    mm = pe.matmul(y, dtbx[:, d, k, q, :], m if d == 0 else back(m), start=True, stop=(step == 0))
                    if step == 1:
                        r = slice(C * q, C * q + DI)
                        mm = pe.matmul(y, hst[r, d, bh, :], cpfx[r, d, bh, :], start=False, stop=True)
                mm.then_inc(S["y_done"], 1)

            transposed(0)
            decays(0)
            products(0)
            decays(1)
            products(1)
            transposed(1)
            prefix_rows(0)
            for i in range(2, 4):
                decays(i)
                products(i)
                if groups[i - 2][2] == 0:
                    outputs(i - 2)
            states(0)
            prefix_rows(1)
            for i in range(4, 6):
                decays(i)
                products(i)
            outputs(1)
            outputs(2)
            outputs(3)
            for i in range(6, 8):
                decays(i)
                products(i)
            outputs(4)
            states(1)
            outputs(6)
            outputs(5)
            outputs(7)

            for d in range(DIRS):
                pe.wait_ge(S["ysq_ready"], d + 1)
                pe.wait_ge(S["scanned"], 7 + d)
                pe.matmul(ms_bank[d][:, :], packs["mean16"], ysq[:, d, :], start=True, stop=True)\
                  .then_inc(S["yms_done"], 1)
            pe.wait_ge(S["out_w_ready"], 2)
            pe.wait_ge(S["m_ready"], 8)
            for d in range(DIRS):
                pe.wait_ge(S["yn_ready"], d + 1)
                mm = pe.matmul(bank[4][:, :], out_w[:, d, :], yn[:, d, :], start=(d == 0), stop=(d == 1))
            mm.then_inc(S["o_done"], 1)
            pe.wait_ge(S["bn_step"], 4)
            pe.matmul(bank[5][:, 0:2], packs["bn_avg"], bme[:, :], start=True, stop=True).then_inc(S["bn_avg_done"], 1)
            pe.wait_ge(S["obn_ready"], 1)
            pe.matmul(bank[5][:, :], packs["conv4"], obn[:, :], start=True, stop=True).then_inc(S["conv4_done"], 1)
            pe.wait_ge(S["x1_ready"], 1)
            pe.matmul(bank[6][:, :], packs["centre"], x1[:, :], start=True, stop=True).then_inc(S["cen_done"], 1)
            for k in range(NBLK):
                mm = pe.transpose(bank[0][:, Q * k:Q * k + Q], x1[:, Q * k:Q * k + Q], packs["ident"])
            mm.then_inc(S["x1t_done"], 1)
            pe.wait_ge(S["csq_ready"], 1)
            pe.matmul(bank[7][:, :], packs["mean32"], c1sq[:, :], start=True, stop=True).then_inc(S["var_done"], 1)
            pe.wait_ge(S["h1_ready"], 1)
            pe.wait_ge(S["mq_ready"], 1)
            pe.matmul(bank[1][:, :], mq[:, :], h1[:, :], start=True, stop=True).then_inc(S["q_done"], 1)
            for k in range(NBLK):
                mm = pe.matmul(bank[2][:, Q * k:Q * k + Q], h1[:, Q * k:Q * k + Q], packs["wv"], start=True, stop=True)
            mm.then_inc(S["v_done"], 1)

            def scores(b):
                bh, q = b // BQ, b % BQ
                r = slice(C * q, C * q + C)
                sc = bank[3 + b % 3]
                if b == 0:
                    pe.wait_ge(S["bf_ready"], 2)
                    pe.wait_ge(S["q_copied"], 1)
                    pe.wait_ge(S["u4_ready"], 1)
                if b >= 3:
                    pe.wait_ge(S["prob_ready"], 2 * (b - 2))
                pe.matmul(sc[:, 0:384], idb[:, :], caus[:, :], start=True, stop=False)
                pe.matmul(sc[:, 0:Q], at_[r, L * bh:L * bh + Q], h1[r, L * bh:L * bh + Q], start=False, stop=False)
                pe.matmul(sc[:, Q:3 * Q], at_[r, L * bh + Q:L * bh + 2 * Q], h1[r, L * bh:L * bh + L],
                          start=False, stop=True).then_inc(S["s_done"], 1)

            def turn(b):
                pe.wait_ge(S["prob_ready"], 2 * (b + 1))
                if b >= 2:
                    pe.wait_ge(S["pt_copied"], b - 1)
                if b < 2:
                    pe.wait_ge(S["h1_ready"], 1)
                for k in range(3):
                    mm = pe.transpose(bank[6 + b % 2][:, Q * k:Q * k + Q], prob[:, b, Q * k:Q * k + Q], packs["ident"])
                mm.then_inc(S["pt_done"], 1)

            def attend(b):
                bh, q = b // BQ, b % BQ
                pe.wait_ge(S["pt_copied"], b + 1)
                if b == 0:
                    pe.wait_ge(S["v_copied"], 1)
                o = bank[1 + bh][:, 0:NC * BQ * (C + 1)].rearrange("p (c q e) -> p c q e", c=NC, q=BQ)
                v = [vaug[:, NC * bh + c, q, :] for c in range(NC)]
                pe.matmul(o[:, 0, q, :], probt[:, b, 0:Q], v[0], start=True, stop=True)
                pe.matmul(o[:, 1, q, :], probt[:, b, Q:2 * Q], v[0], start=True, stop=False)
                pe.matmul(o[:, 1, q, :], probt[:, b, 2 * Q:3 * Q], v[1], start=False, stop=True)\
                  .then_inc(S["o_att_done"], 1)

            for b in range(B + 3):
                if b < B:
                    scores(b)
                if 2 <= b < B + 2:
                    turn(b - 2)
                if b >= 3:
                    attend(b - 3)

            pe.wait_ge(S["h2_ready"], 1)
            pe.wait_ge(S["x1t_copied"], 1)
            for k in range(NBLK):
                pe.transpose(bank[0][:, Q * k:Q * k + Q], h2[:, k, :, :], packs["ident"]).then_inc(S["h2t_done"], 1)
            pe.wait_ge(S["h2t_copied"], 1)
            pe.wait_ge(S["pd_in"], 16)
            pe.wait_ge(S["t2_ready"], 2)
            for k in range(NBLK):
                mm = pe.matmul(bank[1][:, 32 * k:32 * k + 32], h2t[:, Q * k:Q * k + Q], packs["router"],
                               start=True, stop=True)
            mm.then_inc(S["router_done"], 1)

            def experts(j):
                q, half = j % BQ, j // BQ
                r = slice(C * q, C * q + C)
                if j >= 4:
                    pe.wait_ge(S["mix_ready"], j - 3)
                for i in range(2):
                    k = 2 * half + i
                    mm = pe.matmul(bank[2 + (j + 1) % 4][:, 256 * i:256 * i + 256], h2t[r, Q * k:Q * k + Q],
                                   packs["experts"][r, :], start=True, stop=True)
                mm.then_inc(S["e_done"], 1)

            def mixed(k):
                o = bank[6 + k % 2][:, 0:Q]
                pe.wait_ge(S["mix_ready"], BQ * (k // 2) + BQ)
                if k >= 2:
                    pe.wait_ge(S["fin_ready"], k - 1)
                pe.matmul(o, t2[:, k, :, :], packs["ident"], start=True, stop=False)
                for e in range(E):
                    pe.matmul(o, mix[:, k, e, :, :], packs["ident"], start=False, stop=False)
                pe.matmul(o, packs["experts_b"][32 * k:32 * k + 32, :], wtt[32 * k:32 * k + 32, :],
                          start=False, stop=True).then_inc(S["mixed"], 1)

            for j in range(3):
                experts(j)
            pe.wait_ge(S["w_ready"], 1)
            pe.transpose(bank[2][:, 0:P], wtok[:, :, :], packs["ident"]).then_inc(S["wt_done"], 1)
            pe.wait_ge(S["wt_copied"], 1)
            for j in range(3, 8):
                experts(j)
                if j == 5:
                    mixed(0)
                if j == 6:
                    mixed(1)
            mixed(2)
            mixed(3)

        @block.vector
        def _(dve):
            dve.memset(eps_t[:, :], EPS).then_inc(S["wsel"], 1)
            dve.wait_ge(S["pa_in"], 16)
            for t in PE_TAPS:
                dve.tensor_scalar(diag[:, t, :], packs["ident"], packs["dw"][:, t:t + 1], None, ALU.mult)\
                   .then_inc(S["diag_ready"], 1)
            dve.wait_ge(S["lin1_copied"], 1)
            steps = 0
            for i, t in enumerate(DVE_TAPS):
                for bh in range(BH):
                    win = o1p[:, bh, t // 3:t // 3 + H, t % 3:t % 3 + W]
                    to = conv[:, i % 2, bh, :].rearrange("p (h w) -> p h w", h=H)
                    if i == 0:
                        dve.tensor_scalar(to, win, packs["dw"][:, t:t + 1], None, ALU.mult)\
                           .then_inc(S["taps_done"], 1)
                    else:
                        dve.wait_ge(S["taps_done"], steps - 1)
                        dve.scalar_tensor_tensor(to, win, packs["dw"][:, t:t + 1],
                                                 conv[:, (i + 1) % 2, bh, :].rearrange("p (h w) -> p h w", h=H),
                                                 ALU.mult, ALU.add).then_inc(S["taps_done"], 1)
                    steps += 1
            dve.wait_ge(S["conv_part"], 1)
            dve.wait_ge(S["taps_done"], steps)
            for bh in range(BH):
                dve.tensor_tensor(convs[:, bh, :], bank[1][:, L * bh:L * bh + L],
                                  conv[:, (len(DVE_TAPS) + 1) % 2, bh, :], ALU.add).then_inc(S["conv_summed"], 1)
            dve.wait_ge(S["pb_in"], 16)
            dve.wait_ge(S["wc_copied"], 1)
            dve.tensor_tensor(dt_w[:, :, :],
                              wc[:, 128:130].rearrange("p (d o) -> p d o", o=1).to_broadcast([P, DIRS, BQ]),
                              packs["mask4"].rearrange("p (o q) -> p o q", o=1).to_broadcast([P, DIRS, BQ]),
                              ALU.mult).then_inc(S["dt_w_ready"], 1)
            dve.wait_ge(S["zeroed"], 3)
            for q in range(BQ):
                r = slice(C * q, C * q + C)
                dve.tensor_tensor(proj_w[r, :, q, :].rearrange("p (g k) c -> p g k c", k=TAPS1),
                                  wc[r, 0:128].rearrange("p (g o c) -> p g o c", o=1, c=C).to_broadcast([C, 4, TAPS1, C]),
                                  packs["taps"][r, :].rearrange("p (g k c) -> p g k c", g=4, k=TAPS1),
                                  ALU.mult).then_inc(S["proj_w_ready"], 1)
            dve.wait_ge(S["dt_done"], 1)
            dve.tensor_tensor(dtx_[:, 0, :], dt_ps, packs["dt_bias"], ALU.add).then_inc(S["dt_step"], 1)
            dve.wait_ge(S["dt_step"], 1)
            dve.scalar_tensor_tensor(dtx_[:, 1, :], dtx_[:, 0, :], -1.0, dtx_[:, 0, :], ALU.mult, ALU.min).then_inc(S["dt_step"], 1)
            dve.wait_ge(S["fold_done"], 1)
            dve.wait_ge(S["pc_in"], 16)
            for d in range(DIRS):
                dve.scalar_tensor_tensor(out_w[:, d, :], bank[6][:, P * d:P * d + P], packs["norm_w"][:, d:d + 1],
                                         packs["mask"], ALU.mult, ALU.mult).then_inc(S["out_w_ready"], 1)
            dve.scalar_tensor_tensor(mq[:, :], bank[6][:, 2 * P:3 * P], float(C) ** -0.5, packs["mask"],
                                     ALU.mult, ALU.mult).then_inc(S["mq_ready"], 1)
            dve.tensor_copy(idb[:, :], packs["ident"]).then_inc(S["bf_ready"], 1)
            dve.tensor_copy(caus[:, :], packs["causal"]).then_inc(S["bf_ready"], 1)
            for q in range(BQ):
                dve.tensor_copy(data1[:, 0, Q * q:Q * q + Q], packs["ident"]).then_inc(S["data1_ready"], 1)
                dve.tensor_copy(data1[:, 1, Q * q:Q * q + Q], packs["rev"]).then_inc(S["data1_ready"], 1)
            dve.wait_ge(S["dt_act"], 2)
            dve.scalar_tensor_tensor(dtx_[:, 4, :], dtx_[:, 0, :], 0.0, dtx_[:, 3, :], ALU.max, ALU.add)\
               .then_inc(S["dt_step"], 1)
            dve.wait_ge(S["dt_step"], 3)
            dve.wait_ge(S["neg_a_ready"], 1)
            dve.scalar_tensor_tensor(a_tok[:, :], dtx_[:, 4, :], -1.0, neg_a[:, :], ALU.mult, ALU.mult)\
               .then_inc(S["a_ready"], 1)
            dve.wait_ge(S["da_ready"], 1)
            dve.tensor_tensor(da[:, :], da[:, :], packs["keep_da"], ALU.mult).then_inc(S["da_masked"], 1)
            dt_kdq = dtx_[:, 4, :].rearrange("p (k d q) -> p d k q", d=DIRS, q=BQ)

            def scan(i):
                d = groups[i][0]
                dve.wait_ge(S["dab_done"], i + 1)
                dve.wait_ge(S["data1_ready"], 2 * BQ)
                dve.tensor_tensor_scan(lmat[:, i, :], dab_bank[i % 2][:, :], data1[:, d, :], 0.0,
                                       ALU.mult, ALU.add).then_inc(S["scanned"], 1)

            def times(i):
                dve.wait_ge(S["g_done"], i + 1)
                dve.wait_ge(S["scanned"], i + 1)
                dve.tensor_tensor(mmat[:, i, :, :], g_bank[i % 2][:, :].rearrange("p (q t) -> p q t", q=BQ),
                                  lmat[:, i, :].rearrange("p (q t) -> p q t", q=BQ), ALU.mult)\
                   .then_inc(S["m_ready"], 1)

            def weigh(d):
                dve.wait_ge(S["s1t_done"], d + 1)
                dve.tensor_tensor(dtbx[:, d, :, :, :].rearrange("p k q c -> p (k q) c"),
                                  t_bank[d][:, :].rearrange("p (k c) -> p k c", c=C),
                                  dt_flat(d), ALU.mult).then_inc(S["dtbx_ready"], 1)

            def dt_flat(d):
                return dtx_[:, 5 + d, 0:16].rearrange("p (k o) -> p k o", o=1).to_broadcast([P, 16, C])

            def keep(d, bh):
                i = groups.index((d, bh, 0))
                k = blk_of(d, bh, 0)
                dve.wait_ge(S["scanned"], i + 1)
                dve.wait_ge(S["s1t_done"], d + 1)
                last = lmat[:, i, Q - 1::Q]
                dve.tensor_tensor(wbx[:, d, bh, :, :],
                                  t_bank[d][:, Q * k:Q * k + Q].rearrange("p (q c) -> p q c", c=C),
                                  last.rearrange("p (q o) -> p q o", o=1).to_broadcast([P, BQ, C]),
                                  ALU.mult).then_inc(S["wbx_ready"], 1)

            def prefix(d):
                dve.wait_ge(S["pfxb_done"], d + 1)
                c1 = 1 if d == 0 else 0
                dve.wait_ge(S["proj_silu"], 2 * d + 2)
                dve.tensor_tensor(cpfx[:, d, :, :], pb_ps,
                                  s2[:, d, :, Q * c1:Q * c1 + Q], ALU.mult).then_inc(S["cpfx_ready"], 1)

            def gated(d):
                dve.wait_ge(S["y_done"], 4 * (d + 1))
                dve.scalar_tensor_tensor(yd[:, d, :], s1[:, d, :, :].rearrange("p b l -> p (b l)"),
                                         packs["skip_d"][:, d:d + 1], y_bank[d][:, :], ALU.mult, ALU.add)\
                   .then_inc(S["yd_ready"], 1)
                dve.wait_ge(S["yd_ready"], d + 1)
                dve.tensor_tensor(yg[:, d, :], yd[:, d, :], s2[:, d, :, :].rearrange("p b l -> p (b l)"), ALU.mult)\
                   .then_inc(S["yg_ready"], 1)

            for d in range(DIRS):
                dve.tensor_copy(dtx_[:, 5 + d, 0:16].rearrange("p (k q) -> p k q", q=BQ), dt_kdq[:, d, :, :])\
                   .then_inc(S["dt_step"], 1)
            dve.wait_ge(S["dt_step"], 5)
            weigh(0)
            scan(0)
            times(0)
            scan(1)
            times(1)
            scan(2)
            keep(0, 0)
            prefix(0)
            times(2)
            scan(3)
            keep(0, 1)
            times(3)
            scan(4)
            weigh(1)
            times(4)
            prefix(1)
            scan(5)
            times(5)
            scan(6)
            keep(1, 0)
            keep(1, 1)
            times(6)
            scan(7)
            times(7)
            gated(0)
            gated(1)
            for d in range(DIRS):
                dve.wait_ge(S["yrs_ready"], d + 1)
                dve.tensor_tensor(yn[:, d, :], yg[:, d, :], yrs[:, d, :], ALU.mult).then_inc(S["yn_ready"], 1)
            dve.wait_ge(S["o_done"], 1)
            dve.bn_stats(bst[:, :], bank[4][:, :]).then_inc(S["bn_step"], 1)
            dve.wait_ge(S["bn_step"], 1)
            dve.bn_aggr(bmv[:, :], bst[:, :]).then_inc(S["bn_step"], 1)
            dve.wait_ge(S["bn_step"], 2)
            dve.tensor_copy(bme[:, 0:1], bmv[:, 0:1]).then_inc(S["bn_step"], 1)
            dve.scalar_tensor_tensor(bme[:, 1:2], bmv[:, 0:1], bmv[:, 0:1], bmv[:, 1:2], ALU.mult, ALU.add)\
               .then_inc(S["bn_step"], 1)
            dve.wait_ge(S["bn_avg_done"], 1)
            dve.tensor_copy(bm[:, :], bank[5][:, 0:2]).then_inc(S["bn_step"], 1)
            dve.wait_ge(S["bn_step"], 5)
            dve.tensor_tensor(bsm[:, 3:4], bm[:, 0:1], bm[:, 0:1], ALU.mult).then_inc(S["dt_step"], 1)
            dve.wait_ge(S["dt_step"], 6)
            dve.tensor_tensor(bsm[:, 0:1], bm[:, 1:2], bsm[:, 3:4], ALU.subtract).then_inc(S["bn_step"], 1)
            dve.wait_ge(S["bn_act"], 2)
            dve.tensor_tensor(bsm[:, 4:5], packs["bn_g"], bsm[:, 2:3], ALU.mult).then_inc(S["bn_step"], 1)
            dve.wait_ge(S["bn_step"], 7)
            dve.tensor_tensor(bsm[:, 5:6], bm[:, 0:1], bsm[:, 4:5], ALU.mult).then_inc(S["bn_step"], 1)
            dve.wait_ge(S["bn_step"], 8)
            dve.tensor_tensor(bsm[:, 6:7], packs["bn_b"], bsm[:, 5:6], ALU.subtract).then_inc(S["bn_step"], 1)
            dve.wait_ge(S["bn_step"], 9)
            dve.tensor_scalar(obn[:, :], bank[4][:, :], bsm[:, 4:5], bsm[:, 6:7], ALU.mult, ALU.add)\
               .then_inc(S["obn_ready"], 1)
            dve.wait_ge(S["conv4_done"], 1)
            dve.tensor_scalar(u4[:, :], bank[5][:, :], packs["conv4_b"], SIG_CLAMP, ALU.add, ALU.max)\
               .then_inc(S["u4_ready"], 1)
            dve.wait_ge(S["gate_step"], 3)
            dve.scalar_tensor_tensor(x1[:, :], g3[:, :], 1.0, x4[:, :], ALU.add, ALU.mult).then_inc(S["x1_ready"], 1)
            dve.wait_ge(S["x1t_done"], 1)
            dve.tensor_copy(x1t[:, :, :, :].rearrange("p k q c -> p (k q c)"), bank[0][:, :]).then_inc(S["x1t_copied"], 1)
            dve.wait_ge(S["ln1_step"], 2)
            dve.tensor_tensor(h1[:, :], bank[6][:, :], l1r[:, :], ALU.mult).then_inc(S["h1_ready"], 1)
            dve.wait_ge(S["v_done"], 1)
            dve.wait_ge(S["zeroed"], 5)
            dve.tensor_copy(vaug[:, :, :, 0:C].rearrange("p k q c -> p (k q) c"),
                            bank[2][:, :].rearrange("p (k c) -> p k c", c=C)).then_inc(S["v_copied"], 1)
            for b in range(B):
                dve.wait_ge(S["s_done"], b + 1)
                sc = bank[3 + b % 3]
                dve.tensor_reduce(nmax[:, b, 0:1], sc[:, 0:Q], AX_X, ALU.max, negate=True).then_inc(S["nmax_ready"], 1)
                dve.tensor_reduce(nmax[:, b, 1:2], sc[:, Q:3 * Q], AX_X, ALU.max, negate=True)\
                   .then_inc(S["nmax_ready"], 1)
            for bh in range(BH):
                dve.wait_ge(S["o_att_done"], BQ * (bh + 1))
                o = bank[1 + bh][:, 0:NC * BQ * (C + 1)].rearrange("p (k e) -> p k e", e=C + 1)
                ks = slice(NC * bh, NC * bh + NC)
                dve.reciprocal(rden[:, ks, :].rearrange("p c q -> p (c q)"),
                               o[:, :, C:C + 1].rearrange("p k o -> p (k o)")).then_inc(S["att_step"], 1)
                dve.wait_ge(S["att_step"], 2 * bh + 1)
                dve.tensor_tensor(att[:, ks, :, :].rearrange("p c q e -> p (c q) e"), o[:, :, 0:C],
                                  rden[:, ks, :].rearrange("p c (q o) -> p (c q) o", o=1).to_broadcast([P, NC * BQ, C]),
                                  ALU.mult).then_inc(S["att_step"], 1)
                dve.wait_ge(S["att_step"], 2 * bh + 2)
                dve.wait_ge(S["x1t_copied"], 1)
                dve.tensor_tensor(t2[:, ks, :, :].rearrange("p c q e -> p (c q e)"),
                                  att[:, ks, :, :].rearrange("p c q e -> p (c q e)"),
                                  x1t[:, ks, :, :].rearrange("p c q e -> p (c q e)"), ALU.add).then_inc(S["t2_ready"], 1)
            dve.wait_ge(S["t2_ready"], 2)
            per_tok = lambda t: t[:, :, :].rearrange("p k q -> p (k q)")
            wide = lambda t: t[:, :, :].rearrange("p k (q o) -> p (k q) o", o=1).to_broadcast([P, 16, C])
            tok = lambda t: t[:, :, :, :].rearrange("p k q c -> p (k q) c")
            dve.tensor_reduce(per_tok(t2s), tok(t2), AX_X, ALU.add).then_inc(S["ln2_step"], 1)
            dve.wait_ge(S["ln2_step"], 1)
            dve.tensor_scalar(per_tok(t2m), per_tok(t2s), 1.0 / C, None, ALU.mult).then_inc(S["ln2_step"], 1)
            dve.wait_ge(S["ln2_step"], 2)
            dve.tensor_tensor(tok(t2c), tok(t2), wide(t2m), ALU.subtract).then_inc(S["ln2_step"], 1)
            dve.wait_ge(S["ln2_act"], 1)
            dve.tensor_reduce(per_tok(t2v), tok(t2q), AX_X, ALU.add).then_inc(S["ln2_step"], 1)
            dve.wait_ge(S["ln2_step"], 4)
            dve.wait_ge(S["ln2_act"], 3)
            dve.tensor_tensor(tok(h2), tok(t2c), wide(t2r), ALU.mult).then_inc(S["h2_ready"], 1)

            n = [0]

            def route(ins):
                n[0] += 1
                ins.then_inc(S["route_step"], 1)

            rank = packs["rank"].rearrange("p (k e) -> p k e", e=E)
            over = lambda i: lg1[:, i, :].rearrange("p (k o) -> p k o", o=1).to_broadcast([P, 16, E])
            dve.wait_ge(S["router_done"], 1)
            route(dve.tensor_tensor(lg[:, 0, :, :], bank[1][:, 0:P].rearrange("p (k e) -> p k e", e=E),
                                    packs["router_b"].rearrange("p (k e) -> p k e", e=E), ALU.add))
            dve.wait_ge(S["route_step"], n[0])
            route(dve.tensor_reduce(lg1[:, 0, :], lg[:, 0, :, :], AX_X, ALU.max))
            dve.wait_ge(S["route_step"], n[0])
            dve.tensor_tensor(lg[:, 1, :, :], lg[:, 0, :, :], over(0), ALU.is_equal).then_inc(S["wsel"], 1)
            dve.wait_ge(S["wsel"], 2)
            dve.tensor_tensor(lg[:, 2, :, :], lg[:, 1, :, :], rank, ALU.mult).then_inc(S["wsel"], 1)
            dve.wait_ge(S["wsel"], 3)
            route(dve.tensor_reduce(lg1[:, 1, :], lg[:, 2, :, :], AX_X, ALU.max))
            dve.wait_ge(S["route_step"], n[0])
            dve.tensor_tensor(lg[:, 3, :, :], lg[:, 2, :, :], over(1), ALU.is_equal).then_inc(S["wsel"], 1)
            dve.wait_ge(S["wsel"], 4)
            route(dve.scalar_tensor_tensor(lg[:, 4, :, :], lg[:, 3, :, :], MASKED, lg[:, 0, :, :], ALU.mult, ALU.add))
            dve.wait_ge(S["route_step"], n[0])
            route(dve.tensor_reduce(lg1[:, 2, :], lg[:, 4, :, :], AX_X, ALU.max))
            dve.wait_ge(S["route_step"], n[0])
            route(dve.tensor_tensor(lg1[:, 3, :], lg1[:, 2, :], lg1[:, 0, :], ALU.subtract))
            dve.tensor_tensor(lg[:, 5, :, :], lg[:, 4, :, :], over(2), ALU.is_equal).then_inc(S["wsel"], 1)
            dve.wait_ge(S["wsel"], 5)
            dve.tensor_tensor(lg[:, 6, :, :], lg[:, 5, :, :], rank, ALU.mult).then_inc(S["wsel"], 1)
            dve.wait_ge(S["wsel"], 6)
            dve.tensor_reduce(lg1[:, 5, :], lg[:, 6, :, :], AX_X, ALU.max).then_inc(S["wsel"], 1)
            dve.wait_ge(S["wsel"], 7)
            dve.tensor_tensor(lg[:, 7, :, :], lg[:, 6, :, :], over(5), ALU.is_equal).then_inc(S["wsel"], 1)
            dve.wait_ge(S["route_act"], 1)
            dve.tensor_scalar(lg1[:, 6, :], lg1[:, 4, :], 1.0, None, ALU.add).then_inc(S["wsel"], 1)
            dve.wait_ge(S["wsel"], 9)
            dve.reciprocal(lg1[:, 7, :], lg1[:, 6, :]).then_inc(S["wsel"], 1)
            dve.tensor_tensor(lg[:, 8, :, :], lg[:, 7, :, :], over(4), ALU.mult).then_inc(S["wsel"], 1)
            dve.wait_ge(S["wsel"], 11)
            dve.tensor_tensor(lg[:, 9, :, :], lg[:, 8, :, :], lg[:, 3, :, :], ALU.add).then_inc(S["wsel"], 1)
            dve.wait_ge(S["wsel"], 12)
            dve.tensor_tensor(wtok[:, :, :], lg[:, 9, :, :], over(7), ALU.mult).then_inc(S["w_ready"], 1)
            dve.wait_ge(S["w_ready"], 1)
            w4 = wtok[:, :, :].rearrange("p (k q) e -> p k q e", q=BQ)
            for j in range(8):
                q, half = j % BQ, j // BQ
                dve.wait_ge(S["e_done"], j + 1)
                dve.tensor_tensor(mix[:, 2 * half:2 * half + 2, :, q, :],
                                  bank[2 + (j + 1) % 4][:, :].rearrange("p (k e c) -> p k e c", k=2, e=E),
                                  w4[:, 2 * half:2 * half + 2, q, :].rearrange("p k (e o) -> p k e o", o=1)
                                  .to_broadcast([P, 2, E, C]), ALU.mult).then_inc(S["mix_ready"], 1)


def pack_inputs(inp):
    import numpy as np

    f = np.float32
    g = {k: np.asarray(v) for k, v in inp.items()}
    get = lambda n: g["L0_conv_" + n]
    rows = np.arange(P)
    img, ch = rows // C, rows % C

    def rep(a):
        return np.tile(a.reshape(C, -1), (BQ, 1))

    def bd(a):
        n = a.shape[1]
        o = np.zeros((P, BQ * n), f)
        for q in range(BQ):
            o[C * q:C * q + C, n * q:n * q + n] = a
        return o

    def top(a):
        o = np.zeros((P, a.shape[1]), f)
        o[:C] = a
        return o

    def upper(cols):
        o = np.zeros((P, DIRS), f)
        for d in range(DIRS):
            for q in range(BQ):
                o[C * q + DI:C * q + C, d] = cols[d]
        return o

    v = {}
    v["lin1"] = bd(get("lin1_w"))
    v["ident"] = np.eye(P, dtype=f)
    v["rev"] = np.eye(P, dtype=f)[::-1]
    v["lin1_b"], v["dw_b"], v["dw"] = rep(get("lin1_b")), rep(get("dw_b")), rep(get("dw_w").reshape(C, 9))
    v["fc_in_t"] = top(np.tile(get("fc_in_w").T, (1, BQ)))
    win = get("mam_in_w")
    z, xs, bm, cm, dt = (win[:, :, a:b] for a, b in ((0, 16), (16, 32), (32, 48), (48, 64), (64, 65)))
    v["mam_in"] = top(np.concatenate(
        [np.concatenate([bm[d], xs[d], cm[d], z[d]], 1) for d in range(DIRS)] + [dt[0], dt[1]], 1))
    cw, cb = get("mam_conv_w"), get("mam_conv_b")
    taps = np.zeros((DIRS, 2, TAPS1, C), f)
    conv_b = np.zeros((BQ, C, 4), f)
    for d in range(DIRS):
        taps[d, 0] = np.concatenate([cw[d, 16:32], cw[d, 0:16]]).T
        taps[d, 1, :, :DI] = cw[d, 32:48].T
        taps[d, 1, TAPS1 - 1, DI:] = 1.0
        conv_b[:, :, 2 * d] = np.concatenate([cb[d, 16:32], cb[d, 0:16]])
        conv_b[:, :DI, 2 * d + 1] = cb[d, 32:48]
    v["taps"] = np.tile(taps.reshape(1, -1), (P, 1))
    v["conv_b"] = conv_b.reshape(P, 4)
    v["mask4"] = (img[:, None] == np.arange(BQ)[None]).astype(f)
    per_unit = lambda a: np.tile(np.broadcast_to(a.reshape(1, DIRS, 1), (NBLK, DIRS, BQ)).reshape(1, -1), (P, 1))
    v["dt_bias"], v["a_log"] = per_unit(get("mam_dt_bias")), per_unit(get("mam_A_log"))
    keep = np.ones((P, NBLK, DIRS, BQ), f)
    keep[0, :, 0] = 0.0
    keep[P - 1, :, 1] = 0.0
    v["keep_da"] = keep.reshape(P, 32)
    v["skip_d"] = upper([np.full(DI, get("mam_D")[d, 0], f) for d in range(DIRS)])
    r, t = rows[:, None], rows[None]
    v["tri"] = np.concatenate([(r <= t), (r >= t)], 1).astype(f)
    wo = get("mam_out_w")
    v["out_t"] = np.zeros((P, 2 * P), f)
    for d in range(DIRS):
        for q in range(BQ):
            v["out_t"][:C, P * d + C * q + DI:P * d + C * q + C] = wo[d].T
    v["fc_out"] = top(np.tile(get("fc_out_w"), (1, BQ)))
    v["norm_w"] = upper(list(get("mam_norm_w")))
    same = img[:, None] == img[None]
    v["mask"] = same.astype(f)
    v["mean16"] = (same & (ch[:, None] >= DI)).astype(f) / f(DI)
    v["bn_avg"] = (ch[:, None] == ch[None]).astype(f) / f(BQ)
    v["bn_g"], v["bn_b"], v["conv4_b"] = rep(get("bn_g")), rep(get("bn_b")), rep(get("conv4_b"))
    v["conv4"] = bd(get("conv4_w"))
    v["mean32"] = same.astype(f) / f(C)
    v["centre"] = np.eye(P, dtype=f) - v["mean32"]
    v["wq_t"] = top(np.tile(g["L1_attn_W_Q"].T, (1, BQ)))
    v["wk_t"] = top(np.tile(g["L1_attn_W_K"].T, (1, BQ)))
    v["wv"] = bd(g["L1_attn_W_V"])
    tri = np.where(t > r, f(MASKED), f(0.0)).astype(f)
    v["causal"] = np.concatenate([tri, np.zeros((P, P), f), tri], 1)
    v["router"] = bd(g["L1_ffn_router_w"])
    v["router_b"] = np.tile(g["L1_ffn_router_b"].reshape(1, E), (P, 16))
    v["experts"] = np.tile(g["L1_ffn_expert_w"].transpose(1, 0, 2).reshape(C, E * C), (BQ, 1))
    eb = np.zeros((BQ, E, BQ, C), f)
    for q in range(BQ):
        eb[q, :, q] = g["L1_ffn_expert_b"]
    v["experts_b"] = np.tile(eb.reshape(BQ * E, P), (BQ, 1))
    v["rank"] = np.tile((E - np.arange(E, dtype=f)).reshape(1, E), (P, 16))

    arrays = {"x4": np.ascontiguousarray(
        g["x"].reshape(BH, BQ, C, L).transpose(1, 2, 0, 3).reshape(P, N))}
    for pack, parts in PACKS.items():
        for name, width in parts:
            assert v[name].shape == (P, width), (name, v[name].shape)
        arrays[pack] = np.ascontiguousarray(np.concatenate([v[name] for name, _ in parts], 1).astype(f, copy=False))
    return arrays


def kernel(**inputs):
    import numpy as np
    import concourse.bacc as _bacc
    from concourse import mybir as _mybir
    from concourse.bass_utils import run_bass_kernel_spmd as _run

    arrays = pack_inputs(inputs)
    nc = _bacc.Bacc("TRN2", target_bir_lowering=False, num_devices=1)
    args = [nc.dram_tensor(f"in_{n}", a.shape, _mybir.dt.float32, kind="ExternalInput").ap()
            for n, a in arrays.items()]
    out = nc.dram_tensor("out_0", (P, N), _mybir.dt.float32, kind="ExternalOutput").ap()
    program(nc, *args, out)
    r = _run(nc, [{f"in_{n}": a for n, a in arrays.items()}], core_ids=[0])
    o = r.results[0]["out_0"]
    return np.ascontiguousarray(o.reshape(BQ, C, BH, H, W).transpose(2, 0, 1, 3, 4).reshape(B, C, H, W))
```

```python
from contextlib import ExitStack

import concourse.bass as bass
from concourse import mybir

F32 = mybir.dt.float32
BF16 = mybir.dt.bfloat16
ALU = mybir.AluOpType
ACT = mybir.ActivationFunctionType
AX_X = mybir.AxisListType.X

P = 128
B, C, H, W = 8, 32, 16, 16
L = H * W
BQ = P // C
BH = B // BQ
Q = 128
NC = L // Q
NBLK = BH * NC
N = BH * L
DIRS = 2
DI = 16
TAPS1 = 4
FILL = [0,0,0,0,4,8,3,3,3,3,3,4,0]
FOLDED = 1
PAD = TAPS1 - 1
HP, WP = H + 2, W + 2
E = 8
EPS = 1e-5
MASKED = -1.0e30
SIG_CLAMP = -40.0

PACKS = {
    "pa": [("lin1", 128), ("ident", 128), ("lin1_b", 1), ("dw", 9), ("dw_b", 1)],
    "pb": [("fc_in_t", 128), ("mam_in", 130), ("taps", TAPS1 * C), ("tap_col", 16), ("mask4", 4), ("conv_b", 4),
           ("dt_bias", 32), ("a_log", 32), ("keep_da", 32), ("skip_d", 2), ("rev", 128),
           ("tri", 256)],
    "pc": [("out_t", 256), ("fc_out", 128), ("norm_w", 2), ("mask", 128), ("mean16", 128),
           ("bn_avg", 128), ("bn_g", 1), ("bn_b", 1), ("conv4", 128), ("conv4_b", 1),
           ("centre", 128), ("mean32", 128), ("wq_t", 128), ("wk_t", 128), ("wv", 128),
           ("causal", 384)],
    "pd": [("router", 32), ("router_b", 128), ("experts", 256), ("experts_b", 128), ("rank", 128)],
}


def columns(pack):
    at, out = 0, {}
    for name, width in PACKS[pack]:
        out[name] = (at, at + width)
        at += width
    return out, at


def program(nc, x_in, pa_in, pb_in, pc_in, pd_in, out):
    ctx = ExitStack()
    with ctx:
        def sb(name, shape, dt=F32):
            return ctx.enter_context(nc.sbuf_tensor(name, shape, dt))

        def sem(name):
            return ctx.enter_context(nc.semaphore(name))

        packs = {}
        tiles = {}
        for pack in PACKS:
            where, width = columns(pack)
            tiles[pack] = sb(pack, [P, width])
            for name, (a, b) in where.items():
                packs[name] = tiles[pack][:, a:b]

        x4 = sb("x4", [P, N])
        warm = sb("warm", [P, 512], BF16)
        o1p = sb("o1p", [P, BH, HP, WP])
        diag = sb("diag", [P, 9, P])
        conv = sb("conv", [P, 2, BH, L])
        convs = sb("convs", [P, BH, L])
        o4 = sb("o4", [P, BH, L + 2 * PAD])
        wc = sb("wc", [P, 130])
        proj_w = sb("proj_w", [P, 4, BQ, C])
        fold_w = sb("fold_w", [P, TAPS1, BQ, C])
        dt_w = sb("dt_w", [P, DIRS, BQ])
        pre = sb("pre", [P, 4, BH, L])
        tap3 = sb("tap3", [P, PAD, BH, L])
        s1 = sb("s1", [P, DIRS, BH, L])
        s2 = sb("s2", [P, DIRS, BH, L])
        cbd = sb("cbd", [P, DIRS, NBLK, BQ, Q])
        dt_raw = sb("dt_raw", [P, 32])
        dt_neg = sb("dt_neg", [P, 32])
        dt_exp = sb("dt_exp", [P, 32])
        dt_log = sb("dt_log", [P, 32])
        dt = sb("dt", [P, 32])
        dt_dir = sb("dt_dir", [P, DIRS, NBLK * BQ])
        neg_a = sb("neg_a", [P, 32])
        a_tok = sb("a_tok", [P, 32])
        da = sb("da", [P, 32])
        pfx = sb("pfx", [P, DIRS, BH, BQ, C])
        data1 = sb("data1", [P, DIRS, BQ * Q])
        lmat = sb("lmat", [P, 8, BQ * Q])
        mmat = sb("mmat", [P, 8, BQ, Q])
        dtbx = sb("dtbx", [P, DIRS, NBLK, BQ, C])
        wbx = sb("wbx", [P, DIRS, BH, BQ, C])
        hst = sb("hst", [P, DIRS, BH, C])
        cpfx = sb("cpfx", [P, DIRS, BH, Q])
        yd = sb("yd", [P, DIRS, BH, L])
        yg = sb("yg", [P, DIRS, BH, L])
        ysq = sb("ysq", [P, DIRS, BH, L])
        yln = sb("yln", [P, DIRS, BH, L])
        yrs = sb("yrs", [P, DIRS, BH, L])
        yn = sb("yn", [P, DIRS, BH, L])
        out_w = sb("out_w", [P, DIRS, P])
        mq = sb("mq", [P, P])
        eps = sb("eps", [P, 1])
        ones = sb("ones", [1, P])
        bn_st = sb("bn_st", [P, BH, 6])
        bn_mv = sb("bn_mv", [P, 2])
        bn_m = sb("bn_m", [P, 2])
        bn_v = sb("bn_v", [P, 6])
        osb = sb("osb", [P, BH, L])
        conv4_w = sb("conv4_w", [P, P])
        u4 = sb("u4", [P, BH, L])
        g1 = sb("g1", [P, BH, L])
        g2 = sb("g2", [P, BH, L])
        g3 = sb("g3", [P, BH, L])
        x1 = sb("x1", [P, BH, L])
        c1sq = sb("c1sq", [P, BH, L])
        l1 = sb("l1", [P, BH, L])
        l1r = sb("l1r", [P, BH, L])
        h1 = sb("h1", [P, BH, L])
        qt = sb("qt", [P, BH, L])
        vaug = sb("vaug", [P, NBLK, BQ, C + 1])
        idb = sb("idb", [P, P], BF16)
        caus = sb("caus", [P, 384], BF16)
        nmax = sb("nmax", [P, B, 2])
        prob = mmat[:, :, :, :].rearrange("p g q t -> p (g q t)")[:, 0:B * 384].rearrange("p (b t) -> p b t", b=B)
        probt = cbd[:, :, :, :, :].rearrange("p d k q t -> p (d k q t)")[:, 0:B * 384].rearrange("p (b t) -> p b t", b=B)
        x1t = sb("x1t", [P, NBLK, BQ, C])
        rden = sb("rden", [P, BH, NC * BQ])
        att = sb("att", [P, NBLK, BQ, C])
        t2 = sb("t2", [P, NBLK, BQ, C])
        t2s = sb("t2s", [P, BH, NC * BQ])
        t2m = sb("t2m", [P, BH, NC * BQ])
        t2c = sb("t2c", [P, NBLK, BQ, C])
        t2q = sb("t2q", [P, NBLK, BQ, C])
        t2v = sb("t2v", [P, BH, NC * BQ])
        t2l = sb("t2l", [P, BH, NC * BQ])
        t2r = sb("t2r", [P, BH, NC * BQ])
        h2 = sb("h2", [P, NBLK, BQ, C])
        h2t = sb("h2t", [P, NBLK, Q])
        top1 = sb("top1", [P, BH, NC * BQ])
        is1 = sb("is1", [P, BH, NC * BQ, E])
        rank1 = sb("rank1", [P, BH, NC * BQ, E])
        best1 = sb("best1", [P, BH, NC * BQ])
        pick1 = sb("pick1", [P, BH, NC * BQ, E])
        rest = sb("rest", [P, BH, NC * BQ, E])
        top2 = sb("top2", [P, BH, NC * BQ])
        diff = sb("diff", [P, BH, NC * BQ])
        is2 = sb("is2", [P, BH, NC * BQ, E])
        rank2 = sb("rank2", [P, BH, NC * BQ, E])
        best2 = sb("best2", [P, BH, NC * BQ])
        pick2 = sb("pick2", [P, BH, NC * BQ, E])
        p2 = sb("p2", [P, BH, NC * BQ])
        psum2 = sb("psum2", [P, BH, NC * BQ])
        w1 = sb("w1", [P, BH, NC * BQ])
        w2 = sb("w2", [P, BH, NC * BQ])
        wsec = sb("wsec", [P, BH, NC * BQ, E])
        wfirst = sb("wfirst", [P, BH, NC * BQ, E])
        wtok = sb("wtok", [P, BH, NC * BQ, E])
        wtt = sb("wtt", [NC * BQ * E, BH, P])
        mix = lmat[:, :, :].rearrange("p g c -> p (g c)").rearrange("p (k e q c) -> p k e q c", k=NBLK, q=BQ, e=E)
        fin = sb("fin", [P, N])

        bank = [ctx.enter_context(nc.psum_tensor(f"bank{i}", [P, 512], F32)) for i in range(8)]

        names = (
            "x_in pa_in pb_in pc_in pd_in stored warmed zeroed ones_ready eps_ready lin1_done lin1_copied diag_ready conv_part "
            "taps_done conv_summed silu_done wc_done wc_copied dt_w_ready proj_w_ready fold_w_ready dt_done "
            "proj_done tap3_ready tapped3 centred tapped s1_ready s2_ready cbd_dve cbd_act dt_step dt_exp_done dt_log_done "
            "dt_ready dt_dir_ready neg_a_ready a_ready da_ready da_masked cum_done "
            "pfx_ready pfxb_done cpfx_ready data1_ready dab_done scanned g_done m_ready s1t_done "
            "dtbx_ready wbx_ready h_done h_copied y_done yd_ready yg_ready ysq_ready yms_done "
            "yln_ready yrs_ready yn_ready fold_done out_w_ready mq_ready o_done o_copied "
            "bn_stats_done bn_step bn_avg_done bn_var_ready bn_log bn_rs bn_scale_ready bn_shift_ready "
            "conv4_w_ready shift_done bias_ready conv4_done u4_ready g1_ready g2_ready g3_ready x1_ready "
            "cen_done csq_ready var_done l1_ready l1r_ready h1_ready q_done q_copied v_done v_copied x1t_done "
            "x1t_copied bf_ready s_done nmax_ready prob_ready pt_done pt_copied o_att_done "
            "rden_ready att_ready t2_ready t2s_ready t2m_ready t2c_ready t2q_ready t2v_ready t2l_ready t2r_ready "
            "h2_ready h2t_done h2t_copied router_done top1_ready is1_ready rank1_ready best1_ready pick1_ready rest_ready top2_ready diff_ready is2_ready "
            "rank2_ready best2_ready p2_ready psum2_ready w1_ready w2_ready wfirst_ready pick2_ready wsec_ready "
            "w_ready wt_done wt_copied e_done mix_ready summed last_summed mixed fin_ready".split())
        S = {n: sem(n) for n in names}

        block = ctx.enter_context(nc.Block())

        def blk_of(d, bh, step):
            return NC * bh + (step if d == 0 else NC - 1 - step)

        groups = [(d, bh, step) for d in range(DIRS) for bh in range(BH) for step in range(NC)]
        DT, CUM, HC, PB = 0, 32, 64, 192
        small = bank[7]
        dt_ps = small[:, DT:DT + 32]
        cum_ps = small[:, CUM:CUM + 32].rearrange("p (d g) -> p d g", d=DIRS)
        h_ps = small[:, HC:HC + DIRS * BH * C].rearrange("p (d b c) -> p d b c", d=DIRS, b=BH)
        pb_ps = small[:, PB:PB + BH * Q].rearrange("p (b q) -> p b q", b=BH)
        proj_bank = [bank[2], bank[3], bank[4], bank[5]]
        t_bank = bank[6]
        unit_bank = [bank[5], bank[4]]
        dab_bank = [bank[0], bank[1]]
        g_bank = [bank[2], bank[3]]
        e_bank = [bank[3], bank[4], bank[5], bank[6]]
        wt_bank = [bank[7], bank[1]]
        PE_TAPS = [0, 1, 2, 3]
        DVE_TAPS = [4, 5, 6, 7, 8]
        PROJ_ORDER = [0, 1, 3, 2]
        CBD_DVE, CBD_ACT = [0, 1], [2, 3]

        def blocks(ap):
            return ap.rearrange("p (k q) -> p k q", q=Q)

        def half(ap, bh):
            return ap[:, L * bh:L * bh + L]

        def back(ap):
            n = ap.shape[-1]
            return ap[:, n - 1::-1] if len(ap.shape) == 2 else ap[:, :, n - 1::-1]

        def spread(ap, shape):
            names = "p a b"[:2 * len(ap.shape) - 1]
            parts = names.split()
            return ap.rearrange(f"{' '.join(parts[:-1])} ({parts[-1]} o) -> {' '.join(parts)} o", o=1).to_broadcast(shape)

        @block.sync
        def _(sp):
            sp.dma_start(x4[:, :], x_in).then_inc(S["x_in"], 16)
            sp.dma_start(tiles["pb"][:, :], pb_in).then_inc(S["pb_in"], 16)
            sp.dma_start(tiles["pc"][:, :], pc_in).then_inc(S["pc_in"], 16)
            sp.dma_start(tiles["pd"][:, :], pd_in).then_inc(S["pd_in"], 16)
            for k in range(NBLK):
                sp.wait_ge(S["fin_ready"], k + 1)
                sp.dma_start(out[:, k * Q:(k + 1) * Q], fin[:, k * Q:(k + 1) * Q]).then_inc(S["stored"], 16)
            sp.wait_ge(S["stored"], 16 * NBLK)

        @block.gpsimd
        def _(pool):
            pool.memset(o1p[:, :, :, :], 0.0).then_inc(S["zeroed"], 1)
            pool.memset(o4[:, :, :], 0.0).then_inc(S["zeroed"], 1)
            pool.memset(cbd[:, :, :, :, :], 0.0).then_inc(S["zeroed"], 1)
            pool.memset(vaug[:, :, :, C:C + 1], 1.0).then_inc(S["zeroed"], 1)
            pool.memset(ones[:, :], 1.0).then_inc(S["ones_ready"], 1)
            pool.wait_ge(S["pa_in"], 16)
            pool.wait_ge(S["pb_in"], 16)
            for q in range(BQ):
                pool.tensor_scalar(data1[:, 0, Q * q:Q * q + Q], packs["ident"], 1.0, None, ALU.mult)\
                    .then_inc(S["data1_ready"], 1)
            for q in range(BQ):
                pool.tensor_scalar(data1[:, 1, Q * q:Q * q + Q], packs["rev"], 1.0, None, ALU.mult)\
                    .then_inc(S["data1_ready"], 1)
            for s in range(1, TAPS1):
                pool.wait_ge(S["centred"], 2)
                pool.wait_ge(S["tap3_ready"], s)
                if s > 1:
                    pool.wait_ge(S["tapped3"], s - 1)
                pool.tensor_tensor(pre[:, 3, :, 0:L - s], tap3[:, s - 1, :, s:L], pre[:, 3, :, 0:L - s], ALU.add)\
                    .then_inc(S["tapped3"], 1)
            pool.wait_ge(S["pc_in"], 16)
            pool.tensor_scalar(idb[:, :], packs["ident"], 1.0, None, ALU.mult).then_inc(S["bf_ready"], 1)
            pool.tensor_scalar(caus[:, :], packs["causal"], 1.0, None, ALU.mult).then_inc(S["bf_ready"], 1)

            for k in range(NC):
                pool.wait_ge(S["mix_ready"], BQ)
                pool.tensor_tensor(mix[:, k, 0:E // 2, :, :], mix[:, k, 0:E // 2, :, :], mix[:, k, E // 2:E, :, :], ALU.add)\
                    .then_inc(S["summed"], 1)

        @block.scalar
        def _(act):
            act.dma_start(tiles["pa"][:, :], pa_in).then_inc(S["pa_in"], 16)
            act.preload_act_table(ACT.Silu)
            act.wait_ge(S["zeroed"], 1)
            act.wait_ge(S["pa_in"], 16)
            act.wait_ge(S["lin1_done"], 1)
            act.activation(o1p[:, :, 1:H + 1, 1:W + 1],
                           bank[0][:, :].rearrange("p (b h w) -> p b h w", b=BH, h=H),
                           ACT.Identity, bias=packs["lin1_b"]).then_inc(S["lin1_copied"], 1)
            act.wait_ge(S["wc_done"], 1)
            act.activation(wc[:, :], bank[2][:, 0:130], ACT.Copy).then_inc(S["wc_copied"], 1)
            act.wait_ge(S["zeroed"], 2)
            act.wait_ge(S["conv_summed"], 2)
            act.activation(o4[:, :, PAD:PAD + L], convs[:, :, :], ACT.Silu, bias=packs["dw_b"])\
               .then_inc(S["silu_done"], 1)
            act.preload_act_table_set("natural_log_exp_and_others")
            act.wait_ge(S["pb_in"], 16)
            act.activation(neg_a[:, :], packs["a_log"], ACT.Exp).then_inc(S["neg_a_ready"], 1)

            def centre_tap(n):
                act.wait_ge(S["proj_done"], PROJ_ORDER.index(n) + 1)
                act.activation(pre[:, n, :, :], proj_bank[n][:, :].rearrange("p (b l) -> p b l", b=BH), ACT.Copy,
                               scale=packs["tap_col"][:, TAPS1 * n + PAD:TAPS1 * n + TAPS1])\
                   .then_inc(S["centred"], 1)

            def other_taps(n):
                for s in range(1, TAPS1):
                    col = TAPS1 * n + PAD - s
                    act.activation(tap3[:, s - 1, :, :], proj_bank[n][:, :].rearrange("p (b l) -> p b l", b=BH),
                                   ACT.Copy, scale=packs["tap_col"][:, col:col + 1]).then_inc(S["tap3_ready"], 1)

            act.wait_ge(S["dt_step"], 2)
            act.activation(dt_exp[:, :], dt_neg[:, :], ACT.Exp).then_inc(S["dt_exp_done"], 1)
            act.wait_ge(S["dt_exp_done"], 1)
            act.activation(dt_log[:, :], dt_exp[:, :], ACT.Ln, bias=1.0).then_inc(S["dt_log_done"], 1)
            act.wait_ge(S["a_ready"], 1)
            act.activation(da[:, :], a_tok[:, :], ACT.Exp).then_inc(S["da_ready"], 1)
            centre_tap(0)
            act.wait_ge(S["cum_done"], 2)
            for d in range(DIRS):
                for bh in range(BH):
                    k = blk_of(d, bh, 1)
                    act.activation(pfx[:, d, bh, :, :], spread(cum_ps[:, d, BQ * k:BQ * k + BQ], [P, BQ, C]),
                                   ACT.Exp).then_inc(S["pfx_ready"], 1)
            act.preload_act_table(ACT.Silu)

            def silu(n):
                d, g = n // 2, n % 2
                if n == FOLDED:
                    act.wait_ge(S["proj_done"], PROJ_ORDER.index(n) + 1)
                    src = proj_bank[n][:, :].rearrange("p (b l) -> p b l", b=BH)
                else:
                    if n == 3:
                        act.wait_ge(S["tapped3"], PAD)
                    else:
                        act.wait_ge(S["tapped"], PAD * (n // 2 + 1))
                    src = pre[:, n, :, :]
                act.activation((s1, s2)[g][:, d, :, :], src, ACT.Silu, bias=packs["conv_b"][:, n:n + 1])\
                   .then_inc(S["s2_ready" if g else "s1_ready"], 1)
                if g:
                    act.wait_ge(S["s2_ready"], d + 1)
                    act.wait_ge(S["zeroed"], 3)
                    for q in CBD_ACT:
                        r = slice(C * q, C * q + DI)
                        act.activation(cbd[r, d, :, q, :], blocks(s2[r, d, :, :].rearrange("p b l -> p (b l)")),
                                       ACT.Copy).then_inc(S["cbd_act"], 1)

            def state_copy(d, bh):
                act.wait_ge(S["h_done"], BH * d + bh + 1)
                act.activation(hst[:, d, bh, :], h_ps[:, d, bh, :], ACT.Copy).then_inc(S["h_copied"], 1)

            silu(0)
            silu(1)
            centre_tap(3)
            other_taps(3)
            centre_tap(2)
            state_copy(0, 0)
            silu(3)
            state_copy(0, 1)
            silu(2)
            act.preload_act_table_set("natural_log_exp_and_others")

            def square(u):
                d, bh = u // BH, u % BH
                act.wait_ge(S["yg_ready"], u + 1)
                act.activation(ysq[:, d, bh, :], yg[:, d, bh, :], ACT.Square).then_inc(S["ysq_ready"], 1)

            def rms(u):
                d, bh = u // BH, u % BH
                act.wait_ge(S["yms_done"], u + 1)
                act.activation(yln[:, d, bh, :], half(unit_bank[u % 2], 1), ACT.Ln, bias=eps[:, :]).then_inc(S["yln_ready"], 1)
                act.wait_ge(S["yln_ready"], u + 1)
                act.activation(yrs[:, d, bh, :], yln[:, d, bh, :], ACT.Exp, scale=-0.5).then_inc(S["yrs_ready"], 1)

            act.wait_ge(S["eps_ready"], 1)
            square(0)
            rms(0)
            square(1)
            rms(1)
            state_copy(1, 0)
            state_copy(1, 1)
            square(2)
            rms(2)
            square(3)
            rms(3)
            for bh in range(BH):
                act.wait_ge(S["bn_stats_done"], bh + 1)
                act.activation(osb[:, bh, :], bank[bh][:, 0:L], ACT.Copy).then_inc(S["o_copied"], 1)
            act.wait_ge(S["bn_var_ready"], 1)
            act.activation(bn_v[:, 1:2], bn_v[:, 0:1], ACT.Ln, scale=-1.0, bias=eps[:, :]).then_inc(S["bn_log"], 1)
            act.wait_ge(S["bn_log"], 1)
            act.activation(bn_v[:, 2:3], bn_v[:, 1:2], ACT.Exp, scale=-0.5).then_inc(S["bn_rs"], 1)
            for bh in range(BH):
                act.wait_ge(S["u4_ready"], bh + 1)
                act.activation(g1[:, bh, :], u4[:, bh, :], ACT.Exp, scale=-1.0).then_inc(S["g1_ready"], 1)
            for bh in range(BH):
                act.wait_ge(S["g1_ready"], bh + 1)
                act.activation(g2[:, bh, :], g1[:, bh, :], ACT.Ln, bias=1.0).then_inc(S["g2_ready"], 1)
            for bh in range(BH):
                act.wait_ge(S["g2_ready"], bh + 1)
                act.activation(g3[:, bh, :], g2[:, bh, :], ACT.Exp, scale=-1.0).then_inc(S["g3_ready"], 1)
            for bh in range(BH):
                act.wait_ge(S["cen_done"], bh + 1)
                act.activation(c1sq[:, bh, :], bank[4 + bh][:, 0:L], ACT.Square).then_inc(S["csq_ready"], 1)
            for bh in range(BH):
                act.wait_ge(S["var_done"], bh + 1)
                act.activation(l1[:, bh, :], bank[6 + bh][:, 0:L], ACT.Ln, bias=eps[:, :]).then_inc(S["l1_ready"], 1)
                act.wait_ge(S["l1_ready"], bh + 1)
                act.activation(l1r[:, bh, :], l1[:, bh, :], ACT.Exp, scale=-0.5).then_inc(S["l1r_ready"], 1)
            for bh in range(BH):
                act.wait_ge(S["q_done"], bh + 1)
                act.activation(qt[:, bh, :], bank[bh][:, 0:L], ACT.Copy).then_inc(S["q_copied"], 1)

            def probabilities(b):
                act.wait_ge(S["nmax_ready"], 2 * b + 2)
                sc = bank[3 + b % 3]
                act.activation(prob[:, b, 0:Q], sc[:, 0:Q], ACT.Exp, bias=nmax[:, b, 0:1]).then_inc(S["prob_ready"], 1)
                act.activation(prob[:, b, Q:3 * Q], sc[:, Q:3 * Q], ACT.Exp, bias=nmax[:, b, 1:2])\
                   .then_inc(S["prob_ready"], 1)

            def turned(b):
                act.wait_ge(S["pt_done"], b + 1)
                act.activation(probt[:, b, :], bank[6 + b % 2][:, 0:384], ACT.Copy).then_inc(S["pt_copied"], 1)

            def ln2_square(bh):
                ks = slice(NC * bh, NC * bh + NC)
                act.wait_ge(S["t2c_ready"], bh + 1)
                act.activation(t2q[:, ks, :, :], t2c[:, ks, :, :], ACT.Square).then_inc(S["t2q_ready"], 1)

            def ln2_root(bh):
                act.wait_ge(S["t2v_ready"], bh + 1)
                act.activation(t2l[:, bh, :], t2v[:, bh, :], ACT.Ln, scale=1.0 / C, bias=eps[:, :])\
                   .then_inc(S["t2l_ready"], 1)
                act.wait_ge(S["t2l_ready"], bh + 1)
                act.activation(t2r[:, bh, :], t2l[:, bh, :], ACT.Exp, scale=-0.5).then_inc(S["t2r_ready"], 1)

            def h2_copy(bh):
                ks = slice(NC * bh, NC * bh + NC)
                act.wait_ge(S["h2t_done"], bh + 1)
                act.activation(h2t[:, ks, :], blocks(bank[0][:, :])[:, ks, :], ACT.Copy).then_inc(S["h2t_copied"], 1)

            def second_exp(bh):
                act.wait_ge(S["diff_ready"], bh + 1)
                act.activation(p2[:, bh, :], diff[:, bh, :], ACT.Exp).then_inc(S["p2_ready"], 1)

            def w_copy(bh):
                act.wait_ge(S["wt_done"], bh + 1)
                act.activation(wtt[:, bh, :], wt_bank[bh][0:NC * BQ * E, 0:Q], ACT.Copy)\
                   .then_inc(S["wt_copied"], 1)

            def store_copy(k):
                act.wait_ge(S["mixed"], k + 1)
                act.activation(fin[:, k * Q:(k + 1) * Q], bank[k % 2 * 7][:, 0:Q], ACT.Copy)\
                   .then_inc(S["fin_ready"], 1)

            probabilities(0)
            for b in range(1, B):
                probabilities(b)
                turned(b - 1)
            ln2_square(0)
            turned(B - 1)
            ln2_root(0)
            h2_copy(0)
            ln2_square(1)
            ln2_root(1)
            h2_copy(1)
            second_exp(0)
            w_copy(0)
            second_exp(1)
            store_copy(0)
            store_copy(1)
            w_copy(1)
            store_copy(2)
            store_copy(3)

        @block.tensor
        def _(pe):
            def keep_warm(n, scratch=7):
                for _ in range(n):
                    pe.matmul(bank[scratch][:, :], warm[:, 0:P], warm[:, :], start=True, stop=True)

            pe.wait_ge(S["warmed"], 1)
            keep_warm(8)
            pe.wait_ge(S["pa_in"], 16)
            pe.wait_ge(S["x_in"], 16)
            pe.matmul(bank[0][:, :], packs["lin1"], x4[:, :], start=True, stop=True).then_inc(S["lin1_done"], 1)
            pe.wait_ge(S["pb_in"], 16)
            pe.matmul(bank[2][:, 0:130], packs["fc_in_t"][0:C, :], packs["mam_in"][0:C, :],
                      start=True, stop=True).then_inc(S["wc_done"], 1)
            pe.wait_ge(S["diag_ready"], len(PE_TAPS))
            pe.wait_ge(S["lin1_copied"], 1)
            for i, t in enumerate(PE_TAPS):
                mm = pe.matmul(bank[1][:, :], diag[:, t, :],
                               o1p[:, :, t // 3:t // 3 + H, t % 3:t % 3 + W],
                               start=(i == 0), stop=(i == len(PE_TAPS) - 1))
            mm.then_inc(S["conv_part"], 1)
            pe.wait_ge(S["pc_in"], 16)
            for d in range(DIRS):
                pe.matmul(bank[6][:, P * d:P * d + P], packs["out_t"][0:C, P * d:P * d + P],
                          packs["fc_out"][0:C, :], start=True, stop=True)
            pe.matmul(bank[6][:, 2 * P:3 * P], packs["wq_t"][0:C, :], packs["wk_t"][0:C, :],
                      start=True, stop=True).then_inc(S["fold_done"], 1)
            keep_warm(5)
            pe.wait_ge(S["silu_done"], 1)
            pe.wait_ge(S["dt_w_ready"], 1)
            for bh in range(BH):
                for c in range(NC):
                    k = NC * bh + c
                    mm = pe.matmul(dt_ps[:, 8 * k:8 * k + 8], o4[:, bh, PAD + Q * c:PAD + Q * c + Q],
                                   dt_w[:, :, :], start=True, stop=True)
            mm.then_inc(S["dt_done"], 1)

            def project(n):
                pe.wait_ge(S["proj_w_ready"], 1)
                pe.wait_ge(S["wc_copied"], 1)
                pe.matmul(proj_bank[n][:, :], proj_w[:, n, :, :], o4[:, :, PAD:PAD + L],
                          start=True, stop=True).then_inc(S["proj_done"], 1)

            def project_folded():
                pe.wait_ge(S["fold_w_ready"], 1)
                for k in range(TAPS1):
                    at = k if FOLDED < 2 else 2 * PAD - k
                    mm = pe.matmul(proj_bank[FOLDED][:, :], fold_w[:, k, :, :], o4[:, :, at:at + L],
                                   start=(k == 0), stop=(k == TAPS1 - 1))
                mm.then_inc(S["proj_done"], 1)

            def decay_sums():
                pe.wait_ge(S["a_ready"], 1)
                for d in range(DIRS):
                    pe.matmul(cum_ps[:, d, :], packs["tri"][:, P * d:P * d + P],
                              a_tok[:, :].rearrange("p (k d q) -> p d k q", d=DIRS, q=BQ)[:, d, :, :],
                              start=True, stop=True).then_inc(S["cum_done"], 1)

            def transposed(d):
                pe.wait_ge(S["s1_ready"], d + 1)
                if d == 0:
                    pe.wait_ge(S["out_w_ready"], DIRS)
                    pe.wait_ge(S["mq_ready"], 1)
                else:
                    pe.wait_ge(S["dtbx_ready"], 1)
                    pe.wait_ge(S["wbx_ready"], BH)
                for k in range(NBLK):
                    mm = pe.transpose(t_bank[:, Q * k:Q * k + Q], s1[:, d, k // NC, Q * (k % NC):Q * (k % NC) + Q],
                                      packs["ident"])
                mm.then_inc(S["s1t_done"], 1)

            def decays(i):
                d, bh, step = groups[i]
                k = blk_of(d, bh, step)
                if i < 2:
                    pe.wait_ge(S["da_masked"], 1)
                    pe.wait_ge(S["conv_summed"], 2)
                else:
                    pe.wait_ge(S["scanned"], i - 1)
                for q in range(BQ):
                    col = 8 * k + 4 * d + q
                    mm = pe.transpose(dab_bank[i % 2][:, Q * q:Q * q + Q],
                                      da[:, col:col + 1].to_broadcast([P, P]),
                                      packs["ident"] if d == 0 else packs["rev"])
                mm.then_inc(S["dab_done"], 1)

            def products(i):
                d, bh, step = groups[i]
                k = blk_of(d, bh, step)
                pe.wait_ge(S["s1_ready"], d + 1)
                pe.wait_ge(S["cbd_dve"], len(CBD_DVE) * (d + 1))
                pe.wait_ge(S["cbd_act"], len(CBD_ACT) * (d + 1))
                if i < 2:
                    pe.wait_ge(S["tapped"], PAD)
                    pe.wait_ge(S["s2_ready"], 1)
                else:
                    pe.wait_ge(S["m_ready"], i - 1)
                c = cbd[:, d, k, :, :]
                pe.matmul(g_bank[i % 2][:, :], s1[:, d, bh, Q * (k % NC):Q * (k % NC) + Q],
                          c if d == 0 else back(c), start=True, stop=True).then_inc(S["g_done"], 1)

            def prefix_rows(d):
                pe.wait_ge(S["pfx_ready"], DIRS * BH)
                if d == 1:
                    pe.wait_ge(S["cpfx_ready"], 1)
                    pe.wait_ge(S["h_copied"], BH)
                for bh in range(BH):
                    mm = pe.transpose(pb_ps[:, bh, :], pfx[:, d, bh, :, :].rearrange("p q c -> p (q c)"),
                                      packs["ident"])
                mm.then_inc(S["pfxb_done"], 1)

            def states(d, bh):
                pe.wait_ge(S["dtbx_ready"], d + 1)
                pe.wait_ge(S["wbx_ready"], BH * d + bh + 1)
                pe.wait_ge(S["cpfx_ready"], d + 1)
                if d + bh:
                    pe.wait_ge(S["h_copied"], BH * d + bh)
                k = blk_of(d, bh, 0)
                for q in range(BQ):
                    mm = pe.matmul(h_ps[C * q:C * q + C, d, bh, :], dtbx[:, d, k, q, :], wbx[:, d, bh, q, :],
                                   start=True, stop=True)
                mm.then_inc(S["h_done"], 1)

            def outputs(i):
                d, bh, step = groups[i]
                k = blk_of(d, bh, step)
                if i == 0:
                    pe.wait_ge(S["tap3_ready"], PAD)
                elif i == 2:
                    pe.wait_ge(S["tapped"], PAD * 2)
                elif i > 2 and step == 0:
                    pe.wait_ge(S["yln_ready"], i // 2 - 1)
                pe.wait_ge(S["m_ready"], i + 1)
                pe.wait_ge(S["dtbx_ready"], d + 1)
                if step == 1:
                    pe.wait_ge(S["h_copied"], BH * d + bh + 1)
                    pe.wait_ge(S["cpfx_ready"], d + 1)
                for q in range(BQ):
                    y = unit_bank[i // 2 % 2][C * q:C * q + C, Q * (k % NC):Q * (k % NC) + Q]
                    m = mmat[:, i, q, :]
                    mm = pe.matmul(y, dtbx[:, d, k, q, :], m if d == 0 else back(m), start=True, stop=(step == 0))
                    if step == 1:
                        r = slice(C * q, C * q + DI)
                        mm = pe.matmul(y, hst[r, d, bh, :], cpfx[r, d, bh, :], start=False, stop=True)
                mm.then_inc(S["y_done"], 1)

            def mean_squares(u):
                d, bh = u // BH, u % BH
                pe.wait_ge(S["ysq_ready"], u + 1)
                pe.matmul(half(unit_bank[u % 2], 1), packs["mean16"], ysq[:, d, bh, :], start=True, stop=True)\
                  .then_inc(S["yms_done"], 1)

            project(0)
            decay_sums()
            decays(0)
            decays(1)
            project_folded()
            prefix_rows(0)
            project(3)
            project(2)
            transposed(0)
            products(0)
            products(1)
            decays(2)
            outputs(0)
            states(0, 0)
            products(2)
            outputs(1)
            decays(3)
            states(0, 1)
            products(3)
            outputs(2)
            outputs(3)
            decays(4)
            mean_squares(0)
            transposed(1)
            products(4)
            decays(5)
            prefix_rows(1)
            products(5)
            mean_squares(1)
            outputs(4)
            states(1, 0)
            decays(6)
            products(6)
            outputs(5)
            decays(7)
            products(7)
            states(1, 1)
            outputs(6)
            outputs(7)
            mean_squares(2)

            def mixer_out(d, bh):
                pe.wait_ge(S["scanned"], 7 + bh)
                pe.wait_ge(S["out_w_ready"], 2)
                pe.wait_ge(S["yn_ready"], BH * d + bh + 1)
                mm = pe.matmul(bank[bh][:, 0:L], out_w[:, d, :], yn[:, d, bh, :], start=(d == 0), stop=(d == 1))
                if d == 1:
                    mm.then_inc(S["o_done"], 1)

            mixer_out(0, 0)
            mixer_out(0, 1)
            keep_warm(FILL[0], 6)
            mean_squares(3)
            keep_warm(FILL[1], 6)
            mixer_out(1, 0)
            keep_warm(FILL[2], 6)
            mixer_out(1, 1)
            keep_warm(FILL[3], 6)
            pe.wait_ge(S["bn_step"], 2)
            pe.matmul(bank[7][:, 0:2], packs["bn_avg"], bn_mv[:, :], start=True, stop=True).then_inc(S["bn_avg_done"], 1)
            keep_warm(FILL[4], 6)
            pe.wait_ge(S["bn_shift_ready"], 1)
            pe.matmul(bank[7][:, 2:3], packs["conv4"], bn_v[:, 4:5], start=True, stop=True).then_inc(S["shift_done"], 1)
            pe.wait_ge(S["conv4_w_ready"], 1)
            pe.wait_ge(S["m_ready"], 8)
            for bh in range(BH):
                pe.wait_ge(S["o_copied"], bh + 1)
                pe.matmul(bank[2 + bh][:, 0:L], conv4_w[:, :], osb[:, bh, :], start=True, stop=True)\
                  .then_inc(S["conv4_done"], 1)
            keep_warm(FILL[5], 6)
            for bh in range(BH):
                pe.wait_ge(S["x1_ready"], bh + 1)
                pe.matmul(bank[4 + bh][:, 0:L], packs["centre"], x1[:, bh, :], start=True, stop=True)\
                  .then_inc(S["cen_done"], 1)
            pe.wait_ge(S["u4_ready"], 1)
            for k in range(NBLK):
                mm = pe.transpose(bank[2][:, Q * k:Q * k + Q], x1[:, k // NC, Q * (k % NC):Q * (k % NC) + Q],
                                  packs["ident"])
            mm.then_inc(S["x1t_done"], 1)
            keep_warm(FILL[6], 6)
            pe.wait_ge(S["bias_ready"], 1)
            for bh in range(BH):
                pe.wait_ge(S["csq_ready"], bh + 1)
                pe.matmul(bank[6 + bh][:, 0:L], packs["mean32"], c1sq[:, bh, :], start=True, stop=True)\
                  .then_inc(S["var_done"], 1)

            def query(bh):
                pe.wait_ge(S["h1_ready"], bh + 1)
                pe.matmul(bank[bh][:, 0:L], mq[:, :], h1[:, bh, :], start=True, stop=True).then_inc(S["q_done"], 1)

            def values(bh):
                for c in range(NC):
                    mm = pe.matmul(bank[6 + bh][:, Q * c:Q * c + Q], h1[:, bh, Q * c:Q * c + Q], packs["wv"],
                                   start=True, stop=True)
                mm.then_inc(S["v_done"], 1)

            def scores(b):
                bh, q = b // BQ, b % BQ
                r = slice(C * q, C * q + C)
                sc = bank[3 + b % 3]
                pe.wait_ge(S["q_copied"], bh + 1)
                if b < 3:
                    pe.wait_ge(S["bf_ready"], 2)
                if b == 0:
                    pe.wait_ge(S["u4_ready"], 2)
                if b == 2:
                    pe.wait_ge(S["h1_ready"], 2)
                if b >= 3:
                    pe.wait_ge(S["prob_ready"], 2 * (b - 2))
                pe.matmul(sc[:, 0:384], idb[:, :], caus[:, :], start=True, stop=False)
                pe.matmul(sc[:, 0:Q], qt[r, bh, 0:Q], h1[r, bh, 0:Q], start=False, stop=False)
                pe.matmul(sc[:, Q:3 * Q], qt[r, bh, Q:L], h1[r, bh, :], start=False, stop=True).then_inc(S["s_done"], 1)

            def turn(b):
                pe.wait_ge(S["prob_ready"], 2 * (b + 1))
                if b < 2:
                    pe.wait_ge(S["v_copied"], b + 1)
                else:
                    pe.wait_ge(S["pt_copied"], b - 1)
                for k in range(3):
                    mm = pe.transpose(bank[6 + b % 2][:, Q * k:Q * k + Q], prob[:, b, Q * k:Q * k + Q], packs["ident"])
                mm.then_inc(S["pt_done"], 1)

            def attend(b):
                bh, q = b // BQ, b % BQ
                pe.wait_ge(S["pt_copied"], b + 1)
                pe.wait_ge(S["v_copied"], bh + 1)
                if b == BQ:
                    pe.wait_ge(S["x1t_copied"], 1)
                o = bank[1 + bh][:, 0:NC * BQ * (C + 1)].rearrange("p (c q e) -> p c q e", c=NC, q=BQ)
                v = [vaug[:, NC * bh + c, q, :] for c in range(NC)]
                pe.matmul(o[:, 0, q, :], probt[:, b, 0:Q], v[0], start=True, stop=True)
                pe.matmul(o[:, 1, q, :], probt[:, b, Q:2 * Q], v[0], start=True, stop=False)
                pe.matmul(o[:, 1, q, :], probt[:, b, 2 * Q:3 * Q], v[1], start=False, stop=True)\
                  .then_inc(S["o_att_done"], 1)

            def tokens_turned(bh):
                pe.wait_ge(S["h2_ready"], bh + 1)
                if bh == 1:
                    pe.wait_ge(S["h2t_copied"], 1)
                for k in range(NC * bh, NC * bh + NC):
                    mm = pe.transpose(bank[0][:, Q * k:Q * k + Q], h2[:, k, :, :], packs["ident"])
                mm.then_inc(S["h2t_done"], 1)

            def route_bias(bh):
                pe.wait_ge(S["pd_in"], 16)
                pe.wait_ge(S["ones_ready"], 1)
                pe.wait_ge(S["att_ready"], bh + 1)
                pe.matmul(bank[1 + bh][:, 0:NC * BQ * E], ones[:, :], packs["router_b"][0:1, 0:NC * BQ * E],
                          start=True, stop=False)

            def route(bh):
                pe.wait_ge(S["h2t_copied"], bh + 1)
                for c in range(NC):
                    mm = pe.matmul(bank[1 + bh][:, BQ * E * c:BQ * E * (c + 1)], h2t[:, NC * bh + c, :],
                                   packs["router"], start=False, stop=(c == NC - 1))
                mm.then_inc(S["router_done"], 1)

            def experts(j):
                q, bh = j % BQ, j // BQ
                r = slice(C * q, C * q + C)
                pe.wait_ge(S["h2t_copied"], bh + 1)
                if j == 0:
                    pe.wait_ge(S["pt_copied"], B)
                if j >= 4:
                    pe.wait_ge(S["mix_ready"], j - 3)
                for i in range(2):
                    mm = pe.matmul(e_bank[q][:, 256 * i:256 * i + 256], h2t[r, NC * bh + i, :],
                                   packs["experts"][r, :], start=True, stop=True)
                mm.then_inc(S["e_done"], 1)

            def weights_turned(bh):
                pe.wait_ge(S["w_ready"], bh + 1)
                pe.transpose(wt_bank[bh][0:NC * BQ * E, 0:Q], wtok[:, bh, :, :], packs["ident"])\
                  .then_inc(S["wt_done"], 1)

            def mixed(k):
                bh = k // NC
                o = bank[k % 2 * 7][:, 0:Q]
                pe.wait_ge(S["wt_copied"], bh + 1)
                pe.wait_ge(S["t2_ready"], bh + 1)
                pe.wait_ge(S["h2t_copied"], 2)
                if k >= 2:
                    pe.wait_ge(S["fin_ready"], k - 1)
                r = slice(32 * (k % NC), 32 * (k % NC) + 32)
                pe.matmul(o, packs["experts_b"][r, :], wtt[r, bh, :], start=True, stop=False)
                pe.matmul(o, t2[:, k, :, :], packs["ident"], start=False, stop=False)
                terms = E // 2
                if bh == 0:
                    pe.wait_ge(S["summed"], k + 1)
                elif k == NBLK - 1:
                    pe.wait_ge(S["last_summed"], 1)
                else:
                    pe.wait_ge(S["mix_ready"], 2 * BQ)
                    terms = E
                for e in range(terms):
                    mm = pe.matmul(o, mix[:, k, e, :, :], packs["ident"], start=False, stop=(e == terms - 1))
                mm.then_inc(S["mixed"], 1)

            keep_warm(FILL[7], 3)
            query(0)
            values(0)
            query(1)
            scores(0)
            values(1)
            for b in range(1, B + 3):
                if b < B:
                    scores(b)
                if 2 <= b < B + 2:
                    turn(b - 2)
                if b >= 3:
                    attend(b - 3)
            keep_warm(FILL[8])
            route_bias(0)
            tokens_turned(0)
            keep_warm(FILL[9])
            route(0)
            route_bias(1)
            experts(0)
            experts(1)
            keep_warm(FILL[10])
            tokens_turned(1)
            experts(2)
            route(1)
            experts(3)
            weights_turned(0)
            keep_warm(FILL[11], 0)
            for j in range(BQ, 2 * BQ):
                experts(j)
                if j < 2 * BQ - 1:
                    keep_warm(FILL[12], 0)
            mixed(0)
            mixed(1)
            weights_turned(1)
            mixed(2)
            mixed(3)

        @block.vector
        def _(dve):
            dve.memset(warm[:, :], 0.0).then_inc(S["warmed"], 1)
            dve.memset(eps[:, :], EPS).then_inc(S["eps_ready"], 1)
            dve.wait_ge(S["pa_in"], 16)
            for t in PE_TAPS:
                dve.tensor_scalar(diag[:, t, :], packs["ident"], packs["dw"][:, t:t + 1], None, ALU.mult)\
                   .then_inc(S["diag_ready"], 1)
            dve.wait_ge(S["lin1_copied"], 1)
            steps = 0
            for i, t in enumerate(DVE_TAPS):
                for bh in range(BH):
                    win = o1p[:, bh, t // 3:t // 3 + H, t % 3:t % 3 + W]
                    to = conv[:, i % 2, bh, :].rearrange("p (h w) -> p h w", h=H)
                    if i == 0:
                        dve.tensor_scalar(to, win, packs["dw"][:, t:t + 1], None, ALU.mult)\
                           .then_inc(S["taps_done"], 1)
                    else:
                        dve.wait_ge(S["taps_done"], steps - 1)
                        dve.scalar_tensor_tensor(to, win, packs["dw"][:, t:t + 1],
                                                 conv[:, (i + 1) % 2, bh, :].rearrange("p (h w) -> p h w", h=H),
                                                 ALU.mult, ALU.add).then_inc(S["taps_done"], 1)
                    steps += 1
            dve.wait_ge(S["conv_part"], 1)
            dve.wait_ge(S["taps_done"], steps)
            for bh in range(BH):
                dve.tensor_tensor(convs[:, bh, :], half(bank[1], bh),
                                  conv[:, (len(DVE_TAPS) + 1) % 2, bh, :], ALU.add).then_inc(S["conv_summed"], 1)
            dve.wait_ge(S["pb_in"], 16)
            dve.wait_ge(S["wc_copied"], 1)
            mask_q = packs["mask4"].rearrange("p (o q) -> p o q", o=1)
            dve.tensor_tensor(dt_w[:, :, :], spread(wc[:, 128:130], [P, DIRS, BQ]),
                              mask_q.to_broadcast([P, DIRS, BQ]), ALU.mult).then_inc(S["dt_w_ready"], 1)
            dve.tensor_tensor(proj_w[:, :, :, :],
                              wc[:, 0:128].rearrange("p (n o c) -> p n o c", n=4, o=1).to_broadcast([P, 4, BQ, C]),
                              packs["mask4"].rearrange("p (n q c) -> p n q c", n=1, c=1).to_broadcast([P, 4, BQ, C]),
                              ALU.mult).then_inc(S["proj_w_ready"], 1)
            dve.wait_ge(S["fold_done"], 1)
            dve.wait_ge(S["pc_in"], 16)
            for d in range(DIRS):
                dve.scalar_tensor_tensor(out_w[:, d, :], bank[6][:, P * d:P * d + P], packs["norm_w"][:, d:d + 1],
                                         packs["mask"], ALU.mult, ALU.mult).then_inc(S["out_w_ready"], 1)
            dve.scalar_tensor_tensor(mq[:, :], bank[6][:, 2 * P:3 * P], float(C) ** -0.5, packs["mask"],
                                     ALU.mult, ALU.mult).then_inc(S["mq_ready"], 1)
            dve.wait_ge(S["dt_done"], 1)
            dve.tensor_tensor(dt_raw[:, :], dt_ps, packs["dt_bias"], ALU.add).then_inc(S["dt_step"], 1)
            dve.wait_ge(S["dt_step"], 1)
            dve.scalar_tensor_tensor(dt_neg[:, :], dt_raw[:, :], -1.0, dt_raw[:, :], ALU.mult, ALU.min).then_inc(S["dt_step"], 1)
            dve.wait_ge(S["proj_w_ready"], 1)
            dve.tensor_tensor(fold_w[:, :, :, :],
                              proj_w[:, FOLDED:FOLDED + 1, :, :].to_broadcast([P, TAPS1, BQ, C]),
                              packs["taps"].rearrange("p (k o c) -> p k o c", o=1, c=C).to_broadcast([P, TAPS1, BQ, C]),
                              ALU.mult).then_inc(S["fold_w_ready"], 1)
            dve.wait_ge(S["dt_log_done"], 1)
            dve.scalar_tensor_tensor(dt[:, :], dt_raw[:, :], 0.0, dt_log[:, :], ALU.max, ALU.add)\
               .then_inc(S["dt_ready"], 1)
            dve.wait_ge(S["dt_ready"], 1)
            dve.wait_ge(S["neg_a_ready"], 1)
            dve.scalar_tensor_tensor(a_tok[:, :], dt[:, :], -1.0, neg_a[:, :], ALU.mult, ALU.mult)\
               .then_inc(S["a_ready"], 1)
            dve.tensor_copy(dt_dir[:, :, :].rearrange("p d (k q) -> p k d q", q=BQ),
                            dt[:, :].rearrange("p (k d q) -> p k d q", d=DIRS, q=BQ)).then_inc(S["dt_dir_ready"], 1)
            dve.wait_ge(S["da_ready"], 1)
            dve.tensor_tensor(da[:, :], da[:, :], packs["keep_da"], ALU.mult).then_inc(S["da_masked"], 1)

            def tap(n, s):
                if s == 1:
                    dve.wait_ge(S["centred"], 1 if n == 0 else 3)
                else:
                    dve.wait_ge(S["tapped"], PAD * (n // 2) + s - 1)
                src = proj_bank[n][:, :].rearrange("p (b l) -> p b l", b=BH)
                to, of = (slice(s, L), slice(0, L - s)) if n < 2 else (slice(0, L - s), slice(s, L))
                col = TAPS1 * n + PAD - s
                dve.scalar_tensor_tensor(pre[:, n, :, to], src[:, :, of], packs["tap_col"][:, col:col + 1],
                                         pre[:, n, :, to], ALU.mult, ALU.add).then_inc(S["tapped"], 1)

            def own_rows(d):
                dve.wait_ge(S["s2_ready"], d + 1)
                dve.wait_ge(S["zeroed"], 3)
                for q in CBD_DVE:
                    r = slice(C * q, C * q + DI)
                    dve.tensor_copy(cbd[r, d, :, q, :], blocks(s2[r, d, :, :].rearrange("p b l -> p (b l)")))\
                       .then_inc(S["cbd_dve"], 1)

            def scan(i):
                d = groups[i][0]
                dve.wait_ge(S["dab_done"], i + 1)
                if i == 0 or i == 4:
                    dve.wait_ge(S["data1_ready"], BQ * (d + 1))
                dve.tensor_tensor_scan(lmat[:, i, :], dab_bank[i % 2][:, :], data1[:, d, :], 0.0,
                                       ALU.mult, ALU.add).then_inc(S["scanned"], 1)

            def times(i):
                dve.wait_ge(S["g_done"], i + 1)
                dve.wait_ge(S["scanned"], i + 1)
                dve.tensor_tensor(mmat[:, i, :, :], g_bank[i % 2][:, :].rearrange("p (q t) -> p q t", q=BQ),
                                  lmat[:, i, :].rearrange("p (q t) -> p q t", q=BQ), ALU.mult)\
                   .then_inc(S["m_ready"], 1)

            def weigh(d):
                dve.wait_ge(S["s1t_done"], d + 1)
                dve.wait_ge(S["dt_dir_ready"], 1)
                dve.tensor_tensor(dtbx[:, d, :, :, :].rearrange("p k q c -> p (k q) c"),
                                  t_bank[:, :].rearrange("p (k c) -> p k c", c=C),
                                  spread(dt_dir[:, d, :], [P, NBLK * BQ, C]), ALU.mult).then_inc(S["dtbx_ready"], 1)

            def keep(d, bh):
                i = groups.index((d, bh, 0))
                k = blk_of(d, bh, 0)
                dve.wait_ge(S["scanned"], i + 1)
                dve.wait_ge(S["s1t_done"], d + 1)
                dve.tensor_tensor(wbx[:, d, bh, :, :],
                                  t_bank[:, Q * k:Q * k + Q].rearrange("p (q c) -> p q c", c=C),
                                  spread(lmat[:, i, Q - 1::Q], [P, BQ, C]), ALU.mult).then_inc(S["wbx_ready"], 1)

            def prefix(d):
                dve.wait_ge(S["pfxb_done"], d + 1)
                c1 = 1 if d == 0 else 0
                dve.wait_ge(S["s2_ready"], d + 1)
                dve.tensor_tensor(cpfx[:, d, :, :], pb_ps,
                                  s2[:, d, :, Q * c1:Q * c1 + Q], ALU.mult).then_inc(S["cpfx_ready"], 1)

            def gated(u):
                d, bh = u // BH, u % BH
                dve.wait_ge(S["y_done"], 2 * (u + 1))
                dve.scalar_tensor_tensor(yd[:, d, bh, :], s1[:, d, bh, :], packs["skip_d"][:, d:d + 1],
                                         half(unit_bank[u % 2], 0), ALU.mult, ALU.add).then_inc(S["yd_ready"], 1)
                dve.wait_ge(S["yd_ready"], u + 1)
                dve.tensor_tensor(yg[:, d, bh, :], yd[:, d, bh, :], s2[:, d, bh, :], ALU.mult)\
                   .then_inc(S["yg_ready"], 1)

            def normed(u):
                d, bh = u // BH, u % BH
                dve.wait_ge(S["yrs_ready"], u + 1)
                dve.tensor_tensor(yn[:, d, bh, :], yg[:, d, bh, :], yrs[:, d, bh, :], ALU.mult)\
                   .then_inc(S["yn_ready"], 1)

            for s in range(1, TAPS1):
                tap(0, s)
            scan(0)
            scan(1)
            weigh(0)
            own_rows(0)
            keep(0, 0)
            times(0)
            prefix(0)
            times(1)
            tap(2, 1)
            scan(2)
            tap(2, 2)
            keep(0, 1)
            times(2)
            tap(2, 3)
            scan(3)
            times(3)
            gated(0)
            own_rows(1)
            scan(4)
            weigh(1)
            keep(1, 0)
            gated(1)
            times(4)
            scan(5)
            prefix(1)
            times(5)
            scan(6)
            keep(1, 1)
            times(6)
            scan(7)
            times(7)
            gated(2)
            normed(0)
            normed(1)
            gated(3)
            normed(2)
            normed(3)
            for bh in range(BH):
                dve.wait_ge(S["o_done"], bh + 1)
                dve.bn_stats(bn_st[:, bh, :], bank[bh][:, 0:L]).then_inc(S["bn_stats_done"], 1)
            dve.wait_ge(S["bn_stats_done"], 2)
            dve.bn_aggr(bn_mv[:, :], bn_st[:, :, :].rearrange("p b s -> p (b s)")).then_inc(S["bn_step"], 1)
            dve.wait_ge(S["bn_step"], 1)
            dve.scalar_tensor_tensor(bn_mv[:, 1:2], bn_mv[:, 0:1], bn_mv[:, 0:1], bn_mv[:, 1:2], ALU.mult, ALU.add)\
               .then_inc(S["bn_step"], 1)
            dve.wait_ge(S["bn_avg_done"], 1)
            dve.tensor_copy(bn_m[:, :], bank[7][:, 0:2]).then_inc(S["bn_step"], 1)
            dve.wait_ge(S["bn_step"], 3)
            dve.scalar_tensor_tensor(bn_v[:, 0:1], bn_m[:, 0:1], bn_m[:, 0:1], bn_m[:, 1:2], ALU.mult, ALU.subtract)\
               .then_inc(S["bn_var_ready"], 1)
            dve.wait_ge(S["bn_rs"], 1)
            dve.tensor_tensor(bn_v[:, 3:4], packs["bn_g"], bn_v[:, 2:3], ALU.mult).then_inc(S["bn_scale_ready"], 1)
            dve.wait_ge(S["bn_scale_ready"], 1)
            dve.scalar_tensor_tensor(bn_v[:, 4:5], bn_m[:, 0:1], bn_v[:, 3:4], packs["bn_b"], ALU.mult, ALU.subtract)\
               .then_inc(S["bn_shift_ready"], 1)
            dve.tensor_scalar(conv4_w[:, :], packs["conv4"], bn_v[:, 3:4], None, ALU.mult).then_inc(S["conv4_w_ready"], 1)
            dve.wait_ge(S["shift_done"], 1)
            dve.tensor_tensor(bn_v[:, 5:6], packs["conv4_b"], bank[7][:, 2:3], ALU.subtract).then_inc(S["bias_ready"], 1)
            dve.wait_ge(S["bias_ready"], 1)
            for bh in range(BH):
                dve.wait_ge(S["conv4_done"], bh + 1)
                dve.tensor_scalar(u4[:, bh, :], bank[2 + bh][:, 0:L], bn_v[:, 5:6], SIG_CLAMP, ALU.add, ALU.max)\
                   .then_inc(S["u4_ready"], 1)
            for bh in range(BH):
                dve.wait_ge(S["g3_ready"], bh + 1)
                dve.scalar_tensor_tensor(x1[:, bh, :], g3[:, bh, :], 1.0, half(x4[:, :], bh), ALU.add, ALU.mult)\
                   .then_inc(S["x1_ready"], 1)
            dve.wait_ge(S["x1t_done"], 1)
            dve.tensor_copy(x1t[:, :, :, :].rearrange("p k q c -> p (k q c)"), bank[2][:, :]).then_inc(S["x1t_copied"], 1)
            for bh in range(BH):
                dve.wait_ge(S["l1r_ready"], bh + 1)
                dve.tensor_tensor(h1[:, bh, :], bank[4 + bh][:, 0:L], l1r[:, bh, :], ALU.mult).then_inc(S["h1_ready"], 1)

            def value_copy(bh):
                dve.wait_ge(S["v_done"], bh + 1)
                dve.wait_ge(S["zeroed"], 4)
                dve.tensor_copy(vaug[:, NC * bh:NC * bh + NC, :, 0:C].rearrange("p k q c -> p (k q) c"),
                                bank[6 + bh][:, 0:L].rearrange("p (k c) -> p k c", c=C)).then_inc(S["v_copied"], 1)

            def row_max(b):
                dve.wait_ge(S["s_done"], b + 1)
                sc = bank[3 + b % 3]
                dve.tensor_reduce(nmax[:, b, 0:1], sc[:, 0:Q], AX_X, ALU.max, negate=True).then_inc(S["nmax_ready"], 1)
                dve.tensor_reduce(nmax[:, b, 1:2], sc[:, Q:3 * Q], AX_X, ALU.max, negate=True)\
                   .then_inc(S["nmax_ready"], 1)

            units = lambda t, bh: t[:, NC * bh:NC * bh + NC, :, :].rearrange("p k q c -> p (k q) c")

            def residual(bh):
                dve.wait_ge(S["o_att_done"], BQ * (bh + 1))
                o = bank[1 + bh][:, 0:NC * BQ * (C + 1)].rearrange("p (k e) -> p k e", e=C + 1)
                dve.reciprocal(rden[:, bh, :], o[:, :, C:C + 1].rearrange("p k o -> p (k o)"))\
                   .then_inc(S["rden_ready"], 1)
                dve.wait_ge(S["rden_ready"], bh + 1)
                dve.tensor_tensor(units(att, bh), o[:, :, 0:C], spread(rden[:, bh, :], [P, NC * BQ, C]), ALU.mult)\
                   .then_inc(S["att_ready"], 1)
                dve.wait_ge(S["att_ready"], bh + 1)
                dve.wait_ge(S["x1t_copied"], 1)
                dve.tensor_tensor(units(t2, bh), units(att, bh), units(x1t, bh), ALU.add).then_inc(S["t2_ready"], 1)

            def ln2_centre(bh):
                dve.wait_ge(S["t2_ready"], bh + 1)
                dve.tensor_reduce(t2s[:, bh, :], units(t2, bh), AX_X, ALU.add).then_inc(S["t2s_ready"], 1)
                dve.wait_ge(S["t2s_ready"], bh + 1)
                dve.tensor_scalar(t2m[:, bh, :], t2s[:, bh, :], 1.0 / C, None, ALU.mult).then_inc(S["t2m_ready"], 1)
                dve.wait_ge(S["t2m_ready"], bh + 1)
                dve.tensor_tensor(units(t2c, bh), units(t2, bh), spread(t2m[:, bh, :], [P, NC * BQ, C]), ALU.subtract)\
                   .then_inc(S["t2c_ready"], 1)

            def ln2_var(bh):
                dve.wait_ge(S["t2q_ready"], bh + 1)
                dve.tensor_reduce(t2v[:, bh, :], units(t2q, bh), AX_X, ALU.add).then_inc(S["t2v_ready"], 1)

            def ln2_scale(bh):
                dve.wait_ge(S["t2r_ready"], bh + 1)
                dve.tensor_tensor(units(h2, bh), units(t2c, bh), spread(t2r[:, bh, :], [P, NC * BQ, C]), ALU.mult)\
                   .then_inc(S["h2_ready"], 1)

            rank = packs["rank"][:, 0:NC * BQ * E].rearrange("p (k e) -> p k e", e=E)
            over = lambda t, bh: spread(t[:, bh, :], [P, NC * BQ, E])
            logits = [bank[1 + bh][:, 0:NC * BQ * E].rearrange("p (k e) -> p k e", e=E) for bh in range(BH)]

            def find_top1(bh):
                dve.wait_ge(S["router_done"], bh + 1)
                dve.tensor_reduce(top1[:, bh, :], logits[bh], AX_X, ALU.max).then_inc(S["top1_ready"], 1)

            def find_is1(bh):
                dve.wait_ge(S["top1_ready"], bh + 1)
                dve.tensor_tensor(is1[:, bh, :, :], logits[bh], over(top1, bh), ALU.is_equal)\
                   .then_inc(S["is1_ready"], 1)

            def find_rank1(bh):
                dve.wait_ge(S["is1_ready"], bh + 1)
                dve.tensor_tensor(rank1[:, bh, :, :], is1[:, bh, :, :], rank, ALU.mult).then_inc(S["rank1_ready"], 1)

            def find_best1(bh):
                dve.wait_ge(S["rank1_ready"], bh + 1)
                dve.tensor_reduce(best1[:, bh, :], rank1[:, bh, :, :], AX_X, ALU.max).then_inc(S["best1_ready"], 1)

            def find_pick1(bh):
                dve.wait_ge(S["best1_ready"], bh + 1)
                dve.tensor_tensor(pick1[:, bh, :, :], rank1[:, bh, :, :], over(best1, bh), ALU.is_equal)\
                   .then_inc(S["pick1_ready"], 1)

            def find_rest(bh):
                dve.wait_ge(S["pick1_ready"], bh + 1)
                dve.scalar_tensor_tensor(rest[:, bh, :, :], pick1[:, bh, :, :], MASKED, logits[bh],
                                         ALU.mult, ALU.add).then_inc(S["rest_ready"], 1)

            def find_top2(bh):
                dve.wait_ge(S["rest_ready"], bh + 1)
                dve.tensor_reduce(top2[:, bh, :], rest[:, bh, :, :], AX_X, ALU.max).then_inc(S["top2_ready"], 1)

            def find_is2(bh):
                dve.wait_ge(S["top2_ready"], bh + 1)
                dve.tensor_tensor(diff[:, bh, :], top2[:, bh, :], top1[:, bh, :], ALU.subtract).then_inc(S["diff_ready"], 1)
                dve.tensor_tensor(is2[:, bh, :, :], rest[:, bh, :, :], over(top2, bh), ALU.is_equal)\
                   .then_inc(S["is2_ready"], 1)

            def find_rank2(bh):
                dve.wait_ge(S["is2_ready"], bh + 1)
                dve.tensor_tensor(rank2[:, bh, :, :], is2[:, bh, :, :], rank, ALU.mult).then_inc(S["rank2_ready"], 1)

            def find_best2(bh):
                dve.wait_ge(S["rank2_ready"], bh + 1)
                dve.tensor_reduce(best2[:, bh, :], rank2[:, bh, :, :], AX_X, ALU.max).then_inc(S["best2_ready"], 1)

            def find_psum2(bh):
                dve.wait_ge(S["p2_ready"], bh + 1)
                dve.tensor_scalar(psum2[:, bh, :], p2[:, bh, :], 1.0, None, ALU.add).then_inc(S["psum2_ready"], 1)

            def find_w1(bh):
                dve.wait_ge(S["psum2_ready"], bh + 1)
                dve.reciprocal(w1[:, bh, :], psum2[:, bh, :]).then_inc(S["w1_ready"], 1)

            def find_w2(bh):
                dve.wait_ge(S["w1_ready"], bh + 1)
                dve.tensor_tensor(w2[:, bh, :], w1[:, bh, :], p2[:, bh, :], ALU.mult).then_inc(S["w2_ready"], 1)
                dve.tensor_tensor(wfirst[:, bh, :, :], pick1[:, bh, :, :], over(w1, bh), ALU.mult)\
                   .then_inc(S["wfirst_ready"], 1)

            def find_pick2(bh):
                dve.wait_ge(S["best2_ready"], bh + 1)
                dve.tensor_tensor(pick2[:, bh, :, :], rank2[:, bh, :, :], over(best2, bh), ALU.is_equal)\
                   .then_inc(S["pick2_ready"], 1)

            def find_second(bh):
                dve.wait_ge(S["pick2_ready"], bh + 1)
                dve.wait_ge(S["w2_ready"], bh + 1)
                dve.tensor_tensor(wsec[:, bh, :, :], pick2[:, bh, :, :], over(w2, bh), ALU.mult).then_inc(S["wsec_ready"], 1)

            def find_weights(bh):
                dve.wait_ge(S["wsec_ready"], bh + 1)
                dve.wait_ge(S["wfirst_ready"], bh + 1)
                dve.tensor_tensor(wtok[:, bh, :, :], wsec[:, bh, :, :], wfirst[:, bh, :, :], ALU.add).then_inc(S["w_ready"], 1)

            def weighted(q, blks):
                bh = blks[0] // NC
                c0, n = blks[0] % NC, len(blks)
                dve.wait_ge(S["e_done"], BQ * bh + q + 1)
                dve.wait_ge(S["w_ready"], bh + 1)
                w4 = wtok[:, bh, :, :].rearrange("p (k q) e -> p k q e", q=BQ)
                dve.tensor_tensor(mix[:, blks[0]:blks[0] + n, :, q, :],
                                  e_bank[q][:, :].rearrange("p (k e c) -> p k e c", k=NC, e=E)[:, c0:c0 + n, :, :],
                                  w4[:, c0:c0 + n, q, :].rearrange("p k (e o) -> p k e o", o=1).to_broadcast([P, n, E, C]),
                                  ALU.mult).then_inc(S["mix_ready"], 1)

            value_copy(0)
            row_max(0)
            value_copy(1)
            for b in range(1, B - 1):
                row_max(b)
            residual(0)
            row_max(B - 1)
            ln2_centre(0)
            ln2_var(0)
            ln2_scale(0)
            residual(1)
            ln2_centre(1)
            find_top1(0)
            ln2_var(1)
            find_is1(0)
            find_rank1(0)
            find_best1(0)
            ln2_scale(1)
            find_pick1(0)
            find_rest(0)
            find_top2(0)
            find_is2(0)
            find_rank2(0)
            find_best2(0)
            find_psum2(0)
            find_pick2(0)
            find_w1(0)
            find_w2(0)
            find_second(0)
            find_weights(0)
            weighted(0, [0, 1])
            find_top1(1)
            find_is1(1)
            weighted(1, [0, 1])
            find_rank1(1)
            find_best1(1)
            weighted(2, [0, 1])
            find_pick1(1)
            find_rest(1)
            weighted(3, [0, 1])
            find_top2(1)
            find_is2(1)
            find_rank2(1)
            find_best2(1)
            find_psum2(1)
            find_pick2(1)
            find_w1(1)
            find_w2(1)
            find_second(1)
            find_weights(1)
            for k in (2, 3):
                for q in range(BQ):
                    weighted(q, [k])
            dve.wait_ge(S["mix_ready"], 3 * BQ)
            dve.tensor_tensor(mix[:, 3, 0:E // 2, :, :], mix[:, 3, 0:E // 2, :, :], mix[:, 3, E // 2:E, :, :], ALU.add)\
               .then_inc(S["last_summed"], 1)


def pack_inputs(inp):
    import numpy as np

    f = np.float32
    g = {k: np.asarray(v) for k, v in inp.items()}
    get = lambda n: g["L0_conv_" + n]
    rows = np.arange(P)
    img, ch = rows // C, rows % C

    def rep(a):
        return np.tile(a.reshape(C, -1), (BQ, 1))

    def bd(a):
        n = a.shape[1]
        o = np.zeros((P, BQ * n), f)
        for q in range(BQ):
            o[C * q:C * q + C, n * q:n * q + n] = a
        return o

    def top(a):
        o = np.zeros((P, a.shape[1]), f)
        o[:C] = a
        return o

    def upper(cols):
        o = np.zeros((P, DIRS), f)
        for d in range(DIRS):
            for q in range(BQ):
                o[C * q + DI:C * q + C, d] = cols[d]
        return o

    v = {}
    v["lin1"] = bd(get("lin1_w"))
    v["ident"] = np.eye(P, dtype=f)
    v["rev"] = np.eye(P, dtype=f)[::-1]
    v["lin1_b"], v["dw_b"], v["dw"] = rep(get("lin1_b")), rep(get("dw_b")), rep(get("dw_w").reshape(C, 9))
    v["fc_in_t"] = top(np.tile(get("fc_in_w").T, (1, BQ)))
    win = get("mam_in_w")
    z, xs, bm, cm, dt = (win[:, :, a:b] for a, b in ((0, 16), (16, 32), (32, 48), (48, 64), (64, 65)))
    v["mam_in"] = top(np.concatenate(
        [np.concatenate([bm[d], xs[d], cm[d], z[d]], 1) for d in range(DIRS)] + [dt[0], dt[1]], 1))
    cw, cb = get("mam_conv_w"), get("mam_conv_b")
    taps = np.zeros((DIRS, 2, TAPS1, C), f)
    conv_b = np.zeros((BQ, C, 4), f)
    for d in range(DIRS):
        taps[d, 0] = np.concatenate([cw[d, 16:32], cw[d, 0:16]]).T
        taps[d, 1, :, :DI] = cw[d, 32:48].T
        taps[d, 1, TAPS1 - 1, DI:] = 1.0
        conv_b[:, :, 2 * d] = np.concatenate([cb[d, 16:32], cb[d, 0:16]])
        conv_b[:, :DI, 2 * d + 1] = cb[d, 32:48]
    v["taps"] = np.tile(taps[FOLDED // 2, FOLDED % 2].reshape(1, -1), (P, 1))
    v["tap_col"] = np.tile(taps.transpose(3, 0, 1, 2).reshape(C, 16), (BQ, 1))
    v["conv_b"] = conv_b.reshape(P, 4)
    v["mask4"] = (img[:, None] == np.arange(BQ)[None]).astype(f)
    per_unit = lambda a: np.tile(np.broadcast_to(a.reshape(1, DIRS, 1), (NBLK, DIRS, BQ)).reshape(1, -1), (P, 1))
    v["dt_bias"], v["a_log"] = per_unit(get("mam_dt_bias")), per_unit(get("mam_A_log"))
    keep = np.ones((P, NBLK, DIRS, BQ), f)
    keep[0, :, 0] = 0.0
    keep[P - 1, :, 1] = 0.0
    v["keep_da"] = keep.reshape(P, 32)
    v["skip_d"] = upper([np.full(DI, get("mam_D")[d, 0], f) for d in range(DIRS)])
    r, t = rows[:, None], rows[None]
    v["tri"] = np.concatenate([(r <= t), (r >= t)], 1).astype(f)
    wo = get("mam_out_w")
    v["out_t"] = np.zeros((P, 2 * P), f)
    for d in range(DIRS):
        for q in range(BQ):
            v["out_t"][:C, P * d + C * q + DI:P * d + C * q + C] = wo[d].T
    v["fc_out"] = top(np.tile(get("fc_out_w"), (1, BQ)))
    v["norm_w"] = upper(list(get("mam_norm_w")))
    same = img[:, None] == img[None]
    v["mask"] = same.astype(f)
    v["mean16"] = (same & (ch[:, None] >= DI)).astype(f) / f(DI)
    v["bn_avg"] = (ch[:, None] == ch[None]).astype(f) / f(BQ)
    v["bn_g"], v["bn_b"], v["conv4_b"] = rep(get("bn_g")), rep(get("bn_b")), rep(get("conv4_b"))
    v["conv4"] = bd(get("conv4_w"))
    v["mean32"] = same.astype(f) / f(C)
    v["centre"] = np.eye(P, dtype=f) - v["mean32"]
    v["wq_t"] = top(np.tile(g["L1_attn_W_Q"].T, (1, BQ)))
    v["wk_t"] = top(np.tile(g["L1_attn_W_K"].T, (1, BQ)))
    v["wv"] = bd(g["L1_attn_W_V"])
    tri = np.where(t > r, f(MASKED), f(0.0)).astype(f)
    v["causal"] = np.concatenate([tri, np.zeros((P, P), f), tri], 1)
    v["router"] = bd(g["L1_ffn_router_w"])
    v["router_b"] = np.tile(g["L1_ffn_router_b"].reshape(1, E), (P, 16))
    v["experts"] = np.tile(g["L1_ffn_expert_w"].transpose(1, 0, 2).reshape(C, E * C), (BQ, 1))
    eb = np.zeros((BQ, E, BQ, C), f)
    for q in range(BQ):
        eb[q, :, q] = g["L1_ffn_expert_b"]
    v["experts_b"] = np.tile(eb.reshape(BQ * E, P), (BQ, 1))
    v["rank"] = np.tile((E - np.arange(E, dtype=f)).reshape(1, E), (P, 16))

    arrays = {"x4": np.ascontiguousarray(
        g["x"].reshape(BH, BQ, C, L).transpose(1, 2, 0, 3).reshape(P, N))}
    for pack, parts in PACKS.items():
        for name, width in parts:
            assert v[name].shape == (P, width), (name, v[name].shape)
        arrays[pack] = np.ascontiguousarray(np.concatenate([v[name] for name, _ in parts], 1).astype(f, copy=False))
    return arrays


def kernel(**inputs):
    import numpy as np
    import concourse.bacc as _bacc
    from concourse import mybir as _mybir
    from concourse.bass_utils import run_bass_kernel_spmd as _run

    arrays = pack_inputs(inputs)
    nc = _bacc.Bacc("TRN2", target_bir_lowering=False, num_devices=1)
    args = [nc.dram_tensor(f"in_{n}", a.shape, _mybir.dt.float32, kind="ExternalInput").ap()
            for n, a in arrays.items()]
    out = nc.dram_tensor("out_0", (P, N), _mybir.dt.float32, kind="ExternalOutput").ap()
    program(nc, *args, out)
    r = _run(nc, [{f"in_{n}": a for n, a in arrays.items()}], core_ids=[0])
    o = r.results[0]["out_0"]
    return np.ascontiguousarray(o.reshape(BQ, C, BH, H, W).transpose(2, 0, 1, 3, 4).reshape(B, C, H, W))
```

```python
from contextlib import ExitStack

import concourse.bass as bass
from concourse import mybir

F32 = mybir.dt.float32
BF16 = mybir.dt.bfloat16
ALU = mybir.AluOpType
ACT = mybir.ActivationFunctionType
AX_X = mybir.AxisListType.X

P = 128
B, C, H, W = 8, 32, 16, 16
L = H * W
BQ = P // C
BH = B // BQ
Q = 128
NC = L // Q
NBLK = BH * NC
N = BH * L
DIRS = 2
DI = 16
TAPS1 = 4
FOLDED = 1
PAD = TAPS1 - 1
HP, WP = H + 2, W + 2
E = 8
EPS = 1e-5
MASKED = -1.0e30

PACKS = {
    "pa": [("lin1", 128), ("ident", 128), ("lin1_b", 1), ("dw", 9), ("dw_b", 1)],
    "pb": [("fc_in_t", 128), ("mam_in", 130), ("taps", TAPS1 * C), ("tap_col", 16), ("mask4", 4), ("conv_b", 4),
           ("dt_bias", 32), ("a_log", 32), ("keep_da", 32), ("skip_d", 2), ("rev", 128),
           ("tri", 256)],
    "pc": [("out_t", 256), ("fc_out", 128), ("norm_w", 2), ("mask", 128), ("mean16", 128),
           ("bn_avg", 128), ("bn_g", 1), ("bn_b", 1), ("conv4", 128), ("conv4_b", 1),
           ("centre", 128), ("mean32", 128), ("wq_t", 128), ("wk_t", 128), ("wv", 128),
           ("causal", 384)],
    "pd": [("router", 32), ("router_b", 128), ("experts", 256), ("experts_b", 128), ("rank", 128)],
}


def columns(pack):
    at, out = 0, {}
    for name, width in PACKS[pack]:
        out[name] = (at, at + width)
        at += width
    return out, at


def program(nc, x_in, pa_in, pb_in, pc_in, pd_in, out):
    ctx = ExitStack()
    with ctx:
        def sb(name, shape, dt=F32):
            return ctx.enter_context(nc.sbuf_tensor(name, shape, dt))

        def sem(name):
            return ctx.enter_context(nc.semaphore(name))

        packs = {}
        tiles = {}
        for pack in PACKS:
            where, width = columns(pack)
            tiles[pack] = sb(pack, [P, width])
            for name, (a, b) in where.items():
                packs[name] = tiles[pack][:, a:b]

        x4 = sb("x4", [P, N])
        warm = sb("warm", [P, 512], BF16)
        o1p = sb("o1p", [P, BH, HP, WP])
        diag = sb("diag", [P, 9, P])
        conv = sb("conv", [P, 2, BH, L])
        convs = sb("convs", [P, BH, L])
        o4 = sb("o4", [P, BH, L + 2 * PAD])
        wc = sb("wc", [P, 130])
        proj_w = sb("proj_w", [P, 4, BQ, C])
        fold_w = sb("fold_w", [P, TAPS1, BQ, C])
        dt_w = sb("dt_w", [P, DIRS, BQ])
        pre = sb("pre", [P, 4, BH, L])
        tap3 = sb("tap3", [P, PAD, BH, L])
        s1 = sb("s1", [P, DIRS, BH, L])
        s2 = sb("s2", [P, DIRS, BH, L])
        cbd = sb("cbd", [P, DIRS, NBLK, BQ, Q])
        dt_raw = sb("dt_raw", [P, 32])
        dt_neg = sb("dt_neg", [P, 32])
        dt_exp = sb("dt_exp", [P, 32])
        dt_log = sb("dt_log", [P, 32])
        dt = sb("dt", [P, 32])
        dt_dir = sb("dt_dir", [P, DIRS, NBLK * BQ])
        neg_a = sb("neg_a", [P, 32])
        a_tok = sb("a_tok", [P, 32])
        da = sb("da", [P, 32])
        pfx = sb("pfx", [P, DIRS, BH, BQ, C])
        data1 = sb("data1", [P, DIRS, BQ * Q])
        lmat = sb("lmat", [P, 8, BQ * Q])
        mmat = sb("mmat", [P, 8, BQ, Q])
        dtbx = sb("dtbx", [P, DIRS, NBLK, BQ, C])
        wbx = sb("wbx", [P, DIRS, BH, BQ, C])
        hst = sb("hst", [P, DIRS, BH, C])
        cpfx = sb("cpfx", [P, DIRS, BH, Q])
        yd = sb("yd", [P, DIRS, BH, L])
        yg = sb("yg", [P, DIRS, BH, L])
        ysq = sb("ysq", [P, DIRS, BH, L])
        yln = sb("yln", [P, DIRS, BH, L])
        yrs = sb("yrs", [P, DIRS, BH, L])
        yn = sb("yn", [P, DIRS, BH, L])
        out_w = sb("out_w", [P, DIRS, P])
        mq = sb("mq", [P, P])
        eps = sb("eps", [P, 1])
        ones = sb("ones", [1, P])
        bn_st = sb("bn_st", [P, BH, 6])
        bn_mv = sb("bn_mv", [P, 2])
        bn_m = sb("bn_m", [P, 2])
        bn_v = sb("bn_v", [P, 6])
        osb = sb("osb", [P, BH, L])
        conv4_w = sb("conv4_w", [P, P])
        b_half = sb("b_half", [P, 1])
        x_half = sb("x_half", [P, N])
        gate = sb("gate", [P, BH, L])
        x1 = sb("x1", [P, BH, L])
        cen = sb("cen", [P, BH, L])
        c1sq = sb("c1sq", [P, BH, L])
        l1 = sb("l1", [P, BH, L])
        l1r = sb("l1r", [P, BH, L])
        h1 = sb("h1", [P, BH, L])
        qt = sb("qt", [P, BH, L])
        val = sb("val", [P, NBLK, BQ, C])
        idb = sb("idb", [P, P], BF16)
        caus = sb("caus", [P, 384], BF16)
        nmax = sb("nmax", [P, B, 2])
        prob = mmat[:, :, :, :].rearrange("p g q t -> p (g q t)")[:, 0:B * 384].rearrange("p (b t) -> p b t", b=B)
        probt = cbd[:, :, :, :, :].rearrange("p d k q t -> p (d k q t)")[:, 0:B * 384].rearrange("p (b t) -> p b t", b=B)
        den = sb("den", [P, B, NC])
        rden = sb("rden", [P, B, NC])
        t2 = sb("t2", [P, BH, L])
        cen2 = sb("cen2", [P, BH, L])
        c2sq = sb("c2sq", [P, BH, L])
        l2 = sb("l2", [P, BH, L])
        l2r = sb("l2r", [P, BH, L])
        h2 = sb("h2", [P, BH, L])
        top1 = sb("top1", [P, BH, NC * BQ])
        is1 = sb("is1", [P, BH, NC * BQ, E])
        rank1 = sb("rank1", [P, BH, NC * BQ, E])
        best1 = sb("best1", [P, BH, NC * BQ])
        pick1 = sb("pick1", [P, BH, NC * BQ, E])
        rest = sb("rest", [P, BH, NC * BQ, E])
        top2 = sb("top2", [P, BH, NC * BQ])
        diff = sb("diff", [P, BH, NC * BQ])
        is2 = sb("is2", [P, BH, NC * BQ, E])
        rank2 = sb("rank2", [P, BH, NC * BQ, E])
        best2 = sb("best2", [P, BH, NC * BQ])
        pick2 = sb("pick2", [P, BH, NC * BQ, E])
        p2 = sb("p2", [P, BH, NC * BQ])
        psum2 = sb("psum2", [P, BH, NC * BQ])
        w1 = sb("w1", [P, BH, NC * BQ])
        w2 = sb("w2", [P, BH, NC * BQ])
        wsec = sb("wsec", [P, BH, NC * BQ, E])
        wfirst = sb("wfirst", [P, BH, NC * BQ, E])
        wtok = sb("wtok", [P, BH, NC * BQ, E])
        wtt = sb("wtt", [NC * BQ * E, BH, P])
        mix = lmat[:, :, :].rearrange("p g c -> p (g c)").rearrange("p (k e q c) -> p k e q c", k=NBLK, q=BQ, e=E)
        fin = sb("fin", [P, N])

        bank = [ctx.enter_context(nc.psum_tensor(f"bank{i}", [P, 512], F32)) for i in range(8)]

        names = (
            "x_in pa_in pb_in pc_in pd_in stored warmed zeroed ones_ready eps_ready lin1_done lin1_copied "
            "diag_ready conv_part taps_done conv_summed silu_done wc_done wc_copied dt_w_ready proj_w_ready "
            "fold_w_ready dt_done proj_done tap3_ready tapped3 centred tapped s1_ready s2_ready cbd_dve "
            "cbd_act dt_step dt_exp_done dt_log_done dt_ready dt_dir_ready neg_a_ready a_ready da_ready "
            "da_masked cum_done pfx_ready pfxb_done cpfx_ready data1_ready dab_done scanned g_done m_ready "
            "s1t_done dtbx_ready wbx_ready h_done h_copied y_done yd_ready yg_ready ysq_ready yms_done "
            "yln_ready yrs_ready yn_ready fold_done out_w_ready mq_ready o_done o_copied bn_stats_done "
            "bn_step bn_avg_done bn_var_ready bn_log bn_rs bn_scale_ready bn_shift_ready conv4_w_ready "
            "shift_done bias_ready conv4_done halved gate_ready x1_ready cen_done cen_ready csq_ready "
            "var_done l1_ready l1r_ready h1_ready q_done q_ready v_done v_copied bf_ready s_done nmax_ready "
            "prob_ready pt_done pt_copied o_att_done rden_ready normed_prob t2_ready cen2_done cen2_ready "
            "c2sq_ready var2_done l2_ready l2r_ready h2_ready router_done top1_ready is1_ready rank1_ready "
            "best1_ready pick1_ready rest_ready top2_ready diff_ready is2_ready rank2_ready best2_ready "
            "p2_ready psum2_ready w1_ready w2_ready wfirst_ready pick2_ready wsec_ready w_ready wt_done "
            "wt_copied e_done mix_ready summed last_summed mixed fin_ready".split())
        S = {n: sem(n) for n in names}

        block = ctx.enter_context(nc.Block())

        def blk_of(d, bh, step):
            return NC * bh + (step if d == 0 else NC - 1 - step)

        groups = [(d, bh, step) for d in range(DIRS) for bh in range(BH) for step in range(NC)]
        DT, CUM, HC, PB = 0, 32, 64, 192
        small = bank[7]
        dt_ps = small[:, DT:DT + 32]
        cum_ps = small[:, CUM:CUM + 32].rearrange("p (d g) -> p d g", d=DIRS)
        h_ps = small[:, HC:HC + DIRS * BH * C].rearrange("p (d b c) -> p d b c", d=DIRS, b=BH)
        pb_ps = small[:, PB:PB + BH * Q].rearrange("p (b q) -> p b q", b=BH)
        proj_bank = [bank[2], bank[3], bank[4], bank[5]]
        t_bank = bank[6]
        unit_bank = [bank[5], bank[4]]
        dab_bank = [bank[0], bank[1]]
        g_bank = [bank[2], bank[3]]
        e_bank = [bank[3], bank[4], bank[5], bank[6]]
        lin1_bank = [bank[0], bank[3]]
        conv_bank = [bank[1], bank[4]]
        wt_bank = [bank[7], bank[1]]
        PE_TAPS = [0, 1, 2, 3]
        DVE_TAPS = [4, 5, 6, 7, 8]
        PROJ_ORDER = [0, 2, 1, 3]
        CBD_DVE, CBD_ACT = [0, 1], [2, 3]

        def blocks(ap):
            return ap.rearrange("p (k q) -> p k q", q=Q)

        def half(ap, bh):
            return ap[:, L * bh:L * bh + L]

        def back(ap):
            n = ap.shape[-1]
            return ap[:, n - 1::-1] if len(ap.shape) == 2 else ap[:, :, n - 1::-1]

        def spread(ap, shape):
            names = "p a b"[:2 * len(ap.shape) - 1]
            parts = names.split()
            return ap.rearrange(f"{' '.join(parts[:-1])} ({parts[-1]} o) -> {' '.join(parts)} o", o=1).to_broadcast(shape)

        @block.sync
        def _(sp):
            sp.dma_start(x4[:, :], x_in).then_inc(S["x_in"], 16)
            sp.dma_start(tiles["pb"][:, :], pb_in).then_inc(S["pb_in"], 16)
            sp.dma_start(tiles["pc"][:, :], pc_in).then_inc(S["pc_in"], 16)
            sp.dma_start(tiles["pd"][:, :], pd_in).then_inc(S["pd_in"], 16)
            for k in range(NBLK):
                sp.wait_ge(S["fin_ready"], k + 1)
                sp.dma_start(out[:, k * Q:(k + 1) * Q], fin[:, k * Q:(k + 1) * Q]).then_inc(S["stored"], 16)
            sp.wait_ge(S["stored"], 16 * NBLK)

        @block.gpsimd
        def _(pool):
            pool.memset(o1p[:, :, :, :], 0.0).then_inc(S["zeroed"], 1)
            pool.memset(o4[:, :, :], 0.0).then_inc(S["zeroed"], 1)
            pool.memset(cbd[:, :, :, :, :], 0.0).then_inc(S["zeroed"], 1)
            pool.memset(ones[:, :], 1.0).then_inc(S["ones_ready"], 1)
            pool.wait_ge(S["pa_in"], 16)
            pool.wait_ge(S["pb_in"], 16)
            for q in range(BQ):
                pool.tensor_scalar(data1[:, 0, Q * q:Q * q + Q], packs["ident"], 1.0, None, ALU.mult)\
                    .then_inc(S["data1_ready"], 1)
            for q in range(BQ):
                pool.tensor_scalar(data1[:, 1, Q * q:Q * q + Q], packs["rev"], 1.0, None, ALU.mult)\
                    .then_inc(S["data1_ready"], 1)
            for s in range(1, TAPS1):
                pool.wait_ge(S["centred"], 3)
                pool.wait_ge(S["tap3_ready"], s)
                if s > 1:
                    pool.wait_ge(S["tapped3"], s - 1)
                pool.tensor_tensor(pre[:, 3, :, 0:L - s], tap3[:, s - 1, :, s:L], pre[:, 3, :, 0:L - s], ALU.add)\
                    .then_inc(S["tapped3"], 1)
            pool.wait_ge(S["pc_in"], 16)
            pool.tensor_scalar(idb[:, :], packs["ident"], 1.0, None, ALU.mult).then_inc(S["bf_ready"], 1)
            pool.tensor_scalar(caus[:, :], packs["causal"], 1.0, None, ALU.mult).then_inc(S["bf_ready"], 1)

            pool.wait_ge(S["x_in"], 16)
            pool.tensor_scalar(b_half[:, :], packs["conv4_b"], 0.5, None, ALU.mult).then_inc(S["halved"], 1)
            pool.tensor_scalar(x_half[:, :], x4[:, :], 0.5, None, ALU.mult).then_inc(S["halved"], 1)
            for k in range(NC):
                pool.wait_ge(S["mix_ready"], BQ)
                pool.tensor_tensor(mix[:, k, 0:E // 2, :, :], mix[:, k, 0:E // 2, :, :], mix[:, k, E // 2:E, :, :], ALU.add)\
                    .then_inc(S["summed"], 1)

        @block.scalar
        def _(act):
            act.dma_start(tiles["pa"][:, :], pa_in).then_inc(S["pa_in"], 16)
            act.preload_act_table(ACT.Silu)
            act.wait_ge(S["zeroed"], 1)
            act.wait_ge(S["pa_in"], 16)
            for bh in range(BH):
                act.wait_ge(S["lin1_done"], bh + 1)
                act.activation(o1p[:, bh, 1:H + 1, 1:W + 1],
                               lin1_bank[bh][:, 0:L].rearrange("p (h w) -> p h w", h=H),
                               ACT.Identity, bias=packs["lin1_b"]).then_inc(S["lin1_copied"], 1)
            act.wait_ge(S["wc_done"], 1)
            act.activation(wc[:, :], bank[2][:, 0:130], ACT.Copy).then_inc(S["wc_copied"], 1)
            act.wait_ge(S["zeroed"], 2)
            for bh in range(BH):
                act.wait_ge(S["conv_summed"], bh + 1)
                act.activation(o4[:, bh, PAD:PAD + L], convs[:, bh, :], ACT.Silu, bias=packs["dw_b"])\
                   .then_inc(S["silu_done"], 1)
            act.preload_act_table_set("natural_log_exp_and_others")
            act.wait_ge(S["pb_in"], 16)
            act.activation(neg_a[:, :], packs["a_log"], ACT.Exp).then_inc(S["neg_a_ready"], 1)

            def centre_tap(n):
                act.wait_ge(S["proj_done"], PROJ_ORDER.index(n) + 1)
                act.activation(pre[:, n, :, :], proj_bank[n][:, :].rearrange("p (b l) -> p b l", b=BH), ACT.Copy,
                               scale=packs["tap_col"][:, TAPS1 * n + PAD:TAPS1 * n + TAPS1])\
                   .then_inc(S["centred"], 1)

            def other_taps(n):
                for s in range(1, TAPS1):
                    col = TAPS1 * n + PAD - s
                    act.activation(tap3[:, s - 1, :, :], proj_bank[n][:, :].rearrange("p (b l) -> p b l", b=BH),
                                   ACT.Copy, scale=packs["tap_col"][:, col:col + 1]).then_inc(S["tap3_ready"], 1)

            act.wait_ge(S["dt_step"], 2)
            act.activation(dt_exp[:, :], dt_neg[:, :], ACT.Exp).then_inc(S["dt_exp_done"], 1)
            act.wait_ge(S["dt_exp_done"], 1)
            act.activation(dt_log[:, :], dt_exp[:, :], ACT.Ln, bias=1.0).then_inc(S["dt_log_done"], 1)
            act.wait_ge(S["a_ready"], 1)
            act.activation(da[:, :], a_tok[:, :], ACT.Exp).then_inc(S["da_ready"], 1)
            centre_tap(0)
            centre_tap(2)
            act.wait_ge(S["cum_done"], 2)
            for d in range(DIRS):
                for bh in range(BH):
                    k = blk_of(d, bh, 1)
                    act.activation(pfx[:, d, bh, :, :], spread(cum_ps[:, d, BQ * k:BQ * k + BQ], [P, BQ, C]),
                                   ACT.Exp).then_inc(S["pfx_ready"], 1)
            act.preload_act_table(ACT.Silu)

            def silu(n):
                d, g = n // 2, n % 2
                if n == FOLDED:
                    act.wait_ge(S["proj_done"], PROJ_ORDER.index(n) + 1)
                    src = proj_bank[n][:, :].rearrange("p (b l) -> p b l", b=BH)
                else:
                    if n == 3:
                        act.wait_ge(S["tapped3"], PAD)
                    else:
                        act.wait_ge(S["tapped"], PAD * (n // 2 + 1))
                    src = pre[:, n, :, :]
                act.activation((s1, s2)[g][:, d, :, :], src, ACT.Silu, bias=packs["conv_b"][:, n:n + 1])\
                   .then_inc(S["s2_ready" if g else "s1_ready"], 1)
                if g:
                    act.wait_ge(S["s2_ready"], d + 1)
                    act.wait_ge(S["zeroed"], 3)
                    for q in CBD_ACT:
                        r = slice(C * q, C * q + DI)
                        act.activation(cbd[r, d, :, q, :], blocks(s2[r, d, :, :].rearrange("p b l -> p (b l)")),
                                       ACT.Copy).then_inc(S["cbd_act"], 1)

            def state_copy(d, bh):
                act.wait_ge(S["h_done"], BH * d + bh + 1)
                act.activation(hst[:, d, bh, :], h_ps[:, d, bh, :], ACT.Copy).then_inc(S["h_copied"], 1)

            silu(0)
            silu(1)
            centre_tap(3)
            other_taps(3)
            silu(2)
            state_copy(0, 0)
            state_copy(0, 1)
            silu(3)
            act.preload_act_table_set("natural_log_exp_and_others")

            def square(u):
                d, bh = u // BH, u % BH
                act.wait_ge(S["yg_ready"], u + 1)
                act.activation(ysq[:, d, bh, :], yg[:, d, bh, :], ACT.Square).then_inc(S["ysq_ready"], 1)

            def rms(u):
                d, bh = u // BH, u % BH
                act.wait_ge(S["yms_done"], u + 1)
                act.activation(yln[:, d, bh, :], half(unit_bank[u % 2], 1), ACT.Ln, bias=eps[:, :]).then_inc(S["yln_ready"], 1)
                act.wait_ge(S["yln_ready"], u + 1)
                act.activation(yrs[:, d, bh, :], yln[:, d, bh, :], ACT.Exp, scale=-0.5).then_inc(S["yrs_ready"], 1)

            act.wait_ge(S["eps_ready"], 1)
            square(0)
            rms(0)
            square(1)
            rms(1)
            state_copy(1, 0)
            state_copy(1, 1)
            square(2)
            rms(2)
            square(3)
            rms(3)
            for bh in range(BH):
                act.wait_ge(S["bn_stats_done"], bh + 1)
                act.activation(osb[:, bh, :], bank[bh][:, 0:L], ACT.Copy).then_inc(S["o_copied"], 1)
            act.wait_ge(S["bn_var_ready"], 1)
            act.activation(bn_v[:, 1:2], bn_v[:, 0:1], ACT.Ln, scale=-1.0, bias=eps[:, :]).then_inc(S["bn_log"], 1)
            act.wait_ge(S["bn_log"], 1)
            act.activation(bn_v[:, 2:3], bn_v[:, 1:2], ACT.Exp, scale=-0.5).then_inc(S["bn_rs"], 1)
            act.preload_act_table(ACT.Tanh)
            act.wait_ge(S["bias_ready"], 1)
            for bh in range(BH):
                act.wait_ge(S["conv4_done"], bh + 1)
                act.activation(gate[:, bh, :], bank[2 + bh][:, 0:L], ACT.Tanh, bias=bn_v[:, 5:6], scale=0.5)\
                   .then_inc(S["gate_ready"], 1)
            act.preload_act_table_set("natural_log_exp_and_others")
            for bh in range(BH):
                act.wait_ge(S["cen_done"], bh + 1)
                act.activation(c1sq[:, bh, :], bank[4 + bh][:, 0:L], ACT.Square).then_inc(S["csq_ready"], 1)
            for bh in range(BH):
                act.wait_ge(S["var_done"], bh + 1)
                act.activation(l1[:, bh, :], bank[6 + bh][:, 0:L], ACT.Ln, bias=eps[:, :]).then_inc(S["l1_ready"], 1)
                act.wait_ge(S["l1_ready"], bh + 1)
                act.activation(l1r[:, bh, :], l1[:, bh, :], ACT.Exp, scale=-0.5).then_inc(S["l1r_ready"], 1)

            def probabilities(b):
                act.wait_ge(S["nmax_ready"], 2 * b + 2)
                sc = bank[3 + b % 3]
                act.activation(prob[:, b, 0:Q], sc[:, 0:Q], ACT.Exp, bias=nmax[:, b, 0:1],
                               accum_out=den[:, b, 0:1]).then_inc(S["prob_ready"], 1)
                act.activation(prob[:, b, Q:3 * Q], sc[:, Q:3 * Q], ACT.Exp, bias=nmax[:, b, 1:2],
                               accum_out=den[:, b, 1:2])\
                   .then_inc(S["prob_ready"], 1)

            def turned(b):
                act.wait_ge(S["pt_done"], b + 1)
                act.activation(probt[:, b, :], bank[6 + b % 2][:, 0:384], ACT.Copy).then_inc(S["pt_copied"], 1)

            def ln2_square(bh):
                act.wait_ge(S["cen2_done"], bh + 1)
                act.activation(c2sq[:, bh, :], bank[0][:, 0:L], ACT.Square).then_inc(S["c2sq_ready"], 1)

            def ln2_root(bh):
                act.wait_ge(S["var2_done"], bh + 1)
                act.activation(l2[:, bh, :], bank[1 + bh][:, 0:L], ACT.Ln, bias=eps[:, :]).then_inc(S["l2_ready"], 1)
                act.wait_ge(S["l2_ready"], bh + 1)
                act.activation(l2r[:, bh, :], l2[:, bh, :], ACT.Exp, scale=-0.5).then_inc(S["l2r_ready"], 1)

            def second_exp(bh):
                act.wait_ge(S["diff_ready"], bh + 1)
                act.activation(p2[:, bh, :], diff[:, bh, :], ACT.Exp).then_inc(S["p2_ready"], 1)

            def w_copy(bh):
                act.wait_ge(S["wt_done"], bh + 1)
                act.activation(wtt[:, bh, :], wt_bank[bh][0:NC * BQ * E, 0:Q], ACT.Copy)\
                   .then_inc(S["wt_copied"], 1)

            def store_copy(k):
                act.wait_ge(S["mixed"], k + 1)
                act.activation(fin[:, k * Q:(k + 1) * Q], bank[k % 2 * 7][:, 0:Q], ACT.Copy)\
                   .then_inc(S["fin_ready"], 1)

            probabilities(0)
            probabilities(1)
            for b in range(2, B):
                probabilities(b)
                turned(b - 2)
            ln2_square(0)
            turned(6)
            turned(7)
            ln2_root(0)
            ln2_square(1)
            ln2_root(1)
            second_exp(0)
            w_copy(0)
            second_exp(1)
            store_copy(0)
            store_copy(1)
            w_copy(1)
            store_copy(2)
            store_copy(3)

        @block.tensor
        def _(pe):
            def keep_warm(n, scratch=7):
                for _ in range(n):
                    pe.matmul(bank[scratch][:, :], warm[:, 0:P], warm[:, :], start=True, stop=True)

            pe.wait_ge(S["warmed"], 1)
            keep_warm(8, 7)
            pe.wait_ge(S["pa_in"], 16)
            pe.wait_ge(S["x_in"], 16)
            for bh in range(BH):
                pe.matmul(lin1_bank[bh][:, 0:L], packs["lin1"], half(x4[:, :], bh), start=True, stop=True)\
                  .then_inc(S["lin1_done"], 1)
            pe.wait_ge(S["pb_in"], 16)
            pe.matmul(bank[2][:, 0:130], packs["fc_in_t"][0:C, :], packs["mam_in"][0:C, :],
                      start=True, stop=True).then_inc(S["wc_done"], 1)
            pe.wait_ge(S["diag_ready"], len(PE_TAPS))
            for bh in range(BH):
                pe.wait_ge(S["lin1_copied"], bh + 1)
                for i, t in enumerate(PE_TAPS):
                    mm = pe.matmul(conv_bank[bh][:, 0:L], diag[:, t, :],
                                   o1p[:, bh, t // 3:t // 3 + H, t % 3:t % 3 + W],
                                   start=(i == 0), stop=(i == len(PE_TAPS) - 1))
                mm.then_inc(S["conv_part"], 1)
            pe.wait_ge(S["pc_in"], 16)
            for d in range(DIRS):
                pe.matmul(bank[6][:, P * d:P * d + P], packs["out_t"][0:C, P * d:P * d + P],
                          packs["fc_out"][0:C, :], start=True, stop=True)
            pe.matmul(bank[6][:, 2 * P:3 * P], packs["wq_t"][0:C, :], packs["wk_t"][0:C, :],
                      start=True, stop=True).then_inc(S["fold_done"], 1)
            keep_warm(5, 7)
            pe.wait_ge(S["dt_w_ready"], 1)
            for bh in range(BH):
                pe.wait_ge(S["silu_done"], bh + 1)
                for c in range(NC):
                    k = NC * bh + c
                    mm = pe.matmul(dt_ps[:, 8 * k:8 * k + 8], o4[:, bh, PAD + Q * c:PAD + Q * c + Q],
                                   dt_w[:, :, :], start=True, stop=True)
            mm.then_inc(S["dt_done"], 1)

            def project(n):
                pe.wait_ge(S["proj_w_ready"], 1)
                pe.wait_ge(S["wc_copied"], 1)
                pe.matmul(proj_bank[n][:, :], proj_w[:, n, :, :], o4[:, :, PAD:PAD + L],
                          start=True, stop=True).then_inc(S["proj_done"], 1)

            def project_folded():
                pe.wait_ge(S["fold_w_ready"], 1)
                for k in range(TAPS1):
                    at = k if FOLDED < 2 else 2 * PAD - k
                    mm = pe.matmul(proj_bank[FOLDED][:, :], fold_w[:, k, :, :], o4[:, :, at:at + L],
                                   start=(k == 0), stop=(k == TAPS1 - 1))
                mm.then_inc(S["proj_done"], 1)

            def decay_sums():
                pe.wait_ge(S["a_ready"], 1)
                for d in range(DIRS):
                    pe.matmul(cum_ps[:, d, :], packs["tri"][:, P * d:P * d + P],
                              a_tok[:, :].rearrange("p (k d q) -> p d k q", d=DIRS, q=BQ)[:, d, :, :],
                              start=True, stop=True).then_inc(S["cum_done"], 1)

            def transposed(d):
                pe.wait_ge(S["s1_ready"], d + 1)
                if d == 0:
                    pe.wait_ge(S["out_w_ready"], DIRS)
                    pe.wait_ge(S["mq_ready"], 1)
                else:
                    pe.wait_ge(S["dtbx_ready"], 1)
                    pe.wait_ge(S["wbx_ready"], BH)
                for k in range(NBLK):
                    mm = pe.transpose(t_bank[:, Q * k:Q * k + Q], s1[:, d, k // NC, Q * (k % NC):Q * (k % NC) + Q],
                                      packs["ident"])
                mm.then_inc(S["s1t_done"], 1)

            def decays(i):
                d, bh, step = groups[i]
                k = blk_of(d, bh, step)
                if i < 2:
                    pe.wait_ge(S["da_masked"], 1)
                    pe.wait_ge(S["conv_summed"], 2)
                else:
                    pe.wait_ge(S["scanned"], i - 1)
                for q in range(BQ):
                    col = 8 * k + 4 * d + q
                    mm = pe.transpose(dab_bank[i % 2][:, Q * q:Q * q + Q],
                                      da[:, col:col + 1].to_broadcast([P, P]),
                                      packs["ident"] if d == 0 else packs["rev"])
                mm.then_inc(S["dab_done"], 1)

            def products(i):
                d, bh, step = groups[i]
                k = blk_of(d, bh, step)
                pe.wait_ge(S["s1_ready"], d + 1)
                pe.wait_ge(S["cbd_dve"], len(CBD_DVE) * (d + 1))
                pe.wait_ge(S["cbd_act"], len(CBD_ACT) * (d + 1))
                if i < 2:
                    pe.wait_ge(S["tapped"], PAD)
                    pe.wait_ge(S["s2_ready"], 1)
                else:
                    pe.wait_ge(S["m_ready"], i - 1)
                c = cbd[:, d, k, :, :]
                pe.matmul(g_bank[i % 2][:, :], s1[:, d, bh, Q * (k % NC):Q * (k % NC) + Q],
                          c if d == 0 else back(c), start=True, stop=True).then_inc(S["g_done"], 1)

            def prefix_rows(d):
                pe.wait_ge(S["pfx_ready"], DIRS * BH)
                if d == 1:
                    pe.wait_ge(S["cpfx_ready"], 1)
                    pe.wait_ge(S["h_copied"], BH)
                for bh in range(BH):
                    mm = pe.transpose(pb_ps[:, bh, :], pfx[:, d, bh, :, :].rearrange("p q c -> p (q c)"),
                                      packs["ident"])
                mm.then_inc(S["pfxb_done"], 1)

            def states(d, bh):
                pe.wait_ge(S["dtbx_ready"], d + 1)
                pe.wait_ge(S["wbx_ready"], BH * d + bh + 1)
                pe.wait_ge(S["cpfx_ready"], d + 1)
                if d + bh:
                    pe.wait_ge(S["h_copied"], BH * d + bh)
                k = blk_of(d, bh, 0)
                for q in range(BQ):
                    mm = pe.matmul(h_ps[C * q:C * q + C, d, bh, :], dtbx[:, d, k, q, :], wbx[:, d, bh, q, :],
                                   start=True, stop=True)
                mm.then_inc(S["h_done"], 1)

            def outputs(i):
                d, bh, step = groups[i]
                k = blk_of(d, bh, step)
                if i == 0:
                    pe.wait_ge(S["tap3_ready"], PAD)
                elif i == 2:
                    pe.wait_ge(S["tapped"], PAD * 2)
                elif i > 2 and step == 0:
                    pe.wait_ge(S["yln_ready"], i // 2 - 1)
                pe.wait_ge(S["m_ready"], i + 1)
                pe.wait_ge(S["dtbx_ready"], d + 1)
                if step == 1:
                    pe.wait_ge(S["h_copied"], BH * d + bh + 1)
                    pe.wait_ge(S["cpfx_ready"], d + 1)
                for q in range(BQ):
                    y = unit_bank[i // 2 % 2][C * q:C * q + C, Q * (k % NC):Q * (k % NC) + Q]
                    m = mmat[:, i, q, :]
                    mm = pe.matmul(y, dtbx[:, d, k, q, :], m if d == 0 else back(m), start=True, stop=(step == 0))
                    if step == 1:
                        r = slice(C * q, C * q + DI)
                        mm = pe.matmul(y, hst[r, d, bh, :], cpfx[r, d, bh, :], start=False, stop=True)
                mm.then_inc(S["y_done"], 1)

            def mean_squares(u):
                d, bh = u // BH, u % BH
                pe.wait_ge(S["ysq_ready"], u + 1)
                pe.matmul(half(unit_bank[u % 2], 1), packs["mean16"], ysq[:, d, bh, :], start=True, stop=True)\
                  .then_inc(S["yms_done"], 1)

            project(0)
            project(2)
            decay_sums()
            decays(0)
            decays(1)
            project_folded()
            prefix_rows(0)
            project(3)
            products(0)
            transposed(0)
            products(1)
            decays(2)
            outputs(0)
            states(0, 0)
            products(2)
            outputs(1)
            decays(3)
            states(0, 1)
            products(3)
            outputs(2)
            decays(4)
            outputs(3)
            transposed(1)
            products(4)
            mean_squares(0)
            decays(5)
            prefix_rows(1)
            products(5)
            mean_squares(1)
            outputs(4)
            states(1, 0)
            decays(6)
            products(6)
            outputs(5)
            states(1, 1)
            decays(7)
            products(7)
            outputs(7)
            outputs(6)
            mean_squares(2)

            def mixer_out(d, bh):
                pe.wait_ge(S["scanned"], 7 + bh)
                pe.wait_ge(S["out_w_ready"], 2)
                pe.wait_ge(S["yn_ready"], BH * d + bh + 1)
                mm = pe.matmul(bank[bh][:, 0:L], out_w[:, d, :], yn[:, d, bh, :], start=(d == 0), stop=(d == 1))
                if d == 1:
                    mm.then_inc(S["o_done"], 1)

            mixer_out(0, 0)
            mixer_out(0, 1)
            mean_squares(3)
            mixer_out(1, 0)
            keep_warm(1, 6)
            mixer_out(1, 1)
            keep_warm(1, 6)
            pe.wait_ge(S["bn_step"], 2)
            pe.matmul(bank[7][:, 0:2], packs["bn_avg"], bn_mv[:, :], start=True, stop=True).then_inc(S["bn_avg_done"], 1)
            keep_warm(5, 6)
            pe.wait_ge(S["bn_shift_ready"], 1)
            pe.matmul(bank[7][:, 2:3], packs["conv4"], bn_v[:, 4:5], start=True, stop=True).then_inc(S["shift_done"], 1)
            pe.wait_ge(S["conv4_w_ready"], 1)
            pe.wait_ge(S["m_ready"], 8)
            for bh in range(BH):
                pe.wait_ge(S["o_copied"], bh + 1)
                pe.matmul(bank[2 + bh][:, 0:L], conv4_w[:, :], osb[:, bh, :], start=True, stop=True)\
                  .then_inc(S["conv4_done"], 1)
            keep_warm(3, 6)
            for bh in range(BH):
                pe.wait_ge(S["x1_ready"], bh + 1)
                pe.matmul(bank[4 + bh][:, 0:L], packs["centre"], x1[:, bh, :], start=True, stop=True)\
                  .then_inc(S["cen_done"], 1)
            pe.wait_ge(S["bias_ready"], 1)
            for bh in range(BH):
                pe.wait_ge(S["csq_ready"], bh + 1)
                pe.matmul(bank[6 + bh][:, 0:L], packs["mean32"], c1sq[:, bh, :], start=True, stop=True)\
                  .then_inc(S["var_done"], 1)

            def query(bh):
                pe.wait_ge(S["cen_ready"], bh + 1)
                pe.matmul(bank[bh][:, 0:L], mq[:, :], cen[:, bh, :], start=True, stop=True).then_inc(S["q_done"], 1)

            def values(bh):
                pe.wait_ge(S["h1_ready"], bh + 1)
                for c in range(NC):
                    mm = pe.matmul(bank[6 + bh][:, Q * c:Q * c + Q], h1[:, bh, Q * c:Q * c + Q], packs["wv"],
                                   start=True, stop=True)
                mm.then_inc(S["v_done"], 1)

            def scores(b):
                bh, q = b // BQ, b % BQ
                r = slice(C * q, C * q + C)
                sc = bank[3 + b % 3]
                pe.wait_ge(S["q_ready"], bh + 1)
                if b < 3:
                    pe.wait_ge(S["bf_ready"], 2)
                if b == 0:
                    pe.wait_ge(S["gate_ready"], 2)
                if b == 2:
                    pe.wait_ge(S["h1_ready"], 2)
                if b >= 3:
                    pe.wait_ge(S["prob_ready"], 2 * (b - 2))
                pe.matmul(sc[:, 0:384], idb[:, :], caus[:, :], start=True, stop=False)
                pe.matmul(sc[:, 0:Q], qt[r, bh, 0:Q], h1[r, bh, 0:Q], start=False, stop=False)
                pe.matmul(sc[:, Q:3 * Q], qt[r, bh, Q:L], h1[r, bh, :], start=False, stop=True).then_inc(S["s_done"], 1)

            def turn(b):
                pe.wait_ge(S["normed_prob"], 2 * (b + 1))
                if b < 2:
                    pe.wait_ge(S["v_copied"], b + 1)
                else:
                    pe.wait_ge(S["pt_copied"], b - 1)
                for k in range(3):
                    mm = pe.transpose(bank[6 + b % 2][:, Q * k:Q * k + Q], prob[:, b, Q * k:Q * k + Q], packs["ident"])
                mm.then_inc(S["pt_done"], 1)

            def attend(b):
                bh, q = b // BQ, b % BQ
                pe.wait_ge(S["pt_copied"], b + 1)
                pe.wait_ge(S["v_copied"], bh + 1)
                o = bank[1 + bh][C * q:C * q + C, 0:L]
                pe.matmul(o, val[:, NC * bh, q, :], probt[:, b, 0:2 * Q], start=True, stop=False)
                pe.matmul(o[:, Q:L], val[:, NC * bh + 1, q, :], probt[:, b, 2 * Q:3 * Q], start=False, stop=True)\
                  .then_inc(S["o_att_done"], 1)

            def centre2(bh):
                pe.wait_ge(S["t2_ready"], bh + 1)
                if bh == 0:
                    pe.wait_ge(S["q_ready"], 1)
                else:
                    pe.wait_ge(S["cen2_ready"], 1)
                pe.matmul(bank[0][:, 0:L], packs["centre"], t2[:, bh, :], start=True, stop=True).then_inc(S["cen2_done"], 1)

            def variance2(bh):
                pe.wait_ge(S["c2sq_ready"], bh + 1)
                pe.matmul(bank[1 + bh][:, 0:L], packs["mean32"], c2sq[:, bh, :], start=True, stop=True)\
                  .then_inc(S["var2_done"], 1)

            def route_bias(bh):
                pe.wait_ge(S["pd_in"], 16)
                pe.wait_ge(S["ones_ready"], 1)
                pe.wait_ge(S["l2r_ready"], bh + 1)
                pe.matmul(bank[1 + bh][:, 0:NC * BQ * E], ones[:, :], packs["router_b"][0:1, 0:NC * BQ * E],
                          start=True, stop=False)

            def route(bh):
                pe.wait_ge(S["h2_ready"], bh + 1)
                for c in range(NC):
                    mm = pe.matmul(bank[1 + bh][:, BQ * E * c:BQ * E * (c + 1)], h2[:, bh, Q * c:Q * c + Q],
                                   packs["router"], start=False, stop=(c == NC - 1))
                mm.then_inc(S["router_done"], 1)

            def experts(j):
                q, bh = j % BQ, j // BQ
                r = slice(C * q, C * q + C)
                pe.wait_ge(S["h2_ready"], bh + 1)
                if j == 0:
                    pe.wait_ge(S["pt_copied"], B)
                if j >= 4:
                    pe.wait_ge(S["mix_ready"], j - 3)
                for i in range(2):
                    mm = pe.matmul(e_bank[q][:, 256 * i:256 * i + 256], h2[r, bh, Q * i:Q * i + Q],
                                   packs["experts"][r, :], start=True, stop=True)
                mm.then_inc(S["e_done"], 1)

            def weights_turned(bh):
                pe.wait_ge(S["w_ready"], bh + 1)
                pe.transpose(wt_bank[bh][0:NC * BQ * E, 0:Q], wtok[:, bh, :, :], packs["ident"])\
                  .then_inc(S["wt_done"], 1)

            def mixed(k):
                bh = k // NC
                o = bank[k % 2 * 7][:, 0:Q]
                pe.wait_ge(S["wt_copied"], bh + 1)
                pe.wait_ge(S["t2_ready"], bh + 1)
                pe.wait_ge(S["cen2_ready"], 2)
                if k >= 2:
                    pe.wait_ge(S["fin_ready"], k - 1)
                r = slice(32 * (k % NC), 32 * (k % NC) + 32)
                pe.matmul(o, packs["experts_b"][r, :], wtt[r, bh, :], start=True, stop=False)
                pe.matmul(o, packs["ident"], t2[:, bh, Q * (k % NC):Q * (k % NC) + Q], start=False, stop=False)
                terms = E // 2
                if bh == 0:
                    pe.wait_ge(S["summed"], k + 1)
                elif k == NBLK - 1:
                    pe.wait_ge(S["last_summed"], 1)
                else:
                    pe.wait_ge(S["mix_ready"], 2 * BQ)
                    terms = E
                for e in range(terms):
                    mm = pe.matmul(o, mix[:, k, e, :, :], packs["ident"], start=False, stop=(e == terms - 1))
                mm.then_inc(S["mixed"], 1)

            query(0)
            query(1)
            values(0)
            scores(0)
            values(1)
            for b in range(1, B):
                scores(b)
                if b >= 3:
                    turn(b - 3)
                if b >= 4:
                    attend(b - 4)
            turn(5)
            centre2(0)
            attend(4)
            attend(5)
            turn(6)
            turn(7)
            variance2(0)
            attend(6)
            attend(7)
            keep_warm(1, 7)
            route_bias(0)
            centre2(1)
            route(0)
            keep_warm(2, 7)
            variance2(1)
            experts(0)
            experts(1)
            route_bias(1)
            experts(2)
            route(1)
            experts(3)
            keep_warm(4, 0)
            weights_turned(0)
            experts(4)
            experts(5)
            experts(6)
            experts(7)
            mixed(0)
            mixed(1)
            weights_turned(1)
            mixed(2)
            mixed(3)

        @block.vector
        def _(dve):
            dve.memset(warm[:, :], 0.0).then_inc(S["warmed"], 1)
            dve.memset(eps[:, :], EPS).then_inc(S["eps_ready"], 1)
            dve.wait_ge(S["pa_in"], 16)
            for t in PE_TAPS:
                dve.tensor_scalar(diag[:, t, :], packs["ident"], packs["dw"][:, t:t + 1], None, ALU.mult)\
                   .then_inc(S["diag_ready"], 1)
            steps = 0
            for i, t in enumerate(DVE_TAPS):
                for bh in range(BH):
                    win = o1p[:, bh, t // 3:t // 3 + H, t % 3:t % 3 + W]
                    to = conv[:, i % 2, bh, :].rearrange("p (h w) -> p h w", h=H)
                    if i == 0:
                        dve.wait_ge(S["lin1_copied"], bh + 1)
                        dve.tensor_scalar(to, win, packs["dw"][:, t:t + 1], None, ALU.mult)\
                           .then_inc(S["taps_done"], 1)
                    else:
                        dve.wait_ge(S["taps_done"], steps - 1)
                        dve.scalar_tensor_tensor(to, win, packs["dw"][:, t:t + 1],
                                                 conv[:, (i + 1) % 2, bh, :].rearrange("p (h w) -> p h w", h=H),
                                                 ALU.mult, ALU.add).then_inc(S["taps_done"], 1)
                    steps += 1
            for bh in range(BH):
                dve.wait_ge(S["conv_part"], bh + 1)
                dve.wait_ge(S["taps_done"], steps - 1 + bh)
                dve.tensor_tensor(convs[:, bh, :], conv_bank[bh][:, 0:L],
                                  conv[:, (len(DVE_TAPS) + 1) % 2, bh, :], ALU.add).then_inc(S["conv_summed"], 1)
            dve.wait_ge(S["pb_in"], 16)
            dve.wait_ge(S["wc_copied"], 1)
            mask_q = packs["mask4"].rearrange("p (o q) -> p o q", o=1)
            dve.tensor_tensor(dt_w[:, :, :], spread(wc[:, 128:130], [P, DIRS, BQ]),
                              mask_q.to_broadcast([P, DIRS, BQ]), ALU.mult).then_inc(S["dt_w_ready"], 1)
            dve.tensor_tensor(proj_w[:, :, :, :],
                              wc[:, 0:128].rearrange("p (n o c) -> p n o c", n=4, o=1).to_broadcast([P, 4, BQ, C]),
                              packs["mask4"].rearrange("p (n q c) -> p n q c", n=1, c=1).to_broadcast([P, 4, BQ, C]),
                              ALU.mult).then_inc(S["proj_w_ready"], 1)
            dve.wait_ge(S["fold_done"], 1)
            dve.wait_ge(S["pc_in"], 16)
            for d in range(DIRS):
                dve.scalar_tensor_tensor(out_w[:, d, :], bank[6][:, P * d:P * d + P], packs["norm_w"][:, d:d + 1],
                                         packs["mask"], ALU.mult, ALU.mult).then_inc(S["out_w_ready"], 1)
            dve.scalar_tensor_tensor(mq[:, :], bank[6][:, 2 * P:3 * P], float(C) ** -0.5, packs["mask"],
                                     ALU.mult, ALU.mult).then_inc(S["mq_ready"], 1)
            dve.wait_ge(S["dt_done"], 1)
            dve.tensor_tensor(dt_raw[:, :], dt_ps, packs["dt_bias"], ALU.add).then_inc(S["dt_step"], 1)
            dve.wait_ge(S["dt_step"], 1)
            dve.scalar_tensor_tensor(dt_neg[:, :], dt_raw[:, :], -1.0, dt_raw[:, :], ALU.mult, ALU.min).then_inc(S["dt_step"], 1)
            dve.wait_ge(S["proj_w_ready"], 1)
            dve.tensor_tensor(fold_w[:, :, :, :],
                              proj_w[:, FOLDED:FOLDED + 1, :, :].to_broadcast([P, TAPS1, BQ, C]),
                              packs["taps"].rearrange("p (k o c) -> p k o c", o=1, c=C).to_broadcast([P, TAPS1, BQ, C]),
                              ALU.mult).then_inc(S["fold_w_ready"], 1)
            dve.wait_ge(S["dt_log_done"], 1)
            dve.scalar_tensor_tensor(dt[:, :], dt_raw[:, :], 0.0, dt_log[:, :], ALU.max, ALU.add)\
               .then_inc(S["dt_ready"], 1)
            dve.wait_ge(S["dt_ready"], 1)
            dve.wait_ge(S["neg_a_ready"], 1)
            dve.scalar_tensor_tensor(a_tok[:, :], dt[:, :], -1.0, neg_a[:, :], ALU.mult, ALU.mult)\
               .then_inc(S["a_ready"], 1)
            dve.tensor_copy(dt_dir[:, :, :].rearrange("p d (k q) -> p k d q", q=BQ),
                            dt[:, :].rearrange("p (k d q) -> p k d q", d=DIRS, q=BQ)).then_inc(S["dt_dir_ready"], 1)
            dve.wait_ge(S["da_ready"], 1)
            dve.tensor_tensor(da[:, :], da[:, :], packs["keep_da"], ALU.mult).then_inc(S["da_masked"], 1)

            def tap(n, s):
                if s == 1:
                    dve.wait_ge(S["centred"], n // 2 + 1)
                else:
                    dve.wait_ge(S["tapped"], PAD * (n // 2) + s - 1)
                src = proj_bank[n][:, :].rearrange("p (b l) -> p b l", b=BH)
                to, of = (slice(s, L), slice(0, L - s)) if n < 2 else (slice(0, L - s), slice(s, L))
                col = TAPS1 * n + PAD - s
                dve.scalar_tensor_tensor(pre[:, n, :, to], src[:, :, of], packs["tap_col"][:, col:col + 1],
                                         pre[:, n, :, to], ALU.mult, ALU.add).then_inc(S["tapped"], 1)

            def own_rows(d):
                dve.wait_ge(S["s2_ready"], d + 1)
                dve.wait_ge(S["zeroed"], 3)
                for q in CBD_DVE:
                    r = slice(C * q, C * q + DI)
                    dve.tensor_copy(cbd[r, d, :, q, :], blocks(s2[r, d, :, :].rearrange("p b l -> p (b l)")))\
                       .then_inc(S["cbd_dve"], 1)

            def scan(i):
                d = groups[i][0]
                dve.wait_ge(S["dab_done"], i + 1)
                if i == 0 or i == 4:
                    dve.wait_ge(S["data1_ready"], BQ * (d + 1))
                dve.tensor_tensor_scan(lmat[:, i, :], dab_bank[i % 2][:, :], data1[:, d, :], 0.0,
                                       ALU.mult, ALU.add).then_inc(S["scanned"], 1)

            def times(i):
                dve.wait_ge(S["g_done"], i + 1)
                dve.wait_ge(S["scanned"], i + 1)
                dve.tensor_tensor(mmat[:, i, :, :], g_bank[i % 2][:, :].rearrange("p (q t) -> p q t", q=BQ),
                                  lmat[:, i, :].rearrange("p (q t) -> p q t", q=BQ), ALU.mult)\
                   .then_inc(S["m_ready"], 1)

            def weigh(d):
                dve.wait_ge(S["s1t_done"], d + 1)
                dve.wait_ge(S["dt_dir_ready"], 1)
                dve.tensor_tensor(dtbx[:, d, :, :, :].rearrange("p k q c -> p (k q) c"),
                                  t_bank[:, :].rearrange("p (k c) -> p k c", c=C),
                                  spread(dt_dir[:, d, :], [P, NBLK * BQ, C]), ALU.mult).then_inc(S["dtbx_ready"], 1)

            def keep(d, bh):
                i = groups.index((d, bh, 0))
                k = blk_of(d, bh, 0)
                dve.wait_ge(S["scanned"], i + 1)
                dve.wait_ge(S["s1t_done"], d + 1)
                dve.tensor_tensor(wbx[:, d, bh, :, :],
                                  t_bank[:, Q * k:Q * k + Q].rearrange("p (q c) -> p q c", c=C),
                                  spread(lmat[:, i, Q - 1::Q], [P, BQ, C]), ALU.mult).then_inc(S["wbx_ready"], 1)

            def prefix(d):
                dve.wait_ge(S["pfxb_done"], d + 1)
                c1 = 1 if d == 0 else 0
                dve.wait_ge(S["s2_ready"], d + 1)
                dve.tensor_tensor(cpfx[:, d, :, :], pb_ps,
                                  s2[:, d, :, Q * c1:Q * c1 + Q], ALU.mult).then_inc(S["cpfx_ready"], 1)

            def gated(u):
                d, bh = u // BH, u % BH
                dve.wait_ge(S["y_done"], 2 * (u + 1))
                dve.scalar_tensor_tensor(yd[:, d, bh, :], s1[:, d, bh, :], packs["skip_d"][:, d:d + 1],
                                         half(unit_bank[u % 2], 0), ALU.mult, ALU.add).then_inc(S["yd_ready"], 1)
                dve.wait_ge(S["yd_ready"], u + 1)
                dve.tensor_tensor(yg[:, d, bh, :], yd[:, d, bh, :], s2[:, d, bh, :], ALU.mult)\
                   .then_inc(S["yg_ready"], 1)

            def normed(u):
                d, bh = u // BH, u % BH
                dve.wait_ge(S["yrs_ready"], u + 1)
                dve.tensor_tensor(yn[:, d, bh, :], yg[:, d, bh, :], yrs[:, d, bh, :], ALU.mult)\
                   .then_inc(S["yn_ready"], 1)

            tap(0, 1)
            tap(0, 2)
            tap(0, 3)
            scan(0)
            scan(1)
            tap(2, 1)
            tap(2, 2)
            own_rows(0)
            tap(2, 3)
            weigh(0)
            keep(0, 0)
            times(0)
            prefix(0)
            times(1)
            scan(2)
            keep(0, 1)
            gated(0)
            times(2)
            scan(3)
            times(3)
            own_rows(1)
            scan(4)
            weigh(1)
            keep(1, 0)
            scan(5)
            gated(1)
            times(4)
            prefix(1)
            times(5)
            scan(6)
            keep(1, 1)
            times(6)
            scan(7)
            times(7)
            gated(2)
            normed(0)
            normed(1)
            gated(3)
            normed(2)
            normed(3)
            for bh in range(BH):
                dve.wait_ge(S["o_done"], bh + 1)
                dve.bn_stats(bn_st[:, bh, :], bank[bh][:, 0:L]).then_inc(S["bn_stats_done"], 1)
            dve.wait_ge(S["bn_stats_done"], 2)
            dve.bn_aggr(bn_mv[:, :], bn_st[:, :, :].rearrange("p b s -> p (b s)")).then_inc(S["bn_step"], 1)
            dve.wait_ge(S["bn_step"], 1)
            dve.scalar_tensor_tensor(bn_mv[:, 1:2], bn_mv[:, 0:1], bn_mv[:, 0:1], bn_mv[:, 1:2], ALU.mult, ALU.add)\
               .then_inc(S["bn_step"], 1)
            dve.wait_ge(S["bn_avg_done"], 1)
            dve.tensor_copy(bn_m[:, :], bank[7][:, 0:2]).then_inc(S["bn_step"], 1)
            dve.wait_ge(S["bn_step"], 3)
            dve.scalar_tensor_tensor(bn_v[:, 0:1], bn_m[:, 0:1], bn_m[:, 0:1], bn_m[:, 1:2], ALU.mult, ALU.subtract)\
               .then_inc(S["bn_var_ready"], 1)
            dve.wait_ge(S["bn_rs"], 1)
            dve.tensor_tensor(bn_v[:, 3:4], packs["bn_g"], bn_v[:, 2:3], ALU.mult).then_inc(S["bn_scale_ready"], 1)
            dve.wait_ge(S["bn_scale_ready"], 1)
            dve.scalar_tensor_tensor(bn_v[:, 4:5], bn_m[:, 0:1], bn_v[:, 3:4], packs["bn_b"], ALU.mult, ALU.subtract)\
               .then_inc(S["bn_shift_ready"], 1)
            dve.tensor_scalar(conv4_w[:, :], packs["conv4"], bn_v[:, 3:4], None, ALU.mult).then_inc(S["conv4_w_ready"], 1)
            dve.wait_ge(S["shift_done"], 1)
            dve.wait_ge(S["halved"], 1)
            dve.scalar_tensor_tensor(bn_v[:, 5:6], bank[7][:, 2:3], -0.5, b_half[:, :], ALU.mult, ALU.add)\
               .then_inc(S["bias_ready"], 1)
            dve.wait_ge(S["halved"], 2)
            for bh in range(BH):
                dve.wait_ge(S["gate_ready"], bh + 1)
                dve.scalar_tensor_tensor(x1[:, bh, :], gate[:, bh, :], 3.0, half(x_half[:, :], bh), ALU.add, ALU.mult)\
                   .then_inc(S["x1_ready"], 1)
            for bh in range(BH):
                dve.wait_ge(S["csq_ready"], bh + 1)
                dve.tensor_copy(cen[:, bh, :], bank[4 + bh][:, 0:L]).then_inc(S["cen_ready"], 1)
            for bh in range(BH):
                dve.wait_ge(S["l1r_ready"], bh + 1)
                dve.wait_ge(S["q_done"], bh + 1)
                dve.tensor_tensor(qt[:, bh, :], bank[bh][:, 0:L], l1r[:, bh, :], ALU.mult).then_inc(S["q_ready"], 1)
                dve.tensor_tensor(h1[:, bh, :], cen[:, bh, :], l1r[:, bh, :], ALU.mult).then_inc(S["h1_ready"], 1)

            def value_copy(bh):
                dve.wait_ge(S["v_done"], bh + 1)
                dve.tensor_copy(val[:, NC * bh:NC * bh + NC, :, :].rearrange("p k q c -> p (k q c)"), bank[6 + bh][:, 0:L])\
                   .then_inc(S["v_copied"], 1)

            def row_max(b):
                dve.wait_ge(S["s_done"], b + 1)
                sc = bank[3 + b % 3]
                dve.tensor_reduce(nmax[:, b, 0:1], sc[:, 0:Q], AX_X, ALU.max, negate=True).then_inc(S["nmax_ready"], 1)
                dve.tensor_reduce(nmax[:, b, 1:2], sc[:, Q:3 * Q], AX_X, ALU.max, negate=True)\
                   .then_inc(S["nmax_ready"], 1)

            def normalise(b):
                dve.wait_ge(S["prob_ready"], 2 * b + 2)
                dve.reciprocal(rden[:, b, :], den[:, b, :]).then_inc(S["rden_ready"], 1)
                dve.wait_ge(S["rden_ready"], b + 1)
                dve.tensor_scalar(prob[:, b, 0:Q], prob[:, b, 0:Q], rden[:, b, 0:1], None, ALU.mult)\
                   .then_inc(S["normed_prob"], 1)
                dve.tensor_scalar(prob[:, b, Q:3 * Q], prob[:, b, Q:3 * Q], rden[:, b, 1:2], None, ALU.mult)\
                   .then_inc(S["normed_prob"], 1)

            def residual(bh):
                dve.wait_ge(S["o_att_done"], BQ * (bh + 1))
                dve.tensor_tensor(t2[:, bh, :], bank[1 + bh][:, 0:L], x1[:, bh, :], ALU.add).then_inc(S["t2_ready"], 1)

            def ln2_centred(bh):
                dve.wait_ge(S["c2sq_ready"], bh + 1)
                dve.tensor_copy(cen2[:, bh, :], bank[0][:, 0:L]).then_inc(S["cen2_ready"], 1)

            def ln2_scale(bh):
                dve.wait_ge(S["l2r_ready"], bh + 1)
                dve.wait_ge(S["cen2_ready"], bh + 1)
                dve.tensor_tensor(h2[:, bh, :], cen2[:, bh, :], l2r[:, bh, :], ALU.mult).then_inc(S["h2_ready"], 1)

            rank = packs["rank"][:, 0:NC * BQ * E].rearrange("p (k e) -> p k e", e=E)
            over = lambda t, bh: spread(t[:, bh, :], [P, NC * BQ, E])
            logits = [bank[1 + bh][:, 0:NC * BQ * E].rearrange("p (k e) -> p k e", e=E) for bh in range(BH)]

            def find_top1(bh):
                dve.wait_ge(S["router_done"], bh + 1)
                dve.tensor_reduce(top1[:, bh, :], logits[bh], AX_X, ALU.max).then_inc(S["top1_ready"], 1)

            def find_is1(bh):
                dve.wait_ge(S["top1_ready"], bh + 1)
                dve.tensor_tensor(is1[:, bh, :, :], logits[bh], over(top1, bh), ALU.is_equal)\
                   .then_inc(S["is1_ready"], 1)

            def find_rank1(bh):
                dve.wait_ge(S["is1_ready"], bh + 1)
                dve.tensor_tensor(rank1[:, bh, :, :], is1[:, bh, :, :], rank, ALU.mult).then_inc(S["rank1_ready"], 1)

            def find_best1(bh):
                dve.wait_ge(S["rank1_ready"], bh + 1)
                dve.tensor_reduce(best1[:, bh, :], rank1[:, bh, :, :], AX_X, ALU.max).then_inc(S["best1_ready"], 1)

            def find_pick1(bh):
                dve.wait_ge(S["best1_ready"], bh + 1)
                dve.tensor_tensor(pick1[:, bh, :, :], rank1[:, bh, :, :], over(best1, bh), ALU.is_equal)\
                   .then_inc(S["pick1_ready"], 1)

            def find_rest(bh):
                dve.wait_ge(S["pick1_ready"], bh + 1)
                dve.scalar_tensor_tensor(rest[:, bh, :, :], pick1[:, bh, :, :], MASKED, logits[bh],
                                         ALU.mult, ALU.add).then_inc(S["rest_ready"], 1)

            def find_top2(bh):
                dve.wait_ge(S["rest_ready"], bh + 1)
                dve.tensor_reduce(top2[:, bh, :], rest[:, bh, :, :], AX_X, ALU.max).then_inc(S["top2_ready"], 1)

            def find_is2(bh):
                dve.wait_ge(S["top2_ready"], bh + 1)
                dve.tensor_tensor(diff[:, bh, :], top2[:, bh, :], top1[:, bh, :], ALU.subtract).then_inc(S["diff_ready"], 1)
                dve.tensor_tensor(is2[:, bh, :, :], rest[:, bh, :, :], over(top2, bh), ALU.is_equal)\
                   .then_inc(S["is2_ready"], 1)

            def find_rank2(bh):
                dve.wait_ge(S["is2_ready"], bh + 1)
                dve.tensor_tensor(rank2[:, bh, :, :], is2[:, bh, :, :], rank, ALU.mult).then_inc(S["rank2_ready"], 1)

            def find_best2(bh):
                dve.wait_ge(S["rank2_ready"], bh + 1)
                dve.tensor_reduce(best2[:, bh, :], rank2[:, bh, :, :], AX_X, ALU.max).then_inc(S["best2_ready"], 1)

            def find_psum2(bh):
                dve.wait_ge(S["p2_ready"], bh + 1)
                dve.tensor_scalar(psum2[:, bh, :], p2[:, bh, :], 1.0, None, ALU.add).then_inc(S["psum2_ready"], 1)

            def find_w1(bh):
                dve.wait_ge(S["psum2_ready"], bh + 1)
                dve.reciprocal(w1[:, bh, :], psum2[:, bh, :]).then_inc(S["w1_ready"], 1)

            def find_w2(bh):
                dve.wait_ge(S["w1_ready"], bh + 1)
                dve.tensor_tensor(w2[:, bh, :], w1[:, bh, :], p2[:, bh, :], ALU.mult).then_inc(S["w2_ready"], 1)
                dve.tensor_tensor(wfirst[:, bh, :, :], pick1[:, bh, :, :], over(w1, bh), ALU.mult)\
                   .then_inc(S["wfirst_ready"], 1)

            def find_pick2(bh):
                dve.wait_ge(S["best2_ready"], bh + 1)
                dve.tensor_tensor(pick2[:, bh, :, :], rank2[:, bh, :, :], over(best2, bh), ALU.is_equal)\
                   .then_inc(S["pick2_ready"], 1)

            def find_second(bh):
                dve.wait_ge(S["pick2_ready"], bh + 1)
                dve.wait_ge(S["w2_ready"], bh + 1)
                dve.tensor_tensor(wsec[:, bh, :, :], pick2[:, bh, :, :], over(w2, bh), ALU.mult).then_inc(S["wsec_ready"], 1)

            def find_weights(bh):
                dve.wait_ge(S["wsec_ready"], bh + 1)
                dve.wait_ge(S["wfirst_ready"], bh + 1)
                dve.tensor_tensor(wtok[:, bh, :, :], wsec[:, bh, :, :], wfirst[:, bh, :, :], ALU.add).then_inc(S["w_ready"], 1)

            def weighted(q, blks):
                bh = blks[0] // NC
                c0, n = blks[0] % NC, len(blks)
                dve.wait_ge(S["e_done"], BQ * bh + q + 1)
                dve.wait_ge(S["w_ready"], bh + 1)
                w4 = wtok[:, bh, :, :].rearrange("p (k q) e -> p k q e", q=BQ)
                dve.tensor_tensor(mix[:, blks[0]:blks[0] + n, :, q, :],
                                  e_bank[q][:, :].rearrange("p (k e c) -> p k e c", k=NC, e=E)[:, c0:c0 + n, :, :],
                                  w4[:, c0:c0 + n, q, :].rearrange("p k (e o) -> p k e o", o=1).to_broadcast([P, n, E, C]),
                                  ALU.mult).then_inc(S["mix_ready"], 1)

            value_copy(0)
            row_max(0)
            value_copy(1)
            for b in range(1, B - 1):
                row_max(b)
                normalise(b - 1)
            row_max(7)
            residual(0)
            normalise(6)
            normalise(7)
            residual(1)
            ln2_centred(0)
            ln2_scale(0)
            find_top1(0)
            find_is1(0)
            ln2_centred(1)
            find_rank1(0)
            find_best1(0)
            find_pick1(0)
            find_rest(0)
            ln2_scale(1)
            find_top2(0)
            find_is2(0)
            find_rank2(0)
            find_psum2(0)
            find_best2(0)
            find_pick2(0)
            find_w1(0)
            find_w2(0)
            find_top1(1)
            find_second(0)
            find_is1(1)
            find_weights(0)
            find_rank1(1)
            weighted(0, [0, 1])
            weighted(1, [0, 1])
            find_best1(1)
            weighted(2, [0, 1])
            find_pick1(1)
            weighted(3, [0, 1])
            find_rest(1)
            find_top2(1)
            find_is2(1)
            find_rank2(1)
            find_best2(1)
            find_psum2(1)
            find_pick2(1)
            find_w1(1)
            find_w2(1)
            find_second(1)
            find_weights(1)
            for k in (2, 3):
                for q in range(BQ):
                    weighted(q, [k])
            dve.wait_ge(S["mix_ready"], 3 * BQ)
            dve.tensor_tensor(mix[:, 3, 0:E // 2, :, :], mix[:, 3, 0:E // 2, :, :], mix[:, 3, E // 2:E, :, :], ALU.add)\
               .then_inc(S["last_summed"], 1)


def pack_inputs(inp):
    import numpy as np

    f = np.float32
    g = {k: np.asarray(v) for k, v in inp.items()}
    get = lambda n: g["L0_conv_" + n]
    rows = np.arange(P)
    img, ch = rows // C, rows % C

    def rep(a):
        return np.tile(a.reshape(C, -1), (BQ, 1))

    def bd(a):
        n = a.shape[1]
        o = np.zeros((P, BQ * n), f)
        for q in range(BQ):
            o[C * q:C * q + C, n * q:n * q + n] = a
        return o

    def top(a):
        o = np.zeros((P, a.shape[1]), f)
        o[:C] = a
        return o

    def upper(cols):
        o = np.zeros((P, DIRS), f)
        for d in range(DIRS):
            for q in range(BQ):
                o[C * q + DI:C * q + C, d] = cols[d]
        return o

    v = {}
    v["lin1"] = bd(get("lin1_w"))
    v["ident"] = np.eye(P, dtype=f)
    v["rev"] = np.eye(P, dtype=f)[::-1]
    v["lin1_b"], v["dw_b"], v["dw"] = rep(get("lin1_b")), rep(get("dw_b")), rep(get("dw_w").reshape(C, 9))
    v["fc_in_t"] = top(np.tile(get("fc_in_w").T, (1, BQ)))
    win = get("mam_in_w")
    z, xs, bm, cm, dt = (win[:, :, a:b] for a, b in ((0, 16), (16, 32), (32, 48), (48, 64), (64, 65)))
    v["mam_in"] = top(np.concatenate(
        [np.concatenate([bm[d], xs[d], cm[d], z[d]], 1) for d in range(DIRS)] + [dt[0], dt[1]], 1))
    cw, cb = get("mam_conv_w"), get("mam_conv_b")
    taps = np.zeros((DIRS, 2, TAPS1, C), f)
    conv_b = np.zeros((BQ, C, 4), f)
    for d in range(DIRS):
        taps[d, 0] = np.concatenate([cw[d, 16:32], cw[d, 0:16]]).T
        taps[d, 1, :, :DI] = cw[d, 32:48].T
        taps[d, 1, TAPS1 - 1, DI:] = 1.0
        conv_b[:, :, 2 * d] = np.concatenate([cb[d, 16:32], cb[d, 0:16]])
        conv_b[:, :DI, 2 * d + 1] = cb[d, 32:48]
    v["taps"] = np.tile(taps[FOLDED // 2, FOLDED % 2].reshape(1, -1), (P, 1))
    v["tap_col"] = np.tile(taps.transpose(3, 0, 1, 2).reshape(C, 16), (BQ, 1))
    v["conv_b"] = conv_b.reshape(P, 4)
    v["mask4"] = (img[:, None] == np.arange(BQ)[None]).astype(f)
    per_unit = lambda a: np.tile(np.broadcast_to(a.reshape(1, DIRS, 1), (NBLK, DIRS, BQ)).reshape(1, -1), (P, 1))
    v["dt_bias"], v["a_log"] = per_unit(get("mam_dt_bias")), per_unit(get("mam_A_log"))
    keep = np.ones((P, NBLK, DIRS, BQ), f)
    keep[0, :, 0] = 0.0
    keep[P - 1, :, 1] = 0.0
    v["keep_da"] = keep.reshape(P, 32)
    v["skip_d"] = upper([np.full(DI, get("mam_D")[d, 0], f) for d in range(DIRS)])
    r, t = rows[:, None], rows[None]
    v["tri"] = np.concatenate([(r <= t), (r >= t)], 1).astype(f)
    wo = get("mam_out_w")
    v["out_t"] = np.zeros((P, 2 * P), f)
    for d in range(DIRS):
        for q in range(BQ):
            v["out_t"][:C, P * d + C * q + DI:P * d + C * q + C] = wo[d].T
    v["fc_out"] = top(np.tile(get("fc_out_w"), (1, BQ)))
    v["norm_w"] = upper(list(get("mam_norm_w")))
    same = img[:, None] == img[None]
    v["mask"] = same.astype(f)
    v["mean16"] = (same & (ch[:, None] >= DI)).astype(f) / f(DI)
    v["bn_avg"] = (ch[:, None] == ch[None]).astype(f) / f(BQ)
    v["bn_g"], v["bn_b"], v["conv4_b"] = rep(get("bn_g")), rep(get("bn_b")), rep(get("conv4_b"))
    v["conv4"] = bd(get("conv4_w"))
    v["mean32"] = same.astype(f) / f(C)
    v["centre"] = np.eye(P, dtype=f) - v["mean32"]
    v["wq_t"] = top(np.tile(g["L1_attn_W_Q"].T, (1, BQ)))
    v["wk_t"] = top(np.tile(g["L1_attn_W_K"].T, (1, BQ)))
    v["wv"] = bd(g["L1_attn_W_V"])
    tri = np.where(t > r, f(MASKED), f(0.0)).astype(f)
    v["causal"] = np.concatenate([tri, np.zeros((P, P), f), tri], 1)
    v["router"] = bd(g["L1_ffn_router_w"])
    v["router_b"] = np.tile(g["L1_ffn_router_b"].reshape(1, E), (P, 16))
    v["experts"] = np.tile(g["L1_ffn_expert_w"].transpose(1, 0, 2).reshape(C, E * C), (BQ, 1))
    eb = np.zeros((BQ, E, BQ, C), f)
    for q in range(BQ):
        eb[q, :, q] = g["L1_ffn_expert_b"]
    v["experts_b"] = np.tile(eb.reshape(BQ * E, P), (BQ, 1))
    v["rank"] = np.tile((E - np.arange(E, dtype=f)).reshape(1, E), (P, 16))

    arrays = {"x4": np.ascontiguousarray(
        g["x"].reshape(BH, BQ, C, L).transpose(1, 2, 0, 3).reshape(P, N))}
    for pack, parts in PACKS.items():
        for name, width in parts:
            assert v[name].shape == (P, width), (name, v[name].shape)
        arrays[pack] = np.ascontiguousarray(np.concatenate([v[name] for name, _ in parts], 1).astype(f, copy=False))
    return arrays


def kernel(**inputs):
    import numpy as np
    import concourse.bacc as _bacc
    from concourse import mybir as _mybir
    from concourse.bass_utils import run_bass_kernel_spmd as _run

    arrays = pack_inputs(inputs)
    nc = _bacc.Bacc("TRN2", target_bir_lowering=False, num_devices=1)
    args = [nc.dram_tensor(f"in_{n}", a.shape, _mybir.dt.float32, kind="ExternalInput").ap()
            for n, a in arrays.items()]
    out = nc.dram_tensor("out_0", (P, N), _mybir.dt.float32, kind="ExternalOutput").ap()
    program(nc, *args, out)
    r = _run(nc, [{f"in_{n}": a for n, a in arrays.items()}], core_ids=[0])
    o = r.results[0]["out_0"]
    return np.ascontiguousarray(o.reshape(BQ, C, BH, H, W).transpose(2, 0, 1, 3, 4).reshape(B, C, H, W))
```
